# Optimizing a Trainium2 kernel written in Bass

```python
import numpy as np
import jax
import jax.numpy as jnp

def _softmax(x, axis=-1):
    return jax.nn.softmax(x, axis=axis)

def _gelu(x):
    return jax.nn.gelu(x, approximate=True)

def _silu(x):
    return jax.nn.silu(x)

def _sigmoid(x):
    return jax.nn.sigmoid(x)

def _layernorm(x, axis=-1, eps=1e-05):
    m = jnp.mean(x, axis=axis, keepdims=True)
    v = jnp.var(x, axis=axis, keepdims=True)
    return (x - m) / jnp.sqrt(v + eps)

def _scatter_add(tgt, idx, src, axis=0):
    return tgt.at[idx].add(src)

def _segment_sum(src, seg, n):
    return jax.ops.segment_sum(src, seg, n)
kernel_name = 'mk_decoder_preln_d2_seqx_r4_13de55'

def setup_inputs(seed: int=0):
    np.random.seed(seed)
    _w = jnp.asarray

    def _rec_inputs():
        import jax
        import jax.numpy as jnp
        _rk = jax.random.key(seed)
        x = -0.0002928 + 1 * jax.random.normal(jax.random.fold_in(_rk, 1), (2, 512, 256), jnp.float32)
        _lenS = 512 - jax.random.randint(jax.random.fold_in(_rk, 7), (2,), 0, max(1, 512 // 4) + 1, jnp.int32)
        _lenS2 = 1024 - jax.random.randint(jax.random.fold_in(_rk, 8), (2,), 0, max(1, 1024 // 4) + 1, jnp.int32)
        _ctx_1024P = jax.random.normal(jax.random.fold_in(_rk, 11), (2, 16, 256), jnp.float32)
        _ctx_1024c = jax.random.dirichlet(jax.random.fold_in(_rk, 511), 0.3 * jnp.ones((16,), jnp.float32), (2, 1024))
        _ctx_1024t = jnp.einsum('bsk,bkd->bsd', _ctx_1024c, _ctx_1024P)
        _ctx_1024t = _ctx_1024t * jax.lax.rsqrt(jnp.mean(jnp.square(_ctx_1024t)) + 1e-12) * 0.953939
        ctx_1024 = -1.39393e-06 + 0.999914 * (_ctx_1024t + 0.3 * jax.random.normal(jax.random.fold_in(_rk, 611), (2, 1024, 256), jnp.float32))
        return (x, ctx_1024)
    x, ctx_1024 = _rec_inputs()

    def _L0_attn_setup():
        import jax, jax.numpy as jnp
        import numpy as np
        E = 256
        H = 16
        D = E // H
        B = 2
        S = 512
        YAT_EPS = 0.1
        key = jax.random.key(seed)
        ks = jax.random.split(key, 5)
        w_scale = (6.0 / (E + E)) ** 0.5

        def xavier(k):
            return jax.random.uniform(k, (E, E), jnp.float32, -w_scale, w_scale)
        return {'x': jax.random.normal(ks[0], (B, S, E), jnp.float32), 'Wq': xavier(ks[1]), 'bq': jnp.zeros((E,), jnp.float32), 'Wk': xavier(ks[2]), 'bk': jnp.zeros((E,), jnp.float32), 'Wv': xavier(ks[3]), 'bv': jnp.zeros((E,), jnp.float32), 'Wo': xavier(ks[4]), 'bo': jnp.zeros((E,), jnp.float32)}
    _L0_attn_all = _L0_attn_setup()
    _L0_attn_in = {k: v for k, v in _L0_attn_all.items() if k in ('Wq', 'bq', 'Wk', 'bk', 'Wv', 'bv', 'Wo', 'bo')}
    del _L0_attn_all

    def _L0_xattn_setup():
        import jax, jax.numpy as jnp
        import numpy as np
        B, S, D, H = (2, 512, 256, 16)
        DK = D // H
        key = jax.random.key(seed)
        ks = jax.random.split(key, 11)
        s = 1.0 / np.sqrt(D)
        return {'query': jax.random.normal(ks[0], (B, S, D), jnp.float32), 'key': jax.random.normal(ks[1], (B, S, D), jnp.float32), 'value': jax.random.normal(ks[2], (B, S, D), jnp.float32), 'Wq': jax.random.normal(ks[3], (D, D), jnp.float32) * s, 'bq': jnp.zeros((D,), jnp.float32), 'Wk': jax.random.normal(ks[4], (D, D), jnp.float32) * s, 'bk': jnp.zeros((D,), jnp.float32), 'Wv': jax.random.normal(ks[5], (D, D), jnp.float32) * s, 'bv': jnp.zeros((D,), jnp.float32), 'Wo': jax.random.normal(ks[6], (D, D), jnp.float32) * s, 'bo': jnp.zeros((D,), jnp.float32)}
    _L0_xattn_all = _L0_xattn_setup()
    _L0_xattn_in = {k: v for k, v in _L0_xattn_all.items() if k in ('Wq', 'bq', 'Wk', 'bk', 'Wv', 'bv', 'Wo', 'bo')}
    del _L0_xattn_all

    def _L0_ffn_setup():
        import jax, jax.numpy as jnp
        import numpy as np
        B, S, H = (4, 512, 256)
        D = 512
        E = 8
        K = 2
        key = jax.random.key(seed)
        ks = jax.random.split(key, 8)
        w = lambda k, shape: jax.random.normal(k, shape, jnp.float32) * 0.02
        return {'hidden_states': jax.random.normal(ks[0], (B, S, H), jnp.float32), 'gate_w': w(ks[1], (H, E)), 'w_gate': w(ks[2], (E, H, D)), 'w_up': w(ks[3], (E, H, D)), 'w_down': w(ks[4], (E, D, H)), 'ws_gate': w(ks[5], (H, D)), 'ws_up': w(ks[6], (H, D)), 'ws_down': w(ks[7], (D, H))}
    _L0_ffn_all = _L0_ffn_setup()
    _L0_ffn_in = {k: v for k, v in _L0_ffn_all.items() if k in ('gate_w', 'w_gate', 'w_up', 'w_down', 'ws_gate', 'ws_up', 'ws_down')}
    del _L0_ffn_all

    def _L1_attn_setup():
        import jax, jax.numpy as jnp
        import numpy as np
        B, T, D, H = (4, 512, 256, 16)
        HEAD_DIM = D // H
        LOCAL_WINDOW = 128

        def _rotate_half(t):
            t1, t2 = jnp.split(t, 2, axis=-1)
            return jnp.concatenate([-t2, t1], axis=-1)

        def _apply_rope(q, k):
            Tq, d = (q.shape[2], q.shape[3])
            half = d // 2
            theta = 1.0 / 10000.0 ** (jnp.arange(half, dtype=jnp.float32) / half)
            pos = jnp.arange(Tq, dtype=jnp.float32)
            freqs = pos[:, None] * theta[None, :]
            freqs = jnp.concatenate([freqs, freqs], axis=-1)
            cos = jnp.cos(freqs)[None, None]
            sin = jnp.sin(freqs)[None, None]
            q = q * cos + _rotate_half(q) * sin
            k = k * cos + _rotate_half(k) * sin
            return (q, k)
        key = jax.random.key(seed)
        k1, k2, k3 = jax.random.split(key, 3)
        x = jax.random.normal(k1, (B, T, D), dtype=jnp.float32)
        Wqkv = jax.random.normal(k2, (D, 3 * D), dtype=jnp.float32) * 0.02
        Wout = jax.random.normal(k3, (D, D), dtype=jnp.float32) * 0.02
        return {'x': x, 'Wqkv': Wqkv, 'Wout': Wout}
    _L1_attn_all = _L1_attn_setup()
    _L1_attn_in = {k: v for k, v in _L1_attn_all.items() if k in ('Wqkv', 'Wout')}
    del _L1_attn_all

    def _L1_xattn_setup():
        import jax, jax.numpy as jnp
        import numpy as np
        DIM = 256
        NUM_HEADS = 8
        HEAD_DIM = 64
        INNER = NUM_HEADS * HEAD_DIM
        key = jax.random.key(seed)
        ks = jax.random.split(key, 7)
        B, N, M = (8, 128, 1024)
        x = jax.random.normal(ks[0], (B, N, DIM), dtype=jnp.float32)
        context = jax.random.normal(ks[1], (B, M, DIM), dtype=jnp.float32)
        s_in = 1.0 / np.sqrt(DIM)
        s_inner = 1.0 / np.sqrt(INNER)
        Wq = jax.random.normal(ks[2], (DIM, INNER), dtype=jnp.float32) * s_in
        Wk = jax.random.normal(ks[3], (DIM, INNER), dtype=jnp.float32) * s_in
        Wv = jax.random.normal(ks[4], (DIM, INNER), dtype=jnp.float32) * s_in
        Wo = jax.random.normal(ks[5], (INNER, DIM), dtype=jnp.float32) * s_inner
        bo = jax.random.normal(ks[6], (DIM,), dtype=jnp.float32) * 0.01
        return {'x': x, 'context': context, 'Wq': Wq, 'Wk': Wk, 'Wv': Wv, 'Wo': Wo, 'bo': bo}
    _L1_xattn_all = _L1_xattn_setup()
    _L1_xattn_in = {k: v for k, v in _L1_xattn_all.items() if k in ('Wq', 'Wk', 'Wv', 'Wo', 'bo')}
    del _L1_xattn_all

    def _L1_ffn_setup():
        import jax, jax.numpy as jnp
        import numpy as np
        HIDDEN = 256
        NUM_EXPERTS = 8
        TOP_K = 2
        B, S = (2, 512)
        key = jax.random.key(seed)
        k1, k2, k3, k4, k5 = jax.random.split(key, 5)
        d, dff, E = (HIDDEN, 4 * HIDDEN, NUM_EXPERTS)
        x = jax.random.normal(k1, (B, S, d), dtype=jnp.float32)
        W1 = jax.random.normal(k2, (E, d, dff), dtype=jnp.float32) * (1.0 / np.sqrt(d))
        b1 = jax.random.normal(k3, (E, dff), dtype=jnp.float32) * 0.01
        W2 = jax.random.normal(k4, (E, dff, d), dtype=jnp.float32) * (1.0 / np.sqrt(dff))
        b2 = jax.random.normal(k5, (E, d), dtype=jnp.float32) * 0.01
        return {'x': x, 'W1': W1, 'b1': b1, 'W2': W2, 'b2': b2}
    _L1_ffn_all = _L1_ffn_setup()
    _L1_ffn_in = {k: v for k, v in _L1_ffn_all.items() if k in ('W1', 'b1', 'W2', 'b2')}
    del _L1_ffn_all
    return {'x': x, 'ctx_1024': ctx_1024, 'L0_attn_Wq': _L0_attn_in['Wq'], 'L0_attn_bq': _L0_attn_in['bq'], 'L0_attn_Wk': _L0_attn_in['Wk'], 'L0_attn_bk': _L0_attn_in['bk'], 'L0_attn_Wv': _L0_attn_in['Wv'], 'L0_attn_bv': _L0_attn_in['bv'], 'L0_attn_Wo': _L0_attn_in['Wo'], 'L0_attn_bo': _L0_attn_in['bo'], 'L0_xattn_Wq': _L0_xattn_in['Wq'], 'L0_xattn_bq': _L0_xattn_in['bq'], 'L0_xattn_Wk': _L0_xattn_in['Wk'], 'L0_xattn_bk': _L0_xattn_in['bk'], 'L0_xattn_Wv': _L0_xattn_in['Wv'], 'L0_xattn_bv': _L0_xattn_in['bv'], 'L0_xattn_Wo': _L0_xattn_in['Wo'], 'L0_xattn_bo': _L0_xattn_in['bo'], 'L0_ffn_gate_w': _L0_ffn_in['gate_w'], 'L0_ffn_w_gate': _L0_ffn_in['w_gate'], 'L0_ffn_w_up': _L0_ffn_in['w_up'], 'L0_ffn_w_down': _L0_ffn_in['w_down'], 'L0_ffn_ws_gate': _L0_ffn_in['ws_gate'], 'L0_ffn_ws_up': _L0_ffn_in['ws_up'], 'L0_ffn_ws_down': _L0_ffn_in['ws_down'], 'L1_attn_Wqkv': _L1_attn_in['Wqkv'], 'L1_attn_Wout': _L1_attn_in['Wout'], 'L1_xattn_Wq': _L1_xattn_in['Wq'], 'L1_xattn_Wk': _L1_xattn_in['Wk'], 'L1_xattn_Wv': _L1_xattn_in['Wv'], 'L1_xattn_Wo': _L1_xattn_in['Wo'], 'L1_xattn_bo': _L1_xattn_in['bo'], 'L1_ffn_W1': _L1_ffn_in['W1'], 'L1_ffn_b1': _L1_ffn_in['b1'], 'L1_ffn_W2': _L1_ffn_in['W2'], 'L1_ffn_b2': _L1_ffn_in['b2']}

def reference(x, ctx_1024, L0_attn_Wq, L0_attn_bq, L0_attn_Wk, L0_attn_bk, L0_attn_Wv, L0_attn_bv, L0_attn_Wo, L0_attn_bo, L0_xattn_Wq, L0_xattn_bq, L0_xattn_Wk, L0_xattn_bk, L0_xattn_Wv, L0_xattn_bv, L0_xattn_Wo, L0_xattn_bo, L0_ffn_gate_w, L0_ffn_w_gate, L0_ffn_w_up, L0_ffn_w_down, L0_ffn_ws_gate, L0_ffn_ws_up, L0_ffn_ws_down, L1_attn_Wqkv, L1_attn_Wout, L1_xattn_Wq, L1_xattn_Wk, L1_xattn_Wv, L1_xattn_Wo, L1_xattn_bo, L1_ffn_W1, L1_ffn_b1, L1_ffn_W2, L1_ffn_b2):
    import jax
    import jax.numpy as jnp

    def _L0_attn_ref(x, Wq, bq, Wk, bk, Wv, bv, Wo, bo):
        import jax, jax.numpy as jnp
        import numpy as np
        E = 256
        H = 16
        D = E // H
        B = 2
        S = 512
        YAT_EPS = 0.1
        b, s, _ = x.shape
        Q = x @ Wq + bq
        K = x @ Wk + bk
        V = x @ Wv + bv
        Q = Q.reshape(b, s, H, D).transpose(0, 2, 1, 3)
        K = K.reshape(b, s, H, D).transpose(0, 2, 1, 3)
        V = V.reshape(b, s, H, D).transpose(0, 2, 1, 3)
        Qn = Q / (jnp.linalg.norm(Q, axis=-1, keepdims=True) + 1e-08)
        Kn = K / (jnp.linalg.norm(K, axis=-1, keepdims=True) + 1e-08)
        dot = jnp.einsum('bhqd,bhkd->bhqk', Qn, Kn)
        scores = (1.0 + dot) ** 2 / (YAT_EPS + (1.0 - dot))
        attn = scores / (jnp.sum(scores, axis=-1, keepdims=True) + 1e-06)
        out = jnp.einsum('bhqk,bhkd->bhqd', attn, V)
        out = out.transpose(0, 2, 1, 3).reshape(b, s, E)
        return out @ Wo + bo

    def _L0_xattn_ref(query, key, value, Wq, bq, Wk, bk, Wv, bv, Wo, bo):
        import jax, jax.numpy as jnp
        import numpy as np
        B, S, D, H = (2, 512, 256, 16)
        DK = D // H
        b = query.shape[0]
        q = (query @ Wq + bq).reshape(b, -1, H, DK).transpose(0, 2, 1, 3)
        k = (key @ Wk + bk).reshape(b, -1, H, DK).transpose(0, 2, 1, 3)
        v = (value @ Wv + bv).reshape(b, -1, H, DK).transpose(0, 2, 1, 3)
        scores = jnp.einsum('bhqd,bhkd->bhqk', q, k) / jnp.sqrt(jnp.float32(DK))
        attn = jax.nn.softmax(scores, axis=-1)
        x = jnp.einsum('bhqk,bhkd->bhqd', attn, v)
        x = x.transpose(0, 2, 1, 3).reshape(b, -1, H * DK)
        return x @ Wo + bo

    def _L0_ffn_ref(hidden_states, gate_w, w_gate, w_up, w_down, ws_gate, ws_up, ws_down):
        import jax, jax.numpy as jnp
        import numpy as np
        B, S, H = (4, 512, 256)
        D = 512
        E = 8
        K = 2
        b, s, h = hidden_states.shape
        x = hidden_states.reshape(-1, h)
        scores = jax.nn.softmax(x @ gate_w, axis=-1)
        topk_w, topk_idx = jax.lax.top_k(scores, K)
        topk_w = topk_w / (jnp.sum(topk_w, axis=-1, keepdims=True) + 1e-20)
        onehot = jax.nn.one_hot(topk_idx, E, dtype=x.dtype)
        w_per_expert = jnp.einsum('nke,nk->ne', onehot, topk_w)
        y = jnp.zeros_like(x)
        for e in range(E):
            hid = jax.nn.silu(x @ w_gate[e]) * (x @ w_up[e])
            y = y + w_per_expert[:, e:e + 1] * (hid @ w_down[e])
        shared = jax.nn.silu(x @ ws_gate) * (x @ ws_up) @ ws_down
        return (y + shared).reshape(b, s, h)

    def _L1_attn_ref(x, Wqkv, Wout):
        import jax, jax.numpy as jnp
        import numpy as np
        B, T, D, H = (4, 512, 256, 16)
        HEAD_DIM = D // H
        LOCAL_WINDOW = 128

        def _rotate_half(t):
            t1, t2 = jnp.split(t, 2, axis=-1)
            return jnp.concatenate([-t2, t1], axis=-1)

        def _apply_rope(q, k):
            Tq, d = (q.shape[2], q.shape[3])
            half = d // 2
            theta = 1.0 / 10000.0 ** (jnp.arange(half, dtype=jnp.float32) / half)
            pos = jnp.arange(Tq, dtype=jnp.float32)
            freqs = pos[:, None] * theta[None, :]
            freqs = jnp.concatenate([freqs, freqs], axis=-1)
            cos = jnp.cos(freqs)[None, None]
            sin = jnp.sin(freqs)[None, None]
            q = q * cos + _rotate_half(q) * sin
            k = k * cos + _rotate_half(k) * sin
            return (q, k)
        Bx, Tx, C = x.shape
        h, d, w = (H, HEAD_DIM, LOCAL_WINDOW)
        qkv = x @ Wqkv
        q, k, v = jnp.split(qkv, 3, axis=-1)
        q = q.reshape(Bx, Tx, h, d).transpose(0, 2, 1, 3)
        k = k.reshape(Bx, Tx, h, d).transpose(0, 2, 1, 3)
        v = v.reshape(Bx, Tx, h, d).transpose(0, 2, 1, 3)
        q, k = _apply_rope(q, k)
        idx = jnp.arange(Tx)
        dist = idx[None, :] - idx[:, None]
        allowed = (dist <= 0) & (dist >= -(w - 1))
        scores = jnp.einsum('bhqd,bhkd->bhqk', q, k) / jnp.sqrt(jnp.float32(d))
        scores = jnp.where(allowed[None, None], scores, -jnp.inf)
        weights = jax.nn.softmax(scores, axis=-1)
        out = jnp.einsum('bhqk,bhkd->bhqd', weights, v)
        out = out.transpose(0, 2, 1, 3).reshape(Bx, Tx, C)
        return out @ Wout

    def _L1_xattn_ref(x, context, Wq, Wk, Wv, Wo, bo):
        import jax, jax.numpy as jnp
        import numpy as np
        DIM = 256
        NUM_HEADS = 8
        HEAD_DIM = 64
        INNER = NUM_HEADS * HEAD_DIM
        B, N, _ = x.shape
        M = context.shape[1]
        scale = HEAD_DIM ** (-0.5)
        q = (x @ Wq).reshape(B, N, NUM_HEADS, HEAD_DIM).transpose(0, 2, 1, 3)
        k = (context @ Wk).reshape(B, M, NUM_HEADS, HEAD_DIM).transpose(0, 2, 1, 3)
        v = (context @ Wv).reshape(B, M, NUM_HEADS, HEAD_DIM).transpose(0, 2, 1, 3)
        attn = jax.nn.softmax(jnp.einsum('bhnd,bhmd->bhnm', q, k) * scale, axis=-1)
        out = jnp.einsum('bhnm,bhmd->bhnd', attn, v)
        out = out.transpose(0, 2, 1, 3).reshape(B, N, INNER)
        return out @ Wo + bo

    def _L1_ffn_ref(x, W1, b1, W2, b2):
        import jax, jax.numpy as jnp
        import numpy as np
        HIDDEN = 256
        NUM_EXPERTS = 8
        TOP_K = 2
        B, S = (2, 512)
        Bm, Sm, d = x.shape
        E = W1.shape[0]
        x_flat = x.reshape(-1, d)
        h = jnp.mod(x_flat[:, :TOP_K].sum(axis=1).astype(jnp.int32), E)
        sel = jnp.stack([h, jnp.mod(h + 1, E)], axis=1)

        def step(acc, params):
            e, W1e, b1e, W2e, b2e = params
            w = jnp.any(sel == e, axis=1).astype(x.dtype) / TOP_K
            y = jnp.maximum(x_flat @ W1e + b1e, 0.0) @ W2e + b2e
            return (acc + w[:, None] * y, None)
        init = jnp.zeros_like(x_flat)
        out_flat, _ = jax.lax.scan(step, init, (jnp.arange(E), W1, b1, W2, b2))
        return out_flat.reshape(Bm, Sm, d)
    x = x + _L0_attn_ref(_layernorm(x, axis=-1), L0_attn_Wq, L0_attn_bq, L0_attn_Wk, L0_attn_bk, L0_attn_Wv, L0_attn_bv, L0_attn_Wo, L0_attn_bo)
    x = x + _L0_xattn_ref(_layernorm(x, axis=-1), ctx_1024, ctx_1024, L0_xattn_Wq, L0_xattn_bq, L0_xattn_Wk, L0_xattn_bk, L0_xattn_Wv, L0_xattn_bv, L0_xattn_Wo, L0_xattn_bo)
    x = x + _L0_ffn_ref(_layernorm(x, axis=-1), L0_ffn_gate_w, L0_ffn_w_gate, L0_ffn_w_up, L0_ffn_w_down, L0_ffn_ws_gate, L0_ffn_ws_up, L0_ffn_ws_down)
    x = x + _L1_attn_ref(_layernorm(x, axis=-1), L1_attn_Wqkv, L1_attn_Wout)
    x = x + _L1_xattn_ref(_layernorm(x, axis=-1), ctx_1024, L1_xattn_Wq, L1_xattn_Wk, L1_xattn_Wv, L1_xattn_Wo, L1_xattn_bo)
    x = x + _L1_ffn_ref(_layernorm(x, axis=-1), L1_ffn_W1, L1_ffn_b1, L1_ffn_W2, L1_ffn_b2)
    return x

_drawn_inputs = setup_inputs


def setup_inputs(seed=0):
    import zlib

    import numpy as np

    out = dict(_drawn_inputs(seed))
    spreads = {'L0_attn_bq': (0.0, 0.647),
     'L0_attn_bk': (0.0, 0.473),
     'L0_attn_bv': (0.0, 0.1),
     'L0_attn_bo': (0.0, 0.1),
     'L0_xattn_bq': (0.0, 0.1),
     'L0_xattn_bk': (0.0, 0.8),
     'L0_xattn_bv': (0.0, 0.1),
     'L0_xattn_bo': (0.0, 0.1)}
    factors = {'L1_xattn_bo': 5.013, 'L1_ffn_b1': 8.0, 'L1_ffn_b2': 8.0}
    for name, (base, spread) in spreads.items():
        noise = np.random.default_rng([zlib.crc32(name.encode()), seed]).standard_normal(out[name].shape)
        drawn = base * np.exp(spread * noise) if base else spread * noise
        out[name] = jnp.asarray(drawn.astype(out[name].dtype))
    for name, factor in factors.items():
        out[name] = (out[name] * factor).astype(out[name].dtype)
    return out
```

```python
import numpy as np
from contextlib import ExitStack, contextmanager

import concourse.bass as bass
from concourse import mybir

FP32 = mybir.dt.float32
BF16 = mybir.dt.bfloat16
FP32R = mybir.dt.float32r
I32 = mybir.dt.int32
U32 = mybir.dt.uint32
ALU = mybir.AluOpType
ACT = mybir.ActivationFunctionType
AX = mybir.AxisListType

P = 128
B, S, E = 2, 512, 256
CTX = 1024
N = B * S
NT = N // P
ST = S // P
CT = CTX // P
KE = E // P
H, D = 16, 16
G = H // 4
VW = 32
PARTS = 3
Q_ROWS = (0, 0, 0, 1, 1, 2)
K_ROWS = (0, 1, 2, 0, 1, 0)
ROWS = D * len(Q_ROWS)
MAX_ROWS = 2
H1, D1 = 8, 64
LN_EPS = 1e-5
YAT_EPS = 0.1
NEG = -1e30
TABLE_SET = "natural_log_exp_and_others"


class Scope:

    def __init__(self, nc, ctx, tag):
        self.nc, self.ctx, self.tag, self.sems = nc, ctx, tag, []

    def sb(self, name, shape, dt=FP32):
        return self.ctx.enter_context(self.nc.sbuf_tensor(f"{self.tag}_{name}", shape, dt))

    def ps(self, name, shape=(P, 512), dt=FP32):
        return self.ctx.enter_context(self.nc.psum_tensor(f"{self.tag}_{name}", list(shape), dt))

    def sem(self, name):
        s = self.ctx.enter_context(self.nc.semaphore(f"{self.tag}_{name}"))
        self.sems.append(s)
        return s


@contextmanager
def stage(nc, tag):
    with ExitStack() as ctx:
        s = Scope(nc, ctx, tag)
        yield s
        for sem in s.sems:
            nc.gpsimd.sem_clear(sem)
        nc.all_engine_barrier()


class Pair:

    def __init__(self, hi, lo):
        self.hi, self.lo = hi, lo

    def __getitem__(self, key):
        return Pair(self.hi[key], self.lo[key])

    def rearrange(self, *a, **k):
        return Pair(self.hi.rearrange(*a, **k), self.lo.rearrange(*a, **k))


def matmul3(nc, out, a, b, start, stop):
    nc.tensor.matmul(out, a.hi, b.hi, start=start, stop=False)
    nc.tensor.matmul(out, a.hi, b.lo, start=False, stop=False)
    return nc.tensor.matmul(out, a.lo, b.hi, start=False, stop=stop)


def chain_of(engine, sem):
    n = [0]

    def link(ins):
        n[0] += 1
        ins.then_inc(sem, 1)
        engine.wait_ge(sem, n[0])
    return link


def stage_setup(nc, A, R):
    with stage(nc, "setup") as s:
        ctx_tok = s.sb("ctx_tok", [P, B * CT, E])
        tp = [s.ps(f"tp{i}") for i in range(4)]
        x_in, ctx_in, w_in = s.sem("x_in"), [s.sem(f"ctx_in{b}") for b in range(B)], s.sem("w_in")
        ident_step, ident_ready = s.sem("ident_step"), s.sem("ident_ready")
        transposed, evacuated = s.sem("transposed"), s.sem("evacuated")
        made, high_done = s.sem("made"), s.sem("high_done")
        with nc.Block() as block:

            @block.sync
            def _(sp):
                sp.dma_start(R.x[:, :, :], A["x"].rearrange("b (t p) e -> p (b t) e", p=P)).then_inc(x_in, 16)
                for b in range(B):
                    sp.dma_start(ctx_tok[:, b * CT:(b + 1) * CT, :],
                                 A["ctx_1024"][b].rearrange("(t p) e -> p t e", p=P)).then_inc(ctx_in[b], 16)

                sp.dma_start(R.rope[:, :, :, :], A["rope"].rearrange("c (t p) d -> p c t d", p=P)).then_inc(w_in, 16)
                sp.wait_ge(w_in, 16)
                sp.wait_ge(x_in, 16)

            @block.gpsimd
            def _(pool):
                nc.gpsimd.memset(R.ident[:, :], 0.0).then_inc(ident_step, 1)
                nc.gpsimd.memset(R.ones_row[:, :], 1.0).then_inc(made, 1)
                nc.gpsimd.memset(R.yat_one[:, :], 1.0 + YAT_EPS).then_inc(made, 1)
                nc.gpsimd.memset(R.window[:, :, :], 0.0).then_inc(ident_step, 1)
                pool.wait_ge(ident_step, 1)
                nc.gpsimd.affine_select(out=R.ident[:, :], in_=R.ident[:, :], compare_op=ALU.not_equal, fill=1.0,
                                        base=0, pattern=[[-1, P]], channel_multiplier=1).then_inc(ident_ready, 1)
                pool.wait_ge(ident_step, 2)
                nc.gpsimd.affine_select(out=R.window[:, 0, 0:P], in_=R.window[:, 0, 0:P], compare_op=ALU.is_ge,
                                        fill=NEG, base=0, pattern=[[1, P]], channel_multiplier=-1).then_inc(made, 1)
                nc.gpsimd.affine_select(out=R.window[:, 0, P:2 * P], in_=R.window[:, 0, P:2 * P],
                                        compare_op=ALU.is_gt, fill=NEG, base=0, pattern=[[-1, P]],
                                        channel_multiplier=1).then_inc(made, 1)
                nc.gpsimd.affine_select(out=R.window[:, 1, 0:P], in_=R.window[:, 1, 0:P], compare_op=ALU.is_gt,
                                        fill=NEG, base=0, pattern=[[1, P]], channel_multiplier=-1).then_inc(made, 1)
                nc.gpsimd.affine_select(out=R.window[:, 1, P:2 * P], in_=R.window[:, 1, P:2 * P],
                                        compare_op=ALU.is_ge, fill=NEG, base=0, pattern=[[-1, P]],
                                        channel_multiplier=1).then_inc(made, 1)
                pool.wait_ge(ident_ready, 1)
                nc.gpsimd.tensor_copy(R.ident_b[:, :], R.ident[:, :]).then_inc(made, 1)

            banks = [(b, k, q) for b in range(B) for q in range(CT // 4) for k in range(KE)]

            @block.tensor
            def _(pe):
                pe.wait_ge(ident_ready, 1)
                for n, (b, k, q) in enumerate(banks):
                    pe.wait_ge(ctx_in[b], 16)
                    if n >= 4:
                        pe.wait_ge(evacuated, n - 3)
                    for i in range(4):
                        last = nc.tensor.transpose(tp[n % 4][:, i * P:(i + 1) * P],
                                                   ctx_tok[:, b * CT + 4 * q + i, k * P:(k + 1) * P], R.ident[:, :])
                    last.then_inc(transposed, 1)

            @block.vector
            def _(dve):
                for n, (b, k, q) in enumerate(banks):
                    dve.wait_ge(high_done, n + 1)
                    part = R.ctxT[:, k, b * CTX + q * 512:b * CTX + (q + 1) * 512]
                    nc.vector.tensor_tensor(part.lo, tp[n % 4][:, :], part.hi.bitcast(FP32), ALU.subtract)\
                        .then_inc(evacuated, 1)

            @block.scalar
            def _(act):
                nc.scalar.preload_act_table_set(TABLE_SET)
                for n, (b, k, q) in enumerate(banks):
                    act.wait_ge(transposed, n + 1)
                    nc.scalar.activation(R.ctxT[:, k, b * CTX + q * 512:b * CTX + (q + 1) * 512].hi,
                                         tp[n % 4][:, :], ACT.Copy).then_inc(high_done, 1)


def stage_norm(nc, R, tag, loads=(), padded=None, splits=()):
    with stage(nc, tag) as s:
        stats = s.sb("stats", [P, NT, 6])
        mv = s.sb("mv", [P, NT, 2])
        ve, lnv, r, a, nb = (s.sb(n, [P, NT]) for n in ("ve", "lnv", "r", "a", "nb"))
        tp = [s.ps(f"tp{i}") for i in range(4)]
        step, var_ready, rs_step, rs_ready = s.sem("step"), s.sem("var"), s.sem("rs_step"), s.sem("rs")
        normed, transposed, high_done, evac = s.sem("normed"), s.sem("transposed"), s.sem("high_done"), s.sem("evac")
        w_high, w_low = s.sem("w_high"), s.sem("w_low")
        weights_in, zeroed = s.sem("weights_in"), s.sem("zeroed")
        banks = [(k, q) for q in range(NT // 4) for k in range(KE)]
        with nc.Block() as block:

            @block.gpsimd
            def _(pool):
                if padded is not None:
                    nc.gpsimd.memset(padded[:, :, :], 0.0).then_inc(zeroed, 1)

            @block.sync
            def _(sp):
                if padded is not None:
                    sp.wait_ge(zeroed, 1)
                for dst, src in loads:
                    sp.dma_start(dst, src, allow_slow_non_contiguous=True).then_inc(weights_in, 16)
                if loads:
                    sp.wait_ge(weights_in, 16 * len(loads))

            @block.vector
            def _(dve):
                link = chain_of(dve, step)
                for t in range(NT):
                    ins = nc.vector.bn_stats(stats[:, t, :], R.x[:, t, :])
                link(ins)
                for t in range(NT):
                    ins = nc.vector.bn_aggr(mv[:, t, :], stats[:, t, :])
                link(ins)
                nc.vector.tensor_scalar_add(ve[:, :], mv[:, :, 1], LN_EPS).then_inc(var_ready, 1)
                dve.wait_ge(rs_ready, 1)
                dve.wait_ge(var_ready, 1)
                link(nc.vector.tensor_tensor(a[:, :], r[:, :], r[:, :], ALU.mult))
                link(nc.vector.tensor_tensor(a[:, :], a[:, :], ve[:, :], ALU.mult))
                link(nc.vector.tensor_scalar(a[:, :], a[:, :], -0.5, 1.5, ALU.mult, ALU.add))
                link(nc.vector.tensor_tensor(r[:, :], r[:, :], a[:, :], ALU.mult))
                link(nc.vector.scalar_tensor_tensor(out=nb[:, :], in0=mv[:, :, 0], scalar=-1.0, in1=r[:, :],
                                                    op0=ALU.mult, op1=ALU.mult))
                for t in range(NT):
                    nc.vector.tensor_scalar(R.xn[:, t, :], R.x[:, t, :], r[:, t:t + 1], nb[:, t:t + 1],
                                            ALU.mult, ALU.add).then_inc(normed, 1)
                for n, (k, q) in enumerate(banks):
                    dve.wait_ge(high_done, n + 1)
                    part = R.xnT[:, k, q * 512:(q + 1) * 512]
                    nc.vector.tensor_tensor(part.lo, tp[n][:, :], part.hi.bitcast(FP32), ALU.subtract).then_inc(evac, 1)
                for i, (full, part) in enumerate(splits):
                    dve.wait_ge(w_high, i + 1)
                    nc.vector.tensor_tensor(part.lo, full, part.hi.bitcast(FP32), ALU.subtract).then_inc(w_low, 1)

            @block.scalar
            def _(act):
                nc.scalar.preload_act_table_set(TABLE_SET)
                act.wait_ge(var_ready, 1)
                nc.scalar.activation(lnv[:, :], ve[:, :], ACT.Ln).then_inc(rs_step, 1)
                act.wait_ge(rs_step, 1)
                nc.scalar.activation(r[:, :], lnv[:, :], ACT.Exp, scale=-0.5).then_inc(rs_ready, 1)
                for n, (k, q) in enumerate(banks):
                    act.wait_ge(transposed, n + 1)
                    nc.scalar.activation(R.xnT[:, k, q * 512:(q + 1) * 512].hi, tp[n][:, :], ACT.Copy)\
                        .then_inc(high_done, 1)
                if splits:
                    act.wait_ge(weights_in, 16 * len(loads))
                for full, part in splits:
                    nc.scalar.activation(part.hi, full, ACT.Copy).then_inc(w_high, 1)

            @block.tensor
            def _(pe):
                for n, (k, q) in enumerate(banks):
                    for i in range(4):
                        pe.wait_ge(normed, 4 * q + i + 1)
                        last = nc.tensor.transpose(tp[n][:, i * P:(i + 1) * P],
                                                   R.xn[:, 4 * q + i, k * P:(k + 1) * P], R.ident[:, :])
                    last.then_inc(transposed, 1)


def stage_project(nc, R, tag, m, b, kind, wq, wk, wv, bq=None, bk=None, bv=None):
    cross = kind == "cross"
    src, t0, kt_n = (R.ctxT, b * CTX, CT) if cross else (R.xnT, b * S, ST)
    keys = kt_n * P
    chunks = [("q", k, 0) for k in range(KE)] + [("k", k, c) for c in range(keys // 512) for k in range(KE)]
    n_tok = 0 if cross else 2 * ST
    with stage(nc, f"{tag}p{b}") as s:
        qc = s.sb("qc", [P, PARTS, KE, S], BF16)
        kc = s.sb("kc", [P, PARTS, KE, keys], BF16)
        rest = s.sb("rest", [P, 2, 512])
        feat = [s.ps(f"feat{i}") for i in range(4)]
        vps = [s.ps(f"v{i}") for i in range(2)]
        tok = [s.ps(f"tok{i}") for i in range(2)]
        if n_tok:
            qk = s.sb("qk", [P, n_tok, E])
            aux = s.sb("aux", [P, n_tok, E])
            ss, lns = s.sb("ss", [P, n_tok, H]), s.sb("lns", [P, n_tok, H])
        tok_mm, tok_evac, tok_ready = s.sem("tok_mm"), s.sem("tok_evac"), s.sem("tok_ready")
        squared, ss_ready, norm_step, norm_ready = (s.sem(n) for n in ("squared", "ss_ready", "norm_step", "norm_ready"))
        v_mm, v_evac = s.sem("v_mm"), s.sem("v_evac")
        feat_ready, high_ready, rest_ready, rest_used = (s.sem(n) for n in ("feat", "high", "rest", "rest_used"))
        dve_step, middle_ready, stored, stacked, ones = (s.sem(n) for n in ("dve_step", "middle_ready", "stored", "stacked", "ones"))

        def part_of(chunk, part):
            which, k, c = chunk
            return qc[:, part, k, :] if which == "q" else kc[:, part, k, c * 512:(c + 1) * 512]

        with nc.Block() as block:

            @block.tensor
            def _(pe):
                for n in range(n_tok):
                    t, w = n // 2, (wq, wk)[n % 2]
                    if n >= 2:
                        pe.wait_ge(tok_evac, n - 1)
                    for k in range(KE):
                        last = matmul3(nc, tok[n % 2][:, 0:E], R.xnT[:, k, b * S + t * P:b * S + (t + 1) * P],
                                                w[:, k, :], start=k == 0, stop=k == KE - 1)
                    last.then_inc(tok_mm, 1)

                def value(n):
                    if n >= 2:
                        pe.wait_ge(v_evac, n - 1)
                    for i in range(2):
                        at = t0 + (2 * n + i) * P
                        for k in range(KE):
                            last = matmul3(nc, vps[n % 2][:, i * E:(i + 1) * E], src[:, k, at:at + P],
                                                    wv[:, k, :], start=k == 0, stop=k == KE - 1)
                    last.then_inc(v_mm, 1)
                if not cross:
                    for n in range(kt_n // 2):
                        value(n)
                for n, (which, mt, c) in enumerate(chunks):
                    if n >= 4:
                        pe.wait_ge(rest_ready, n - 3)
                    if cross:
                        w, x, at = (wq, R.xnT, b * S) if which == "q" else (wk, src, t0 + c * 512)
                        for k in range(KE):
                            last = matmul3(nc, feat[n % 4][:, :], w[:, k, mt * P:(mt + 1) * P],
                                                    x[:, k, at:at + 512], start=k == 0, stop=k == KE - 1)
                    else:
                        pe.wait_ge(tok_ready, n_tok)
                        for t in range(ST):
                            last = nc.tensor.transpose(feat[n % 4][:, t * P:(t + 1) * P],
                                                       qk[:, 2 * t + (which == "k"), mt * P:(mt + 1) * P],
                                                       R.ident[:, :])
                    last.then_inc(feat_ready, 1)
                if cross:
                    for n in range(kt_n // 2):
                        value(n)

            @block.scalar
            def _(act):
                nc.scalar.preload_act_table_set(TABLE_SET)
                if kind == "yat":
                    act.wait_ge(ss_ready, 1)
                    nc.scalar.activation(lns[:, :, :], ss[:, :, :], ACT.Ln).then_inc(norm_step, 1)
                    act.wait_ge(norm_step, 1)
                    nc.scalar.activation(lns[:, :, :], lns[:, :, :], ACT.Exp, scale=0.5).then_inc(norm_ready, 1)
                for n, chunk in enumerate(chunks):
                    bias = {"q": bq, "k": bk}[chunk[0]] if cross else None
                    act.wait_ge(feat_ready, n + 1)
                    if bias is None:
                        nc.scalar.activation(part_of(chunk, 0), feat[n % 4][:, :], ACT.Copy).then_inc(high_ready, 1)
                    else:
                        nc.scalar.activation(part_of(chunk, 0), feat[n % 4][:, :], ACT.Identity,
                                             bias=bias[:, chunk[1]:chunk[1] + 1]).then_inc(high_ready, 1)

            @block.vector
            def _(dve):
                link = chain_of(dve, dve_step)
                heads = lambda ap: ap.rearrange("p (h d) -> p h d", d=D)

                def value(n):
                    dve.wait_ge(v_mm, n + 1)
                    out = m.vaug[:, 2 * n:2 * n + 2, :, 0:D]
                    ps = vps[n % 2][:, :].rearrange("p (i h d) -> p i h d", i=2, d=D)
                    for i in range(2):
                        if bv is not None:
                            ins = nc.vector.tensor_tensor(out[:, i], ps[:, i], heads(bv[:, :]), ALU.add)
                        else:
                            ins = nc.vector.tensor_copy(out[:, i], ps[:, i])
                    ins.then_inc(v_evac, 1)
                if kind == "yat":
                    for n in range(n_tok + 1):
                        if n < n_tok:
                            dve.wait_ge(tok_mm, n + 1)
                            nc.vector.tensor_tensor(qk[:, n, :], tok[n % 2][:, 0:E], (bq, bk)[n % 2][:, :], ALU.add)\
                                .then_inc(tok_evac, 1)
                        if n >= 1:
                            dve.wait_ge(squared, n)
                            ins = nc.vector.tensor_reduce(out=ss[:, n - 1, :], in_=heads(aux[:, n - 1, :]),
                                                          op=ALU.add, axis=AX.X)
                    link(ins)
                    nc.vector.tensor_scalar_max(ss[:, :, :], ss[:, :, :], 1e-19).then_inc(ss_ready, 1)
                    for n in range(kt_n // 2):
                        value(n)
                    dve.wait_ge(norm_ready, 1)
                    link(nc.vector.tensor_scalar_add(lns[:, :, :], lns[:, :, :], 1e-8))
                    link(nc.vector.reciprocal(lns[:, :, :], lns[:, :, :]))
                    for n in range(n_tok):
                        nc.vector.tensor_tensor(heads(qk[:, n, :]), heads(qk[:, n, :]),
                                                lns[:, n, :].unsqueeze(2).broadcast_to([P, H, D]), ALU.mult)\
                            .then_inc(tok_ready, 1)
                if kind == "rope":
                    half = D // 2
                    for n in range(n_tok):
                        dve.wait_ge(tok_mm, n + 1)
                        ps, a, r = heads(tok[n % 2][:, 0:E]), heads(qk[:, n, :]), heads(aux[:, n, :])
                        table = lambda c, lo, hi: R.rope[:, c, n // 2, lo:hi].unsqueeze(1).broadcast_to([P, H, hi - lo])
                        nc.vector.tensor_tensor(a, ps, table(0, 0, D), ALU.mult)
                        nc.vector.tensor_tensor(r[:, :, 0:half], ps[:, :, half:D], table(1, 0, half), ALU.mult)
                        nc.vector.tensor_tensor(r[:, :, half:D], ps[:, :, 0:half], table(1, half, D), ALU.mult)\
                            .then_inc(tok_evac, 1)
                    for n in range(kt_n // 2):
                        value(n)
                for n, chunk in enumerate(chunks):
                    bias = {"q": bq, "k": bk}[chunk[0]] if cross else None
                    dve.wait_ge(high_ready, n + 1)
                    if n >= 2:
                        dve.wait_ge(rest_used, n - 1)
                    nc.vector.scalar_tensor_tensor(
                        out=rest[:, n % 2, :], in0=feat[n % 4][:, :],
                        scalar=0.0 if bias is None else bias[:, chunk[1]:chunk[1] + 1],
                        in1=part_of(chunk, 0), op0=ALU.add, op1=ALU.subtract).then_inc(rest_ready, 1)
                    dve.wait_ge(rest_ready, n + 1)
                    nc.vector.tensor_copy(part_of(chunk, 1), rest[:, n % 2, :]).then_inc(middle_ready, 1)
                if cross:
                    for n in range(kt_n // 2):
                        value(n)

            @block.gpsimd
            def _(pool):
                if b == 0:
                    nc.gpsimd.memset(m.vaug[:, :, :, D:VW], 1.0).then_inc(ones, 1)
                    pool.wait_ge(ones, 1)
                    if kind != "yat":
                        nc.gpsimd.memset(m.kst[ROWS:ROWS + MAX_ROWS, :, :], 1.0).then_inc(ones, 1)
                        pool.wait_ge(ones, 2)
                for n in range(n_tok):
                    pool.wait_ge(tok_evac, n + 1)
                    if kind == "yat":
                        nc.gpsimd.tensor_tensor(aux[:, n, :], qk[:, n, :], qk[:, n, :], ALU.mult).then_inc(squared, 1)
                    else:
                        nc.gpsimd.tensor_tensor(qk[:, n, :], qk[:, n, :], aux[:, n, :], ALU.add).then_inc(tok_ready, 1)
                for n, chunk in enumerate(chunks):
                    pool.wait_ge(middle_ready, n + 1)
                    nc.gpsimd.tensor_tensor(part_of(chunk, 2), rest[:, n % 2, :], part_of(chunk, 1), ALU.subtract)\
                        .then_inc(rest_used, 1)

            @block.sync
            def _(sp):
                total = 0
                for comp, scratch, rows, stack, ready in ((qc, m.q_dram, Q_ROWS, m.qst, KE),
                                                          (kc, m.k_dram, K_ROWS, m.kst, len(chunks))):
                    sp.wait_ge(rest_used, ready)
                    for part in range(PARTS):
                        sp.dma_start(scratch[part].rearrange("(k p) t -> p k t", p=P), comp[:, part, :, :])\
                            .then_inc(stored, 16)
                    total += 16 * PARTS
                    sp.wait_ge(stored, total)
                    for i, part in enumerate(rows):
                        sp.dma_start(stack[D * i:D * (i + 1), :, :],
                                     scratch[part].rearrange("(h d) t -> d h t", d=D)).then_inc(stacked, 16)
                sp.wait_ge(stacked, 16 * (len(Q_ROWS) + len(K_ROWS)))


def stage_max(nc, R, tag, m, b, kind):
    kt_n = CT if kind == "cross" else ST
    with stage(nc, f"{tag}m{b}") as s:
        mx = s.sb("mx", [P, ST, H])
        neg = s.sb("neg", [H, MAX_ROWS, S], BF16)
        sc = [s.ps(f"sc{i}", [P, 1024]) for i in range(3)]
        mxt = s.ps("mxt")
        ready, reduced, transposed, step, negated, placed = (s.sem(n) for n in (
            "ready", "reduced", "transposed", "step", "negated", "placed"))
        units = [(h, qt) for h in range(H) for qt in range(ST)] if kind == "cross" else [(h, 0) for h in range(H)]
        with nc.Block() as block:

            @block.tensor
            def _(pe):
                for n, (h, qt) in enumerate(units):
                    ps = sc[n % 3]
                    if n >= 3:
                        pe.wait_ge(reduced, n - 2)
                    if kind == "cross":
                        for c in range(2):
                            last = nc.tensor.matmul(ps[:, c * 512:(c + 1) * 512],
                                                    m.qst[0:ROWS, h, qt * P:(qt + 1) * P],
                                                    m.kst[0:ROWS, h, c * 512:(c + 1) * 512], start=True, stop=True)
                    else:
                        for t in range(ST):
                            lo = 0 if t else P
                            out = ps[:, 2 * P * t + lo:2 * P * (t + 1)]
                            nc.tensor.matmul(out, R.ident_b[:, :], R.window[:, 1, lo:], start=True, stop=False)
                            last = nc.tensor.matmul(out, m.qst[0:ROWS, h, t * P:(t + 1) * P],
                                                    m.kst[0:ROWS, h, (t - 1) * P + lo:(t + 1) * P],
                                                    start=False, stop=True)
                    last.then_inc(ready, 1)
                pe.wait_ge(reduced, len(units))
                for t in range(ST):
                    last = nc.tensor.transpose(mxt[0:H, t * P:(t + 1) * P], mx[:, t, :], R.ident[:, :])
                last.then_inc(transposed, 1)

            @block.vector
            def _(dve):
                for n, (h, qt) in enumerate(units):
                    dve.wait_ge(ready, n + 1)
                    if kind == "cross":
                        nc.vector.tensor_reduce(out=mx[:, qt, h:h + 1], in_=sc[n % 3][:, :], op=ALU.max, axis=AX.X)\
                            .then_inc(reduced, 1)
                    else:
                        nc.vector.tensor_reduce(out=mx[:, 0, h:h + 1], in_=sc[n % 3][:, P:2 * P], op=ALU.max, axis=AX.X)
                        nc.vector.tensor_reduce(out=mx[:, 1:ST, h],
                                                in_=sc[n % 3][:, 2 * P:].rearrange("p (t k) -> p t k", t=ST - 1),
                                                op=ALU.max, axis=AX.X).then_inc(reduced, 1)
                dve.wait_ge(transposed, 1)
                nc.vector.tensor_scalar(neg[:, 0, :], mxt[0:H, :], -1.0, None, ALU.mult).then_inc(step, 1)
                dve.wait_ge(step, 1)
                nc.vector.scalar_tensor_tensor(out=neg[:, 1, :], in0=mxt[0:H, :], scalar=-1.0, in1=neg[:, 0, :],
                                               op0=ALU.mult, op1=ALU.subtract).then_inc(negated, 1)

            @block.sync
            def _(sp):
                sp.wait_ge(negated, 1)
                for i in range(MAX_ROWS):
                    sp.dma_start(m.qst[ROWS + i:ROWS + i + 1, :, :], neg[:, i, :]).then_inc(placed, 16)
                sp.wait_ge(placed, 16 * MAX_ROWS)


def stage_attend(nc, R, tag, m, b, kind):
    yat, window = kind == "yat", kind == "rope"
    kt_n = CT if kind == "cross" else ST
    QPG = 1 if window else kt_n // 2
    UPG = 4 * QPG
    units = G * UPG
    cols = 7 * P if window else 1024
    rows = ROWS if yat else ROWS + MAX_ROWS
    PR = 8
    base = [2 * P * t for t in range(ST)]
    width = [2 * P] * (ST - 1) + [P]
    with stage(nc, f"{tag}a{b}") as s:
        probs = s.sb("probs", [P, PR, 1024])
        lnb = s.sb("lnb", [P, 3, 1024]) if yat else None
        den, rec, tmp = (s.sb(n, [P, 2, 512]) for n in ("den", "rec", "tmp"))
        sc = [s.ps(f"sc{i}", [P, 1024]) for i in range(3)]
        acc = [s.ps(f"acc{i}") for i in range(2)]
        scores_ready, probs_ready, pv_done = s.sem("scores_ready"), s.sem("probs_ready"), s.sem("pv_done")
        ln_done, rec_done, once_done = s.sem("ln_done"), s.sem("rec_done"), s.sem("once_done")
        den_step, den_ready, den_ln, den_rec, step, acc_free = (s.sem(n) for n in (
            "den_step", "den_ready", "den_ln", "den_rec", "step", "acc_free"))

        def head(u):
            return 4 * (u // UPG) + u % 4

        def after(u):
            g = u // UPG - 1
            return g if g >= 0 and u % UPG == min(6, UPG - 1) else None

        with nc.Block() as block:

            @block.tensor
            def _(pe):
                def scores(u):
                    ps, h, kp = sc[u % 3], head(u), (u % UPG) // 4
                    if u >= 3:
                        pe.wait_ge(probs_ready, u - 2)
                    if window:
                        for t in range(ST):
                            out = ps[:, base[t]:base[t] + width[t]]
                            nc.tensor.matmul(out, R.ident_b[:, :], R.window[:, 0, 0:width[t]], start=True, stop=False)
                            last = nc.tensor.matmul(out, m.kst[0:rows, h, t * P:(t + 1) * P],
                                                    m.qst[0:rows, h, t * P:t * P + width[t]], start=False, stop=True)
                    else:
                        for i in range(2):
                            kt = 2 * kp + i
                            last = nc.tensor.matmul(ps[:, i * 512:(i + 1) * 512], m.kst[0:rows, h, kt * P:(kt + 1) * P],
                                                    m.qst[0:rows, h, :], start=True, stop=True)
                    last.then_inc(scores_ready, 1)

                def pv(quad, piece):
                    g, kp = quad // QPG, quad % QPG
                    if piece == 0:
                        pe.wait_ge(probs_ready, 4 * quad + 4)
                        if kp == 0 and g >= 2:
                            pe.wait_ge(acc_free, g - 1)
                    out, last = acc[g % 2], None
                    if window:
                        for kt in ([piece] if piece == 0 else [piece - 1, piece]):
                            at = base[kt] + (P if kt < piece else 0)
                            for j in range(4):
                                last = nc.tensor.matmul(
                                    out[VW * j:VW * (j + 1), piece * P:(piece + 1) * P], m.vaug[:, kt, 4 * g + j, :],
                                    probs[:, (4 * quad + j) % PR, at:at + P],
                                    start=kt == max(piece - 1, 0), stop=kt == piece)
                    else:
                        i, kt = piece // 2, 2 * kp + piece // 2
                        for j in (2 * (piece % 2), 2 * (piece % 2) + 1):
                            last = nc.tensor.matmul(
                                out[VW * j:VW * (j + 1), :], m.vaug[:, kt, 4 * g + j, :],
                                probs[:, (4 * quad + j) % PR, i * 512:(i + 1) * 512],
                                start=kt == 0, stop=kt == kt_n - 1)
                    if piece == 3:
                        last.then_inc(pv_done, 1)

                lag = 6 if yat else 4
                for u in range(units + lag):
                    if u < units:
                        scores(u)
                    if u >= lag:
                        pv((u - lag) // 4, (u - lag) % 4)

            @block.scalar
            def _(act):
                nc.scalar.preload_act_table_set(TABLE_SET)
                def weights(u):
                    act.wait_ge(scores_ready, u + 1)
                    if u >= PR:
                        act.wait_ge(pv_done, (u - PR) // 4 + 1)
                    nc.scalar.activation(probs[:, u % PR, 0:cols], sc[u % 3][:, 0:cols], ACT.Exp,
                                         scale=float(D) ** -0.5).then_inc(probs_ready, 1)

                def ln_of(u):
                    act.wait_ge(scores_ready, u + 1)
                    if u >= 3:
                        act.wait_ge(once_done, u - 2)
                    nc.scalar.activation(lnb[:, u % 3, :], sc[u % 3][:, :], ACT.Ln, bias=R.yat_one[:, 0:1], scale=-1.0)\
                        .then_inc(ln_done, 1)

                def rec_of(u):
                    act.wait_ge(ln_done, u + 1)
                    nc.scalar.activation(lnb[:, u % 3, :], lnb[:, u % 3, :], ACT.Exp, scale=-1.0).then_inc(rec_done, 1)

                def sums(g):
                    act.wait_ge(den_ready, g + 1)
                    nc.scalar.activation(rec[:, g % 2, :], den[:, g % 2, :], ACT.Ln).then_inc(den_ln, 1)
                    act.wait_ge(den_ln, g + 1)
                    nc.scalar.activation(rec[:, g % 2, :], rec[:, g % 2, :], ACT.Exp, scale=-1.0).then_inc(den_rec, 1)
                for u in range(units):
                    if yat:
                        ln_of(u)
                        rec_of(u)
                    else:
                        weights(u)
                    if after(u) is not None:
                        sums(after(u))
                sums(G - 1)

            @block.vector
            def _(dve):
                link = chain_of(dve, step)

                def once(u):
                    dve.wait_ge(rec_done, u + 1)
                    nc.vector.scalar_tensor_tensor(out=lnb[:, u % 3, :], in0=sc[u % 3][:, :], scalar=1.0,
                                                   in1=lnb[:, u % 3, :], op0=ALU.add, op1=ALU.mult).then_inc(once_done, 1)

                def twice(u):
                    dve.wait_ge(once_done, u + 1)
                    if u >= PR:
                        dve.wait_ge(pv_done, (u - PR) // 4 + 1)
                    nc.vector.scalar_tensor_tensor(out=probs[:, u % PR, :], in0=sc[u % 3][:, :], scalar=1.0,
                                                   in1=lnb[:, u % 3, :], op0=ALU.add, op1=ALU.mult).then_inc(probs_ready, 1)

                def sums(g):
                    a, d, r, t = acc[g % 2][:, :], den[:, g % 2, :], rec[:, g % 2, :], tmp[:, g % 2, :]
                    dve.wait_ge(pv_done, (g + 1) * QPG)
                    if yat:
                        link(nc.vector.stream_shuffle(d, a, [D + i % D for i in range(VW)]))
                        nc.vector.tensor_scalar_add(d, d, 1e-6).then_inc(den_ready, 1)
                    else:
                        nc.vector.stream_shuffle(d, a, [D + i % D for i in range(VW)]).then_inc(den_ready, 1)
                    dve.wait_ge(den_rec, g + 1)
                    link(nc.vector.tensor_tensor(t, d, r, ALU.mult))
                    link(nc.vector.scalar_tensor_tensor(out=t, in0=t, scalar=-2.0, in1=r, op0=ALU.add, op1=ALU.mult))
                    nc.vector.scalar_tensor_tensor(out=m.outT[:, g, :], in0=a, scalar=-1.0, in1=t,
                                                   op0=ALU.mult, op1=ALU.mult).then_inc(acc_free, 1)
                for u in range(units):
                    if after(u) is not None:
                        sums(after(u))
                    if yat:
                        once(u)
                        twice(u)
                sums(G - 1)


def stage_out(nc, R, tag, outT, w, bias, b):
    with stage(nc, f"{tag}o{b}") as s:
        ps = [s.ps(f"y{i}") for i in range(ST)]
        ready, added = s.sem("ready"), s.sem("added")
        with nc.Block() as block:

            @block.tensor
            def _(pe):
                for t in range(ST):
                    for g in range(G):
                        last = nc.tensor.matmul(ps[t][:, 0:E], outT[:, g, t * P:(t + 1) * P], w[:, g, :],
                                                start=g == 0, stop=bias is None and g == G - 1)
                    if bias is not None:
                        last = nc.tensor.matmul(ps[t][:, 0:E], R.ones_row[:, :], bias[:, :], start=False, stop=True)
                    last.then_inc(ready, 1)

            @block.vector
            def _(dve):
                for t in range(ST):
                    dve.wait_ge(ready, t + 1)
                    nc.vector.tensor_tensor(R.x[:, b * ST + t, :], R.x[:, b * ST + t, :], ps[t][:, 0:E], ALU.add)\
                        .then_inc(added, 1)


def attention16(nc, A, R, tag, kind, wq, wk, wv, wo, bq=None, bk=None, bv=None, bo=None):
    keys = CTX if kind == "cross" else S
    with ExitStack() as ctx:
        m = Resident()

        def sb(name, shape, dt=FP32):
            return ctx.enter_context(nc.sbuf_tensor(f"{tag}_{name}", shape, dt))
        m.qst = sb("qst", [ROWS + MAX_ROWS, H, S], BF16)
        m.kst = sb("kst", [ROWS + MAX_ROWS, H, keys], BF16)
        m.vaug = sb("vaug", [P, keys // P, H, VW])
        m.outT = R.xn[:, :, :].rearrange("p (g a) e -> p g (a e)", g=G)
        m.q_dram = nc.dram_tensor(f"{tag}_q_parts", (PARTS, E, S), BF16, kind="Internal").ap()
        m.k_dram = nc.dram_tensor(f"{tag}_k_parts", (PARTS, E, keys), BF16, kind="Internal").ap()
        w_full = [sb(n, [P, KE, E]) for n in ("wq", "wk", "wv")]
        w = [Pair(sb(n + "h", [P, KE, E], FP32R), sb(n + "l", [P, KE, E], FP32R)) for n in ("wq", "wk", "wv")]
        splits = [(f[:, :, :], p[:, :, :]) for f, p in zip(w_full, w)]
        w_out = sb("wo", [P, G, E])
        loads = [(t[:, :, :], a.rearrange("(k p) n -> p k n", p=P)) for t, a in zip(w_full, (wq, wk, wv))]
        wo_j = wo.rearrange("(g j d) n -> j d g n", g=G, j=4)
        loads += [(w_out[VW * j:VW * j + D, :, :], wo_j[j]) for j in range(4)]
        bias = []
        for n, a in (("bq", bq), ("bk", bk)):
            t = None
            if a is not None:
                t = sb(n, [P, KE]) if kind == "cross" else sb(n, [P, E])
                loads.append((t[:, :], a.rearrange("(m p) -> p m", p=P) if kind == "cross" else a.partition_broadcast(P)))
            bias.append(t)
        if bv is not None:
            bias.append(sb("bv", [P, E]))
            loads.append((bias[2][:, :], bv.partition_broadcast(P)))
        b_out = None
        if bo is not None:
            b_out = sb("bo", [1, E])
            loads.append((b_out[:, :], bo.rearrange("(a n) -> a n", a=1)))
        stage_norm(nc, R, f"{tag}n", loads, w_out, splits)
        for b in range(B):
            stage_project(nc, R, tag, m, b, kind, *w, *bias)
            if kind != "yat":
                stage_max(nc, R, tag, m, b, kind)
            stage_attend(nc, R, tag, m, b, kind)
            stage_out(nc, R, tag, m.outT, w_out, b_out, b)


def stage_project_wide(nc, R, m, b, wq, wk, wv):
    chunks = [("q", mt, 0) for mt in range(H1 // 2)] + [("k", mt, c) for c in range(CTX // 512) for mt in range(H1 // 2)]
    with stage(nc, f"cp{b}") as s:
        feat = [s.ps(f"feat{i}") for i in range(5)]
        vps = [s.ps(f"v{i}") for i in range(3)]
        feat_ready, even_done, odd_done, copied, v_mm, v_evac, pads = (s.sem(n) for n in (
            "feat_ready", "even_done", "odd_done", "copied", "v_mm", "v_evac", "pads"))

        with nc.Block() as block:

            @block.tensor
            def _(pe):
                for n, (which, mt, c) in enumerate(chunks):
                    if n >= 5:
                        pe.wait_ge(even_done, n - 4)
                        pe.wait_ge(odd_done, n - 4)
                    w, x, at = (wq, R.xnT, b * S) if which == "q" else (wk, R.ctxT, b * CTX + c * 512)
                    for k in range(KE):
                        last = matmul3(nc, feat[n % 5][:, :], w[:, k, mt * P:(mt + 1) * P], x[:, k, at:at + 512],
                                                start=k == 0, stop=k == KE - 1)
                    last.then_inc(feat_ready, 1)
                for kt in range(CT):
                    if kt >= 3:
                        pe.wait_ge(v_evac, kt - 2)
                    for k in range(KE):
                        last = matmul3(nc, vps[kt % 3][:, :], R.ctxT[:, k, b * CTX + kt * P:b * CTX + (kt + 1) * P],
                                                wv[:, k, :], start=k == 0, stop=k == KE - 1)
                    last.then_inc(v_mm, 1)

            def target(which, wide):
                return {("q", 1): m.q, ("k", 1): m.k, ("q", 0): m.qb, ("k", 0): m.kb}[(which, wide)]

            @block.scalar
            def _(act):
                nc.scalar.preload_act_table_set(TABLE_SET)
                act.wait_ge(pads, 2)
                for n, (which, mt, c) in enumerate(chunks):
                    act.wait_ge(feat_ready, n + 1)
                    nc.scalar.activation(target(which, 1)[0:D1, 2 * mt, c * 512:(c + 1) * 512],
                                         feat[n % 5][0:D1, :], ACT.Copy).then_inc(even_done, 1)

            @block.vector
            def _(dve):
                dve.wait_ge(pads, 2)
                for n, (which, mt, c) in enumerate(chunks):
                    dve.wait_ge(feat_ready, n + 1)
                    nc.vector.tensor_copy(target(which, 1)[0:D1, 2 * mt + 1, c * 512:(c + 1) * 512],
                                          feat[n % 5][D1:P, :]).then_inc(odd_done, 1)
                for kt in range(CT):
                    dve.wait_ge(v_mm, kt + 1)
                    ps = vps[kt % 3][:, :].rearrange("p (h o d) -> p h o d", o=2, d=D1)
                    out = m.vaug[:, kt, :, :].rearrange("p (h o) (u d) -> p h o u d", o=2, u=2)
                    nc.vector.tensor_copy(out[:, :, 0, 0, :], ps[:, :, 0, :])
                    nc.vector.tensor_copy(out[:, :, 1, 1, :], ps[:, :, 1, :]).then_inc(v_evac, 1)

            @block.gpsimd
            def _(pool):
                if b == 0:
                    nc.gpsimd.memset(m.q[D1:P, :, :], 0.0).then_inc(pads, 1)
                    nc.gpsimd.memset(m.k[D1:P, :, :], 0.0).then_inc(copied, 1)
                    pool.wait_ge(copied, 1)
                    nc.gpsimd.memset(m.k[D1:D1 + 1, :, :], 1.0).then_inc(pads, 1)
                    pool.wait_ge(pads, 2)
                    v = m.vaug[:, :, :, :].rearrange("p t (h o) (u d) -> p (t h) o u d", o=2, u=2)
                    nc.gpsimd.memset(v[:, :, 0, 1, :], 1.0).then_inc(pads, 1)
                    nc.gpsimd.memset(v[:, :, 1, 0, :], 1.0).then_inc(pads, 1)
                    pool.wait_ge(pads, 4)
                else:
                    nc.gpsimd.nop().then_inc(pads, 2)
                for n, (which, mt, c) in enumerate(chunks):
                    pool.wait_ge(even_done, n + 1)
                    pool.wait_ge(odd_done, n + 1)
                    nc.gpsimd.tensor_copy(target(which, 0)[:, 2 * mt:2 * mt + 2, c * 512:(c + 1) * 512],
                                          target(which, 1)[0:D1, 2 * mt:2 * mt + 2, c * 512:(c + 1) * 512])


def stage_max_wide(nc, R, m, b):
    with stage(nc, f"cm{b}") as s:
        mx = s.sb("mx", [P, ST, H1])
        neg = s.sb("neg", [H1, S])
        sc = [s.ps(f"sc{i}", [P, 1024]) for i in range(3)]
        mxt = s.ps("mxt")
        ready, reduced, transposed, negated, placed = (s.sem(n) for n in (
            "ready", "reduced", "transposed", "negated", "placed"))
        units = [(h, qt) for h in range(H1) for qt in range(ST)]
        with nc.Block() as block:

            @block.tensor
            def _(pe):
                for n, (h, qt) in enumerate(units):
                    if n >= 3:
                        pe.wait_ge(reduced, n - 2)
                    for c in range(2):
                        last = nc.tensor.matmul(sc[n % 3][:, c * 512:(c + 1) * 512], m.qb[:, h, qt * P:(qt + 1) * P],
                                                m.kb[:, h, c * 512:(c + 1) * 512], start=True, stop=True)
                    last.then_inc(ready, 1)
                pe.wait_ge(reduced, len(units))
                for t in range(ST):
                    last = nc.tensor.transpose(mxt[0:H1, t * P:(t + 1) * P], mx[:, t, :], R.ident[:, :])
                last.then_inc(transposed, 1)

            @block.vector
            def _(dve):
                for n, (h, qt) in enumerate(units):
                    dve.wait_ge(ready, n + 1)
                    nc.vector.tensor_reduce(out=mx[:, qt, h:h + 1], in_=sc[n % 3][:, :], op=ALU.max, axis=AX.X)\
                        .then_inc(reduced, 1)
                dve.wait_ge(transposed, 1)
                nc.vector.tensor_scalar(neg[:, :], mxt[0:H1, :], -1.0, None, ALU.mult).then_inc(negated, 1)

            @block.sync
            def _(sp):
                sp.wait_ge(negated, 1)
                sp.dma_start(m.q[D1:D1 + 1, :, :], neg[:, :]).then_inc(placed, 16)
                sp.wait_ge(placed, 16)


def stage_attend_wide(nc, R, m, b):
    KP = CT // 2
    units = H1 * KP
    PR = 4
    with stage(nc, f"ca{b}") as s:
        probs = m.scratch[:, 0:PR * 1024].rearrange("p (u n) -> p u n", u=PR)
        den, rec = (m.scratch[:, (PR + i) * 1024:(PR + i + 1) * 1024].rearrange("p (g n) -> p g n", g=2) for i in range(2))
        tmp = s.sb("tmp", [P, 2, 512])
        sc = [s.ps(f"sc{i}", [P, 1024]) for i in range(2)]
        acc = [s.ps(f"acc{i}") for i in range(4)]
        scores_ready, probs_ready, pv_done = s.sem("scores_ready"), s.sem("probs_ready"), s.sem("pv_done")
        den_ready, den_ln, den_rec, step, acc_free = (s.sem(n) for n in ("den_ready", "den_ln", "den_rec", "step", "acc_free"))
        with nc.Block() as block:

            @block.tensor
            def _(pe):
                def scores(u):
                    h, kp = u // KP, u % KP
                    if u >= 2:
                        pe.wait_ge(probs_ready, u - 1)
                    for i in range(2):
                        kt = 2 * kp + i
                        last = nc.tensor.matmul(sc[u % 2][:, i * 512:(i + 1) * 512], m.k[:, h, kt * P:(kt + 1) * P],
                                                m.q[:, h, :], start=True, stop=True)
                    last.then_inc(scores_ready, 1)

                def pv(u):
                    h, kp = u // KP, u % KP
                    pe.wait_ge(probs_ready, u + 1)
                    if h >= 4 and kp == 0:
                        pe.wait_ge(acc_free, h // 2 - 1)
                    for i in range(2):
                        kt = 2 * kp + i
                        last = nc.tensor.matmul(acc[h % 4][:, :], m.vaug[:, kt, h, :],
                                                probs[:, u % PR, i * 512:(i + 1) * 512], start=kt == 0, stop=kt == CT - 1)
                    last.then_inc(pv_done, 1)
                for u in range(units + 1):
                    if u < units:
                        scores(u)
                    if u >= 1:
                        pv(u - 1)

            def after(u):
                g = (u - 3) // (2 * KP) - 1
                return g if g >= 0 and (u - 3) % (2 * KP) == 0 else None

            @block.scalar
            def _(act):
                nc.scalar.preload_act_table_set(TABLE_SET)
                def sums(g):
                    act.wait_ge(den_ready, g + 1)
                    nc.scalar.activation(rec[:, g % 2, :], den[:, g % 2, :], ACT.Ln).then_inc(den_ln, 1)
                    act.wait_ge(den_ln, g + 1)
                    nc.scalar.activation(rec[:, g % 2, :], rec[:, g % 2, :], ACT.Exp, scale=-1.0).then_inc(den_rec, 1)
                for u in range(units):
                    act.wait_ge(scores_ready, u + 1)
                    if u >= PR:
                        act.wait_ge(pv_done, u - PR + 1)
                    nc.scalar.activation(probs[:, u % PR, :], sc[u % 2][:, :], ACT.Exp, scale=float(D1) ** -0.5)\
                        .then_inc(probs_ready, 1)
                    if after(u) is not None:
                        sums(after(u))
                sums(H1 // 2 - 1)

            @block.vector
            def _(dve):
                link = chain_of(dve, step)
                for g in range(H1 // 2):
                    even, odd = acc[2 * (g % 2)], acc[2 * (g % 2) + 1]
                    d, r, t = den[:, g % 2, :], rec[:, g % 2, :], tmp[:, g % 2, :]
                    dve.wait_ge(pv_done, 2 * KP * (g + 1))
                    nc.vector.tensor_copy(den[0:D1, g % 2, :], even[D1:P, :])
                    nc.vector.tensor_copy(den[D1:P, g % 2, :], odd[0:D1, :]).then_inc(den_ready, 1)
                    dve.wait_ge(den_rec, g + 1)
                    link(nc.vector.tensor_tensor(t, d, r, ALU.mult))
                    link(nc.vector.scalar_tensor_tensor(out=t, in0=t, scalar=-2.0, in1=r, op0=ALU.add, op1=ALU.mult))
                    nc.vector.scalar_tensor_tensor(out=m.outT[0:D1, g, :], in0=even[0:D1, :], scalar=-1.0,
                                                   in1=tmp[0:D1, g % 2, :], op0=ALU.mult, op1=ALU.mult)
                    nc.vector.scalar_tensor_tensor(out=m.outT[D1:P, g, :], in0=odd[D1:P, :], scalar=-1.0,
                                                   in1=tmp[D1:P, g % 2, :], op0=ALU.mult, op1=ALU.mult)\
                        .then_inc(acc_free, 1)


def attention_wide(nc, A, R):
    with ExitStack() as ctx:
        m = Resident()

        def sb(name, shape, dt=FP32):
            return ctx.enter_context(nc.sbuf_tensor(f"c_{name}", shape, dt))
        m.q, m.k = sb("q", [P, H1, S]), sb("k", [P, H1, CTX])
        m.scratch = sb("scratch", [P, H1 * (S + CTX) // 2])
        half_q = H1 * S // 2
        m.qb = m.scratch[0:D1, 0:half_q].bitcast(BF16).rearrange("p (h t) -> p h t", h=H1)
        m.kb = m.scratch[0:D1, half_q:].bitcast(BF16).rearrange("p (h t) -> p h t", h=H1)
        m.vaug = sb("vaug", [P, CT, H1, 2 * D1])
        m.outT = R.xn[:, :, :].rearrange("p (g a) e -> p g (a e)", g=G)
        w = [Pair(sb(n + "h", [P, KE, H1 * D1], FP32R), sb(n + "l", [P, KE, H1 * D1], FP32R)) for n in ("wq", "wk", "wv")]
        w_out, b_out = sb("wo", [P, G, E]), sb("bo", [1, E])
        flat = m.k[:, :, :].rearrange("p h t -> p (h t)")
        n_w = KE * H1 * D1
        w_full = [flat[:, i * n_w:(i + 1) * n_w].rearrange("p (k n) -> p k n", k=KE) for i in range(3)]
        loads = [(t[:, :, :], A[f"L1_xattn_{n}"].rearrange("(k p) n -> p k n", p=P))
                 for t, n in zip(w_full + [w_out], ("Wq", "Wk", "Wv", "Wo"))]
        loads.append((b_out[:, :], A["L1_xattn_bo"].rearrange("(a n) -> a n", a=1)))
        stage_norm(nc, R, "cn", loads, splits=[(f[:, :, :], p[:, :, :]) for f, p in zip(w_full, w)])
        for b in range(B):
            stage_project_wide(nc, R, m, b, *w)
            stage_max_wide(nc, R, m, b)
            stage_attend_wide(nc, R, m, b)
            stage_out(nc, R, "c", m.outT, w_out, b_out, b)


def route_top2(nc, R, s, m, gate_w, block):
    NE = 8
    logits = s.ps("logits", [P, NT, NE])
    e, top, we2 = s.sb("e", [P, NT, NE]), s.sb("top", [P, NT, NE]), s.sb("we2", [P, NT, NE])
    idx, idxf = s.sb("idx", [P, NT, NE], U32), s.sb("idxf", [P, NT, NE])
    col = s.sb("col", [P, NT, 1])
    io_i, io_f = s.sb("io_i", [P, NE], I32), s.sb("io_f", [P, NE])
    ready, shifted, exps, iota_done, step = (s.sem(n) for n in ("r_logits", "r_shifted", "r_exps", "r_iota", "r_step"))
    bc = lambda ap: ap.broadcast_to([P, NT, NE])

    @block.tensor
    def _(pe):
        for t in range(NT):
            for k in range(KE):
                last = matmul3(nc, logits[:, t, :], R.xnT[:, k, t * P:(t + 1) * P], gate_w[:, k, :],
                                        start=k == 0, stop=k == KE - 1)
        last.then_inc(ready, 1)

    @block.gpsimd
    def _(pool):
        nc.gpsimd.iota(io_i[:, :], pattern=[[1, NE]], base=0, channel_multiplier=0).then_inc(iota_done, 1)

    @block.scalar
    def _(act):
        act.wait_ge(shifted, 1)
        nc.scalar.activation(e[:, :, :], e[:, :, :], ACT.Exp).then_inc(exps, 1)

    @block.vector
    def _(dve):
        link = chain_of(dve, step)
        v = nc.vector
        dve.wait_ge(ready, 1)
        link(v.tensor_reduce(out=col[:, :, 0], in_=logits[:, :, :], op=ALU.max, axis=AX.X))
        v.tensor_tensor(e[:, :, :], logits[:, :, :], bc(col[:, :, :]), ALU.subtract).then_inc(shifted, 1)
        dve.wait_ge(exps, 1)
        link(v.tensor_reduce(out=col[:, :, 0], in_=e[:, :, :], op=ALU.add, axis=AX.X))
        link(v.reciprocal(col[:, :, :], col[:, :, :]))
        link(v.tensor_tensor(e[:, :, :], e[:, :, :], bc(col[:, :, :]), ALU.mult))
        for t in range(NT):
            last = v.max(top[:, t, :], e[:, t, :])
        link(last)
        for t in range(NT):
            last = v.max_index(idx[:, t, :], top[:, t, :], e[:, t, :])
        link(last)
        link(v.tensor_copy(idxf[:, :, :], idx[:, :, :]))
        link(v.tensor_tensor(col[:, :, :], top[:, :, 0:1], top[:, :, 1:2], ALU.add))
        link(v.tensor_scalar_add(col[:, :, :], col[:, :, :], 1e-20))
        link(v.reciprocal(col[:, :, :], col[:, :, :]))
        link(v.tensor_tensor(top[:, :, :], top[:, :, :], bc(col[:, :, :]), ALU.mult))
        dve.wait_ge(iota_done, 1)
        link(v.tensor_copy(io_f[:, :], io_i[:, :]))
        grid = io_f[:, :].unsqueeze(1).broadcast_to([P, NT, NE])
        link(v.tensor_tensor(m.we[:, :, :], grid, bc(idxf[:, :, 0:1]), ALU.is_equal))
        link(v.tensor_tensor(we2[:, :, :], grid, bc(idxf[:, :, 1:2]), ALU.is_equal))
        link(v.tensor_tensor(m.we[:, :, :], m.we[:, :, :], bc(top[:, :, 0:1]), ALU.mult))
        link(v.tensor_tensor(we2[:, :, :], we2[:, :, :], bc(top[:, :, 1:2]), ALU.mult))
        link(v.tensor_tensor(m.we[:, :, :], m.we[:, :, :], we2[:, :, :], ALU.add))


def route_hash(nc, R, s, m, block):
    NE = 8
    sm, r, a, c = (s.sb(n, [P, NT, 1]) for n in ("sm", "r", "a", "c"))
    hi, hj = s.sb("hi", [P, NT, 1], I32), s.sb("hj", [P, NT, 1], I32)
    io_i, io_f, we2 = s.sb("io_i", [P, NE], I32), s.sb("io_f", [P, NE]), s.sb("we2", [P, NT, NE])
    iota_done, step = s.sem("h_iota"), s.sem("h_step")
    b1_t, b1_ready, wt_mm, wt_done = (s.sem(n) for n in ("h_b1t", "h_b1", "h_wt_mm", "h_wt"))
    tp = s.ps("b1_tp")
    wps = s.ps("wt_ps", [NE, N])
    routed = s.sem("h_routed")

    @block.gpsimd
    def _(pool):
        nc.gpsimd.iota(io_i[:, :], pattern=[[1, NE]], base=0, channel_multiplier=0).then_inc(iota_done, 1)

    @block.tensor
    def _(pe):
        rows = m.b1_rows.shape[0]
        nc.tensor.transpose(tp[:, 0:rows], m.b1_rows[:, :], R.ident[0:rows, 0:rows]).then_inc(b1_t, 1)
        pe.wait_ge(routed, 1)
        for t in range(NT):
            last = nc.tensor.transpose(wps[:, t * P:(t + 1) * P], m.we[:, t, :], R.ident[:, :])
        last.then_inc(wt_mm, 1)

    @block.vector
    def _(dve):
        link = chain_of(dve, step)
        v = nc.vector
        dve.wait_ge(b1_t, 1)
        v.tensor_copy(m.b1[:, :], tp[:, 0:m.b1_rows.shape[0]]).then_inc(b1_ready, 1)
        link(v.tensor_tensor(sm[:, :, :], R.xn[:, :, 0:1], R.xn[:, :, 1:2], ALU.add))
        link(v.tensor_copy(hi[:, :, :], sm[:, :, :]))
        link(v.tensor_copy(r[:, :, :], hi[:, :, :]))
        link(v.tensor_tensor(a[:, :, :], r[:, :, :], sm[:, :, :], ALU.is_gt))
        link(v.tensor_scalar(c[:, :, :], sm[:, :, :], 0.0, None, ALU.is_gt))
        link(v.tensor_tensor(c[:, :, :], a[:, :, :], c[:, :, :], ALU.mult))
        link(v.tensor_tensor(a[:, :, :], r[:, :, :], sm[:, :, :], ALU.is_lt))
        link(v.tensor_tensor(r[:, :, :], r[:, :, :], c[:, :, :], ALU.subtract))
        link(v.tensor_scalar(c[:, :, :], sm[:, :, :], 0.0, None, ALU.is_lt))
        link(v.tensor_tensor(c[:, :, :], a[:, :, :], c[:, :, :], ALU.mult))
        link(v.tensor_tensor(r[:, :, :], r[:, :, :], c[:, :, :], ALU.add))
        dve.wait_ge(iota_done, 1)
        link(v.tensor_copy(io_f[:, :], io_i[:, :]))
        grid = io_f[:, :].unsqueeze(1).broadcast_to([P, NT, NE])
        bc = lambda ap: ap.broadcast_to([P, NT, NE])
        for i, out in enumerate((m.we, we2)):
            link(v.tensor_scalar_add(c[:, :, :], r[:, :, :], float(i)))
            link(v.tensor_copy(hi[:, :, :], c[:, :, :]))
            link(v.tensor_scalar(hj[:, :, :], hi[:, :, :], NE - 1, None, ALU.bitwise_and))
            link(v.tensor_copy(c[:, :, :], hj[:, :, :]))
            link(v.tensor_tensor(out[:, :, :], grid, bc(c[:, :, :]), ALU.is_equal))
        link(v.tensor_tensor(m.we[:, :, :], m.we[:, :, :], we2[:, :, :], ALU.add))
        v.tensor_scalar(m.we[:, :, :], m.we[:, :, :], 0.5, None, ALU.mult).then_inc(routed, 1)
        dve.wait_ge(wt_mm, 1)
        for i in range(2):
            v.tensor_copy(m.weT[:, i * 512:(i + 1) * 512], wps[:, i * 512:(i + 1) * 512]).then_inc(wt_done, 1)


def stage_experts(nc, R, m, tag, experts, hid, gated):
    HT = hid // P
    n_w = 3 if gated else 2
    slot_w = n_w * KE * hid
    CH = N // 512
    units = [(e, c) for e in range(len(experts)) for c in range(CH)]
    with stage(nc, tag) as s:
        wfull = s.sb("wfull", [P, slot_w])
        wslot = Pair(s.sb("wslot_h", [P, 2, slot_w], FP32R), s.sb("wslot_l", [P, 2, slot_w], FP32R))
        hT = Pair(s.sb("hT_h", [P, 2, HT, 512], FP32R), s.sb("hT_l", [P, 2, HT, 512], FP32R))
        act_t = s.sb("act_t", [P, 3, 512]) if gated else None
        hid_t = s.sb("hid_t", [P, 3, 512])
        up = [s.ps(f"up{i}") for i in range(3)]
        gate = [s.ps(f"gate{i}") for i in range(3)] if gated else None
        down = [s.ps(f"down{i}") for i in range(2)]
        w_in, w_high, w_low, hid_done, h_high = (s.sem(n) for n in ("w_in", "w_high", "w_low", "hid_done", "h_high"))
        first_ready, act_done, h_done, y_ready, y_added = (s.sem(n) for n in (
            "first_ready", "act_done", "h_done", "y_ready", "y_added"))

        def weights(e):
            w = wslot[:, e % 2, :]
            k = KE * hid
            ups = [w[:, i * k:(i + 1) * k].rearrange("p (k n) -> p k n", k=KE) for i in range(n_w - 1)]
            return (*ups, w[:, (n_w - 1) * k:n_w * k].rearrange("p (k n) -> p k n", k=HT))

        with nc.Block() as block:

            @block.sync
            def _(sp):
                for e, (*drams, _) in enumerate(experts):
                    if e >= 1:
                        sp.wait_ge(w_low, e)
                    at = 0
                    for src in drams:
                        n = src.shape[0] * src.shape[1] // P
                        sp.dma_start(wfull[:, at:at + n].rearrange("p (k n) -> p k n", n=src.shape[1]),
                                     src.rearrange("(k p) n -> p k n", p=P)).then_inc(w_in, 16)
                        at += n

            @block.tensor
            def _(pe):
                def first(n):
                    e, c = units[n]
                    w = weights(e)
                    if c == 0:
                        pe.wait_ge(w_low, e + 1)
                    for i in range(HT):
                        u = n * HT + i
                        if u >= 3:
                            pe.wait_ge(hid_done, u - 2)
                        for out, wi in zip((gate, up) if gated else (up,), w):
                            for k in range(KE):
                                last = matmul3(nc, out[u % 3][:, :], wi[:, k, i * P:(i + 1) * P],
                                                        R.xnT[:, k, c * 512:(c + 1) * 512],
                                                        start=k == 0, stop=k == KE - 1)
                        last.then_inc(first_ready, 1)

                def second(n):
                    e, c = units[n]
                    wd = weights(e)[-1]
                    pe.wait_ge(h_done, (n + 1) * HT)
                    for t in range(4):
                        u = 4 * n + t
                        if u >= 2:
                            pe.wait_ge(y_added, u - 1)
                        for k in range(HT):
                            last = matmul3(nc, down[u % 2][:, 0:E], hT[:, n % 2, k, t * P:(t + 1) * P],
                                                    wd[:, k, :], start=k == 0, stop=k == HT - 1)
                        last.then_inc(y_ready, 1)
                for n in range(len(units) + 1):
                    if n < len(units):
                        first(n)
                    if n >= 1:
                        second(n - 1)
                if not gated:
                    for t in range(NT):
                        u = 4 * len(units) + t
                        pe.wait_ge(y_added, u - 1)
                        nc.tensor.matmul(down[u % 2][:, 0:E], m.weT[:, t * P:(t + 1) * P], m.b2[:, :],
                                         start=True, stop=True).then_inc(y_ready, 1)

            @block.scalar
            def _(act):
                if not gated:
                    nc.scalar.preload_act_table_set(TABLE_SET)

                def split_weights(e):
                    act.wait_ge(w_in, 16 * n_w * (e + 1))
                    if e >= 2:
                        act.wait_ge(y_ready, 4 * CH * (e - 1))
                    nc.scalar.activation(wslot.hi[:, e % 2, :], wfull[:, :], ACT.Copy).then_inc(w_high, 1)

                def high_part(u):
                    act.wait_ge(hid_done, u + 1)
                    n, i = u // HT, u % HT
                    if n >= 2:
                        act.wait_ge(y_ready, 4 * (n - 1))
                    nc.scalar.activation(hT.hi[:, n % 2, i, :], hid_t[:, u % 3, :], ACT.Copy).then_inc(h_high, 1)
                split_weights(0)
                for n, (e, c) in enumerate(units):
                    for i in range(HT):
                        u = n * HT + i
                        act.wait_ge(first_ready, u + 1)
                        if gated:
                            if u >= 3:
                                act.wait_ge(hid_done, u - 2)
                            nc.scalar.activation(act_t[:, u % 3, :], gate[u % 3][:, :], ACT.Silu).then_inc(act_done, 1)
                        else:
                            if u >= 3:
                                act.wait_ge(h_done, u - 2)
                            nc.scalar.activation(hid_t[:, u % 3, :], up[u % 3][:, :], ACT.Relu,
                                                 bias=m.b1[:, e * HT + i:e * HT + i + 1]).then_inc(hid_done, 1)
                        if u >= 1:
                            high_part(u - 1)
                        if c == CH - 1 and i == 0 and e + 1 < len(experts):
                            split_weights(e + 1)
                high_part(len(units) * HT - 1)

            @block.vector
            def _(dve):
                def low_weights(e):
                    dve.wait_ge(w_high, e + 1)
                    nc.vector.tensor_tensor(wslot.lo[:, e % 2, :], wfull[:, :], wslot.hi[:, e % 2, :].bitcast(FP32),
                                            ALU.subtract).then_inc(w_low, 1)

                def low_part(u):
                    n, i = u // HT, u % HT
                    dve.wait_ge(h_high, u + 1)
                    nc.vector.tensor_tensor(hT.lo[:, n % 2, i, :], hid_t[:, u % 3, :],
                                            hT.hi[:, n % 2, i, :].bitcast(FP32), ALU.subtract).then_inc(h_done, 1)

                def residual(n):
                    e, c = units[n]
                    column = experts[e][-1]
                    for t in range(4):
                        x = R.x[:, 4 * c + t, :]
                        u = 4 * n + t
                        dve.wait_ge(y_ready, u + 1)
                        if column is None:
                            nc.vector.tensor_tensor(x, down[u % 2][:, 0:E], x, ALU.add).then_inc(y_added, 1)
                        else:
                            nc.vector.scalar_tensor_tensor(out=x, in0=down[u % 2][:, 0:E],
                                                           scalar=m.we[:, 4 * c + t, column:column + 1], in1=x,
                                                           op0=ALU.mult, op1=ALU.add).then_inc(y_added, 1)
                low_weights(0)
                for n in range(len(units) + 1):
                    if n < len(units):
                        for i in range(HT):
                            u = n * HT + i
                            if gated:
                                dve.wait_ge(act_done, u + 1)
                                if u >= 3:
                                    dve.wait_ge(h_done, u - 2)
                                nc.vector.tensor_tensor(hid_t[:, u % 3, :], act_t[:, u % 3, :], up[u % 3][:, :], ALU.mult)\
                                    .then_inc(hid_done, 1)
                            if u >= 1:
                                low_part(u - 1)
                            e, c = units[n]
                            if c == CH - 1 and i == 1 and e + 1 < len(experts):
                                low_weights(e + 1)
                            if i == HT // 2 and n >= 1:
                                residual(n - 1)
                    else:
                        low_part(n * HT - 1)
                        residual(n - 1)
                if not gated:
                    for t in range(NT):
                        u = 4 * len(units) + t
                        dve.wait_ge(y_ready, u + 1)
                        dve.wait_ge(y_added, u)
                        nc.vector.tensor_tensor(R.x[:, t, :], down[u % 2][:, 0:E], R.x[:, t, :], ALU.add).then_inc(y_added, 1)


def experts_top2(nc, A, R):
    with ExitStack() as ctx:
        m = Resident()
        m.we = ctx.enter_context(nc.sbuf_tensor("f_we", [P, NT, 8], FP32))
        full = ctx.enter_context(nc.sbuf_tensor("f_gate_w", [P, KE, 8], FP32))
        gate_w = Pair(*(ctx.enter_context(nc.sbuf_tensor(f"f_gate_{n}", [P, KE, 8], FP32R)) for n in "hl"))
        stage_norm(nc, R, "fn", [(full[:, :, :], A["L0_ffn_gate_w"].rearrange("(k p) n -> p k n", p=P))],
                   splits=[(full[:, :, :], gate_w[:, :, :])])
        with stage(nc, "fr") as s:
            with nc.Block() as block:
                route_top2(nc, R, s, m, gate_w, block)
        experts = [(A["L0_ffn_ws_gate"], A["L0_ffn_ws_up"], A["L0_ffn_ws_down"], None)]
        experts += [(A["L0_ffn_w_gate"][e], A["L0_ffn_w_up"][e], A["L0_ffn_w_down"][e], e) for e in range(8)]
        stage_experts(nc, R, m, "fe", experts, 512, True)


def experts_hash(nc, A, R):
    with ExitStack() as ctx:
        m = Resident()

        def sb(name, shape):
            return ctx.enter_context(nc.sbuf_tensor(f"g_{name}", shape, FP32))
        n_e, hid = A["L1_ffn_b1"].shape
        m.we, m.weT = sb("we", [P, NT, 8]), sb("weT", [8, N])
        m.b1_rows, m.b1, m.b2 = sb("b1_rows", [n_e * hid // P, P]), sb("b1", [P, n_e * hid // P]), sb("b2", [n_e, E])
        stage_norm(nc, R, "gn", [(m.b1_rows[:, :], A["L1_ffn_b1"].rearrange("e (m p) -> (e m) p", p=P)),
                                 (m.b2[:, :], A["L1_ffn_b2"])])
        with stage(nc, "gr") as s:
            with nc.Block() as block:
                route_hash(nc, R, s, m, block)
        stage_experts(nc, R, m, "ge", [(A["L1_ffn_W1"][e], A["L1_ffn_W2"][e], e) for e in range(n_e)], hid, False)


class Resident:
    pass


def build(nc, A, out, upto=None):
    with ExitStack() as ctx:
        def sb(name, shape, dt=FP32):
            return ctx.enter_context(nc.sbuf_tensor(name, shape, dt))
        R = Resident()
        R.x = sb("x", [P, NT, E])
        R.xn = sb("xn", [P, NT, E])
        R.xnT = Pair(sb("xnT_h", [P, KE, N], FP32R), sb("xnT_l", [P, KE, N], FP32R))
        R.ident = sb("ident", [P, P])
        R.ident_b = sb("ident_b", [P, P], BF16)
        R.window = sb("window", [P, 2, 2 * P], BF16)
        R.ones_row = sb("ones_row", [1, P])
        R.yat_one = sb("yat_one", [P, 1])
        R.rope = sb("rope_t", [P, 2, ST, D])
        stored = ctx.enter_context(nc.semaphore("out_stored"))
        a = lambda p, names: [A[f"{p}_{n}"] for n in names]
        wqkv = A["L1_attn_Wqkv"]
        parts = [
            lambda: attention16(nc, A, R, "ya", "yat", *a("L0_attn", ("Wq", "Wk", "Wv", "Wo", "bq", "bk", "bv", "bo"))),
            lambda: attention16(nc, A, R, "xa", "cross",
                                *a("L0_xattn", ("Wq", "Wk", "Wv", "Wo", "bq", "bk", "bv", "bo"))),
            lambda: experts_top2(nc, A, R),
            lambda: attention16(nc, A, R, "wa", "rope", *(wqkv[:, i * E:(i + 1) * E] for i in range(3)),
                                A["L1_attn_Wout"]),
            lambda: attention_wide(nc, A, R),
        ]
        with ExitStack() as ctx_tiles:
            R.ctxT = Pair(*(ctx_tiles.enter_context(nc.sbuf_tensor(f"ctxT_{n}", [P, KE, B * CTX], FP32R)) for n in "hl"))
            stage_setup(nc, A, R)
            for i, part in enumerate(parts):
                if upto is None or i in upto:
                    part()
        if upto is None or len(parts) in upto:
            experts_hash(nc, A, R)
        with stage(nc, "store") as s:
            with nc.Block() as block:
                @block.sync
                def _(sp):
                    sp.dma_start(out.rearrange("b (t p) e -> p (b t) e", p=P), R.x[:, :, :]).then_inc(stored, 16)
                    sp.wait_ge(stored, 16)


_INS = ["x", "ctx_1024", "L0_attn_Wq", "L0_attn_bq", "L0_attn_Wk", "L0_attn_bk", "L0_attn_Wv", "L0_attn_bv",
        "L0_attn_Wo", "L0_attn_bo", "L0_xattn_Wq", "L0_xattn_bq", "L0_xattn_Wk", "L0_xattn_bk", "L0_xattn_Wv",
        "L0_xattn_bv", "L0_xattn_Wo", "L0_xattn_bo", "L0_ffn_gate_w", "L0_ffn_w_gate", "L0_ffn_w_up",
        "L0_ffn_w_down", "L0_ffn_ws_gate", "L0_ffn_ws_up", "L0_ffn_ws_down", "L1_attn_Wqkv", "L1_attn_Wout",
        "L1_xattn_Wq", "L1_xattn_Wk", "L1_xattn_Wv", "L1_xattn_Wo", "L1_xattn_bo", "L1_ffn_W1", "L1_ffn_b1",
        "L1_ffn_W2", "L1_ffn_b2", "rope"]


def shape_constants():
    half = D // 2
    theta = (1.0 / np.float32(10000.0) ** (np.arange(half, dtype=np.float32) / np.float32(half))).astype(np.float32)
    freqs = np.arange(S, dtype=np.float32)[:, None] * theta[None, :]
    cos, sin = np.cos(freqs), np.sin(freqs)
    return {"rope": np.stack([np.concatenate([cos, cos], 1), np.concatenate([-sin, sin], 1)]).astype(np.float32)}


def kernel(**inputs):
    import concourse.bacc as bacc
    from concourse.bass_utils import run_bass_kernel_spmd

    nc = bacc.Bacc("TRN2", target_bir_lowering=False, num_devices=1)
    arrays, patterns = {}, {}
    for name, value in {**inputs, **shape_constants()}.items():
        value = np.ascontiguousarray(value)
        arrays[f"in_{name}"] = value
        patterns[name] = nc.dram_tensor(f"in_{name}", value.shape, mybir.dt.from_np(value.dtype), kind="ExternalInput").ap()
    out = nc.dram_tensor("out", (B, S, E), FP32, kind="ExternalOutput").ap()
    build(nc, patterns, out)
    return run_bass_kernel_spmd(nc, [arrays], core_ids=[0]).results[0]["out"]
```

```python
import numpy as np
from contextlib import ExitStack, contextmanager

import concourse.bass as bass
from concourse import mybir

FP32 = mybir.dt.float32
BF16 = mybir.dt.bfloat16
FP32R = mybir.dt.float32r
I32 = mybir.dt.int32
U32 = mybir.dt.uint32
ALU = mybir.AluOpType
ACT = mybir.ActivationFunctionType
AX = mybir.AxisListType

P = 128
B, S, E = 2, 512, 256
CTX = 1024
N = B * S
NT = N // P
ST = S // P
CT = CTX // P
KE = E // P
H, D = 16, 16
G = H // 4
VW = 32
PARTS = 3
Q_ROWS = (0, 0, 0, 1, 1, 2)
K_ROWS = (0, 1, 2, 0, 1, 0)
ROWS = D * len(Q_ROWS)
MAX_ROWS = 2
H1, D1 = 8, 64
LN_EPS = 1e-5
YAT_EPS = 0.1
NEG = -1e30
TABLE_SET = "natural_log_exp_and_others"


class Scope:

    def __init__(self, nc, ctx, tag):
        self.nc, self.ctx, self.tag, self.sems = nc, ctx, tag, []

    def sb(self, name, shape, dt=FP32):
        return self.ctx.enter_context(self.nc.sbuf_tensor(f"{self.tag}_{name}", shape, dt))

    def ps(self, name, shape=(P, 512), dt=FP32):
        return self.ctx.enter_context(self.nc.psum_tensor(f"{self.tag}_{name}", list(shape), dt))

    def sem(self, name):
        s = self.ctx.enter_context(self.nc.semaphore(f"{self.tag}_{name}"))
        self.sems.append(s)
        return s


@contextmanager
def stage(nc, tag):
    with ExitStack() as ctx:
        s = Scope(nc, ctx, tag)
        yield s
        for sem in s.sems:
            nc.gpsimd.sem_clear(sem)
        nc.all_engine_barrier()


class Pair:

    def __init__(self, hi, lo):
        self.hi, self.lo = hi, lo

    def __getitem__(self, key):
        return Pair(self.hi[key], self.lo[key])

    def rearrange(self, *a, **k):
        return Pair(self.hi.rearrange(*a, **k), self.lo.rearrange(*a, **k))


def matmul3(nc, out, a, b, start, stop):
    nc.tensor.matmul(out, a.hi, b.hi, start=start, stop=False)
    nc.tensor.matmul(out, a.hi, b.lo, start=False, stop=False)
    return nc.tensor.matmul(out, a.lo, b.hi, start=False, stop=stop)


def chain_of(engine, sem):
    n = [0]

    def link(ins):
        n[0] += 1
        ins.then_inc(sem, 1)
        engine.wait_ge(sem, n[0])
    return link


def stage_setup(nc, A, R):
    with stage(nc, "setup") as s:
        ctx_tok = s.sb("ctx_tok", [P, B * CT, E])
        tp = [s.ps(f"tp{i}") for i in range(4)]
        x_in, ctx_in, w_in = s.sem("x_in"), [s.sem(f"ctx_in{b}") for b in range(B)], s.sem("w_in")
        ident_step, ident_ready = s.sem("ident_step"), s.sem("ident_ready")
        transposed, evacuated = s.sem("transposed"), s.sem("evacuated")
        made, high_done = s.sem("made"), s.sem("high_done")
        with nc.Block() as block:

            @block.sync
            def _(sp):
                sp.dma_start(R.x[:, :, :], A["x"].rearrange("b (t p) e -> p (b t) e", p=P)).then_inc(x_in, 16)
                for b in range(B):
                    sp.dma_start(ctx_tok[:, b * CT:(b + 1) * CT, :],
                                 A["ctx_1024"][b].rearrange("(t p) e -> p t e", p=P)).then_inc(ctx_in[b], 16)

                sp.dma_start(R.rope[:, :, :, :], A["rope"].rearrange("c (t p) d -> p c t d", p=P)).then_inc(w_in, 16)
                sp.wait_ge(w_in, 16)
                sp.wait_ge(x_in, 16)

            @block.gpsimd
            def _(pool):
                nc.gpsimd.memset(R.ident[:, :], 0.0).then_inc(ident_step, 1)
                nc.gpsimd.memset(R.ones_row[:, :], 1.0).then_inc(made, 1)
                nc.gpsimd.memset(R.yat_one[:, :], 1.0 + YAT_EPS).then_inc(made, 1)
                nc.gpsimd.memset(R.window[:, :, :], 0.0).then_inc(ident_step, 1)
                pool.wait_ge(ident_step, 1)
                nc.gpsimd.affine_select(out=R.ident[:, :], in_=R.ident[:, :], compare_op=ALU.not_equal, fill=1.0,
                                        base=0, pattern=[[-1, P]], channel_multiplier=1).then_inc(ident_ready, 1)
                pool.wait_ge(ident_step, 2)
                nc.gpsimd.affine_select(out=R.window[:, 0, 0:P], in_=R.window[:, 0, 0:P], compare_op=ALU.is_ge,
                                        fill=NEG, base=0, pattern=[[1, P]], channel_multiplier=-1).then_inc(made, 1)
                nc.gpsimd.affine_select(out=R.window[:, 0, P:2 * P], in_=R.window[:, 0, P:2 * P],
                                        compare_op=ALU.is_gt, fill=NEG, base=0, pattern=[[-1, P]],
                                        channel_multiplier=1).then_inc(made, 1)
                nc.gpsimd.affine_select(out=R.window[:, 1, 0:P], in_=R.window[:, 1, 0:P], compare_op=ALU.is_gt,
                                        fill=NEG, base=0, pattern=[[1, P]], channel_multiplier=-1).then_inc(made, 1)
                nc.gpsimd.affine_select(out=R.window[:, 1, P:2 * P], in_=R.window[:, 1, P:2 * P],
                                        compare_op=ALU.is_ge, fill=NEG, base=0, pattern=[[-1, P]],
                                        channel_multiplier=1).then_inc(made, 1)
                pool.wait_ge(ident_ready, 1)
                nc.gpsimd.tensor_copy(R.ident_b[:, :], R.ident[:, :]).then_inc(made, 1)

            banks = [(b, k, q) for b in range(B) for q in range(CT // 4) for k in range(KE)]

            @block.tensor
            def _(pe):
                pe.wait_ge(ident_ready, 1)
                for n, (b, k, q) in enumerate(banks):
                    pe.wait_ge(ctx_in[b], 16)
                    if n >= 4:
                        pe.wait_ge(evacuated, n - 3)
                    for i in range(4):
                        last = nc.tensor.transpose(tp[n % 4][:, i * P:(i + 1) * P],
                                                   ctx_tok[:, b * CT + 4 * q + i, k * P:(k + 1) * P], R.ident[:, :])
                    last.then_inc(transposed, 1)

            @block.vector
            def _(dve):
                for n, (b, k, q) in enumerate(banks):
                    dve.wait_ge(high_done, n + 1)
                    part = R.ctxT[:, k, b * CTX + q * 512:b * CTX + (q + 1) * 512]
                    nc.vector.tensor_tensor(part.lo, tp[n % 4][:, :], part.hi.bitcast(FP32), ALU.subtract)\
                        .then_inc(evacuated, 1)

            @block.scalar
            def _(act):
                nc.scalar.preload_act_table_set(TABLE_SET)
                for n, (b, k, q) in enumerate(banks):
                    act.wait_ge(transposed, n + 1)
                    nc.scalar.activation(R.ctxT[:, k, b * CTX + q * 512:b * CTX + (q + 1) * 512].hi,
                                         tp[n % 4][:, :], ACT.Copy).then_inc(high_done, 1)


def stage_norm(nc, R, tag, loads=(), padded=None, splits=()):
    with stage(nc, tag) as s:
        stats = s.sb("stats", [P, NT, 6])
        mv = s.sb("mv", [P, NT, 2])
        ve, lnv, r, a, nb = (s.sb(n, [P, NT]) for n in ("ve", "lnv", "r", "a", "nb"))
        tp = [s.ps(f"tp{i}") for i in range(4)]
        step, var_ready, rs_step, rs_ready = s.sem("step"), s.sem("var"), s.sem("rs_step"), s.sem("rs")
        normed, transposed, high_done, evac = s.sem("normed"), s.sem("transposed"), s.sem("high_done"), s.sem("evac")
        w_high, w_low = s.sem("w_high"), s.sem("w_low")
        weights_in, zeroed = s.sem("weights_in"), s.sem("zeroed")
        banks = [(k, q) for q in range(NT // 4) for k in range(KE)]
        with nc.Block() as block:

            @block.gpsimd
            def _(pool):
                if padded is not None:
                    nc.gpsimd.memset(padded[:, :, :], 0.0).then_inc(zeroed, 1)

            @block.sync
            def _(sp):
                if padded is not None:
                    sp.wait_ge(zeroed, 1)
                for dst, src in loads:
                    sp.dma_start(dst, src, allow_slow_non_contiguous=True).then_inc(weights_in, 16)
                if loads:
                    sp.wait_ge(weights_in, 16 * len(loads))

            @block.vector
            def _(dve):
                link = chain_of(dve, step)
                for t in range(NT):
                    ins = nc.vector.bn_stats(stats[:, t, :], R.x[:, t, :])
                link(ins)
                for t in range(NT):
                    ins = nc.vector.bn_aggr(mv[:, t, :], stats[:, t, :])
                link(ins)
                nc.vector.tensor_scalar_add(ve[:, :], mv[:, :, 1], LN_EPS).then_inc(var_ready, 1)
                dve.wait_ge(rs_ready, 1)
                dve.wait_ge(var_ready, 1)
                link(nc.vector.tensor_tensor(a[:, :], r[:, :], r[:, :], ALU.mult))
                link(nc.vector.tensor_tensor(a[:, :], a[:, :], ve[:, :], ALU.mult))
                link(nc.vector.tensor_scalar(a[:, :], a[:, :], -0.5, 1.5, ALU.mult, ALU.add))
                link(nc.vector.tensor_tensor(r[:, :], r[:, :], a[:, :], ALU.mult))
                link(nc.vector.scalar_tensor_tensor(out=nb[:, :], in0=mv[:, :, 0], scalar=-1.0, in1=r[:, :],
                                                    op0=ALU.mult, op1=ALU.mult))
                for t in range(NT):
                    nc.vector.tensor_scalar(R.xn[:, t, :], R.x[:, t, :], r[:, t:t + 1], nb[:, t:t + 1],
                                            ALU.mult, ALU.add).then_inc(normed, 1)
                for n, (k, q) in enumerate(banks):
                    dve.wait_ge(high_done, n + 1)
                    part = R.xnT[:, k, q * 512:(q + 1) * 512]
                    nc.vector.tensor_tensor(part.lo, tp[n][:, :], part.hi.bitcast(FP32), ALU.subtract).then_inc(evac, 1)
                for i, (full, part) in enumerate(splits):
                    dve.wait_ge(w_high, i + 1)
                    nc.vector.tensor_tensor(part.lo, full, part.hi.bitcast(FP32), ALU.subtract).then_inc(w_low, 1)

            @block.scalar
            def _(act):
                nc.scalar.preload_act_table_set(TABLE_SET)
                act.wait_ge(var_ready, 1)
                nc.scalar.activation(lnv[:, :], ve[:, :], ACT.Ln).then_inc(rs_step, 1)
                act.wait_ge(rs_step, 1)
                nc.scalar.activation(r[:, :], lnv[:, :], ACT.Exp, scale=-0.5).then_inc(rs_ready, 1)
                for n, (k, q) in enumerate(banks):
                    act.wait_ge(transposed, n + 1)
                    nc.scalar.activation(R.xnT[:, k, q * 512:(q + 1) * 512].hi, tp[n][:, :], ACT.Copy)\
                        .then_inc(high_done, 1)
                if splits:
                    act.wait_ge(weights_in, 16 * len(loads))
                for full, part in splits:
                    nc.scalar.activation(part.hi, full, ACT.Copy).then_inc(w_high, 1)

            @block.tensor
            def _(pe):
                for n, (k, q) in enumerate(banks):
                    for i in range(4):
                        pe.wait_ge(normed, 4 * q + i + 1)
                        last = nc.tensor.transpose(tp[n][:, i * P:(i + 1) * P],
                                                   R.xn[:, 4 * q + i, k * P:(k + 1) * P], R.ident[:, :])
                    last.then_inc(transposed, 1)


def stage_project(nc, R, tag, m, kind, wq, wk, wv, bq=None, bk=None, bv=None):
    cross = kind == "cross"
    src, kt_n = (R.ctxT, CT) if cross else (R.xnT, ST)
    keys = kt_n * P
    chunks = [(b, w, k, c) for b in range(B) for w, n in (("q", 1), ("k", keys // 512))
              for c in range(n) for k in range(KE)]
    n_tok = 0 if cross else 2 * NT
    n_v = B * kt_n // 2
    with stage(nc, f"{tag}p") as s:
        qc = s.sb("qc", [P, PARTS, B, KE, S], BF16)
        kc = s.sb("kc", [P, PARTS, B, KE, keys], BF16)
        rest = s.sb("rest", [P, 2, 512])
        feat = [s.ps(f"feat{i}") for i in range(4)]
        vps = [s.ps(f"v{i}") for i in range(2)]
        tok = [s.ps(f"tok{i}") for i in range(2)]
        if n_tok:
            qk = s.sb("qk", [P, n_tok, E])
            aux = s.sb("aux", [P, 4, E])
            ss, lns = s.sb("ss", [P, n_tok, H]), s.sb("lns", [P, n_tok, H])
        tok_mm, tok_evac, tok_ready = s.sem("tok_mm"), s.sem("tok_evac"), s.sem("tok_ready")
        aux_used, ss_ready, norm_step, norm_ready = (s.sem(n) for n in ("aux_used", "ss_ready", "norm_step", "norm_ready"))
        v_mm, v_evac = s.sem("v_mm"), s.sem("v_evac")
        feat_ready, high_ready, rest_ready, rest_used = (s.sem(n) for n in ("feat", "high", "rest", "rest_used"))
        dve_step, middle_ready, stored, ones, reduced = (s.sem(n) for n in (
            "dve_step", "middle_ready", "stored", "ones", "reduced"))

        def part_of(chunk, part):
            b, which, k, c = chunk
            return qc[:, part, b, k, :] if which == "q" else kc[:, part, b, k, c * 512:(c + 1) * 512]

        with nc.Block() as block:

            @block.tensor
            def _(pe):
                for n in range(n_tok):
                    t, w = n // 2, (wq, wk)[n % 2]
                    if n >= 2:
                        pe.wait_ge(tok_evac, n - 1)
                    for k in range(KE):
                        last = matmul3(nc, tok[n % 2][:, 0:E], R.xnT[:, k, t * P:(t + 1) * P], w[:, k, :],
                                       start=k == 0, stop=k == KE - 1)
                    last.then_inc(tok_mm, 1)

                def value(n):
                    if n >= 2:
                        pe.wait_ge(v_evac, n - 1)
                    for i in range(2):
                        at = (2 * n + i) * P
                        for k in range(KE):
                            last = matmul3(nc, vps[n % 2][:, i * E:(i + 1) * E], src[:, k, at:at + P], wv[:, k, :],
                                           start=k == 0, stop=k == KE - 1)
                    last.then_inc(v_mm, 1)
                if not cross:
                    for n in range(n_v):
                        value(n)
                for n, (b, which, mt, c) in enumerate(chunks):
                    if n >= 4:
                        pe.wait_ge(rest_ready, n - 3)
                    if cross:
                        w, x, at = (wq, R.xnT, b * S) if which == "q" else (wk, src, b * CTX + c * 512)
                        for k in range(KE):
                            last = matmul3(nc, feat[n % 4][:, :], w[:, k, mt * P:(mt + 1) * P], x[:, k, at:at + 512],
                                           start=k == 0, stop=k == KE - 1)
                    else:
                        pe.wait_ge(tok_ready, 2 * ST * (b + 1))
                        for t in range(ST):
                            last = nc.tensor.transpose(feat[n % 4][:, t * P:(t + 1) * P],
                                                       qk[:, 2 * (b * ST + t) + (which == "k"), mt * P:(mt + 1) * P],
                                                       R.ident[:, :])
                    last.then_inc(feat_ready, 1)
                if cross:
                    for n in range(n_v):
                        value(n)

            @block.scalar
            def _(act):
                nc.scalar.preload_act_table_set(TABLE_SET)
                if kind == "yat":
                    act.wait_ge(ss_ready, 1)
                    nc.scalar.activation(lns[:, :, :], ss[:, :, :], ACT.Ln).then_inc(norm_step, 1)
                    act.wait_ge(norm_step, 1)
                    nc.scalar.activation(lns[:, :, :], lns[:, :, :], ACT.Exp, scale=0.5).then_inc(norm_ready, 1)
                for n, chunk in enumerate(chunks):
                    bias = {"q": bq, "k": bk}[chunk[1]] if cross else None
                    act.wait_ge(feat_ready, n + 1)
                    if bias is None:
                        nc.scalar.activation(part_of(chunk, 0), feat[n % 4][:, :], ACT.Copy).then_inc(high_ready, 1)
                    else:
                        nc.scalar.activation(part_of(chunk, 0), feat[n % 4][:, :], ACT.Identity,
                                             bias=bias[:, chunk[2]:chunk[2] + 1]).then_inc(high_ready, 1)

            @block.vector
            def _(dve):
                link = chain_of(dve, dve_step)
                heads = lambda ap: ap.rearrange("p (h d) -> p h d", d=D)

                def value(n):
                    dve.wait_ge(v_mm, n + 1)
                    out = m.vaug[:, 2 * n:2 * n + 2, :, 0:D]
                    ps = vps[n % 2][:, :].rearrange("p (i h d) -> p i h d", i=2, d=D)
                    for i in range(2):
                        if bv is not None:
                            ins = nc.vector.tensor_tensor(out[:, i], ps[:, i], heads(bv[:, :]), ALU.add)
                        else:
                            ins = nc.vector.tensor_copy(out[:, i], ps[:, i])
                    ins.then_inc(v_evac, 1)
                if kind == "yat":
                    for n in range(n_tok + 2):
                        if n < n_tok:
                            dve.wait_ge(tok_mm, n + 1)
                            nc.vector.tensor_tensor(qk[:, n, :], tok[n % 2][:, 0:E], (bq, bk)[n % 2][:, :], ALU.add)\
                                .then_inc(tok_evac, 1)
                        if n >= 2:
                            dve.wait_ge(aux_used, n - 1)
                            nc.vector.tensor_reduce(out=ss[:, n - 2, :], in_=heads(aux[:, (n - 2) % 4, :]),
                                                    op=ALU.add, axis=AX.X).then_inc(reduced, 1)
                    dve.wait_ge(reduced, n_tok)
                    nc.vector.tensor_scalar_max(ss[:, :, :], ss[:, :, :], 1e-19).then_inc(ss_ready, 1)
                    for n in range(n_v):
                        value(n)
                    dve.wait_ge(norm_ready, 1)
                    link(nc.vector.tensor_scalar_add(lns[:, :, :], lns[:, :, :], 1e-8))
                    link(nc.vector.reciprocal(lns[:, :, :], lns[:, :, :]))
                    for n in range(n_tok):
                        nc.vector.tensor_tensor(heads(qk[:, n, :]), heads(qk[:, n, :]),
                                                lns[:, n, :].unsqueeze(2).broadcast_to([P, H, D]), ALU.mult)\
                            .then_inc(tok_ready, 1)
                if kind == "rope":
                    half = D // 2
                    for n in range(n_tok):
                        dve.wait_ge(tok_mm, n + 1)
                        if n >= 4:
                            dve.wait_ge(tok_ready, n - 3)
                        ps, a, r = heads(tok[n % 2][:, 0:E]), heads(qk[:, n, :]), heads(aux[:, n % 4, :])
                        t = n // 2 % ST
                        table = lambda c, lo, hi: R.rope[:, c, t, lo:hi].unsqueeze(1).broadcast_to([P, H, hi - lo])
                        nc.vector.tensor_tensor(a, ps, table(0, 0, D), ALU.mult)
                        nc.vector.tensor_tensor(r[:, :, 0:half], ps[:, :, half:D], table(1, 0, half), ALU.mult)
                        nc.vector.tensor_tensor(r[:, :, half:D], ps[:, :, 0:half], table(1, half, D), ALU.mult)\
                            .then_inc(tok_evac, 1)
                    for n in range(n_v):
                        value(n)
                for n, chunk in enumerate(chunks):
                    bias = {"q": bq, "k": bk}[chunk[1]] if cross else None
                    dve.wait_ge(high_ready, n + 1)
                    if n >= 2:
                        dve.wait_ge(rest_used, n - 1)
                    nc.vector.scalar_tensor_tensor(
                        out=rest[:, n % 2, :], in0=feat[n % 4][:, :],
                        scalar=0.0 if bias is None else bias[:, chunk[2]:chunk[2] + 1],
                        in1=part_of(chunk, 0), op0=ALU.add, op1=ALU.subtract).then_inc(rest_ready, 1)
                    dve.wait_ge(rest_ready, n + 1)
                    nc.vector.tensor_copy(part_of(chunk, 1), rest[:, n % 2, :]).then_inc(middle_ready, 1)
                if cross:
                    for n in range(n_v):
                        value(n)

            @block.gpsimd
            def _(pool):
                for n in range(n_tok):
                    pool.wait_ge(tok_evac, n + 1)
                    if kind == "yat":
                        if n >= 4:
                            pool.wait_ge(reduced, n - 3)
                        nc.gpsimd.tensor_tensor(aux[:, n % 4, :], qk[:, n, :], qk[:, n, :], ALU.mult).then_inc(aux_used, 1)
                    else:
                        nc.gpsimd.tensor_tensor(qk[:, n, :], qk[:, n, :], aux[:, n % 4, :], ALU.add).then_inc(tok_ready, 1)
                for n, chunk in enumerate(chunks):
                    pool.wait_ge(middle_ready, n + 1)
                    nc.gpsimd.tensor_tensor(part_of(chunk, 2), rest[:, n % 2, :], part_of(chunk, 1), ALU.subtract)\
                        .then_inc(rest_used, 1)

            @block.sync
            def _(sp):
                done = n_dma = 0
                for b in range(B):
                    for comp, scratch, n in ((qc, m.q_dram[b], KE), (kc, m.k_dram[b], KE * keys // 512)):
                        done += n
                        sp.wait_ge(rest_used, done)
                        for part in range(PARTS):
                            sp.dma_start(scratch[part].rearrange("(k p) t -> p k t", p=P), comp[:, part, b, :, :])\
                                .then_inc(stored, 16)
                            n_dma += 1
                sp.wait_ge(stored, 16 * n_dma)


def stage_attend(nc, R, tag, m, kind):
    yat, window = kind == "yat", kind == "rope"
    kt_n = CT if kind == "cross" else ST
    keys = kt_n * P
    GR = B * G
    QPG = 1 if window else kt_n // 2
    UPG = 4 * QPG
    units = GR * UPG
    cols = 7 * P if window else 1024
    rows = ROWS if yat else ROWS + MAX_ROWS
    PR = 8
    NS, NA = (3, 2) if yat else (2, 1)
    AHEAD = 2 if window else 1
    MU = 8 if window else 32
    LAG = 6 if yat else 4
    base = [2 * P * t for t in range(ST)]
    width = [2 * P] * (ST - 1) + [P]
    loads_per_group = len(Q_ROWS) + len(K_ROWS)
    with stage(nc, f"{tag}a") as s:
        qst = s.sb("qst", [ROWS + MAX_ROWS, H, S], BF16)
        kst = s.sb("kst", [ROWS + MAX_ROWS, H, keys], BF16)
        probs = s.sb("probs", [P, PR, 1024])
        lnb = s.sb("lnb", [P, 3, 1024]) if yat else None
        den, rec, accs = (s.sb(n, [P, 2, 512]) for n in ("den", "rec", "accs"))
        sc = [s.ps(f"sc{i}", [P, 1024]) for i in range(NS)]
        acc = [s.ps(f"acc{i}") for i in range(NA)]
        if not yat:
            side_ps = [s.ps(f"side{i}") for i in range(3)]
            mx = s.sb("mx", [P, 2, ST, 4, 2])
            mxm = s.sb("mxm", [P, 2, ST, 4])
            neg = s.sb("neg", [4, MAX_ROWS, S], BF16)
        stack_in = [s.sem(f"stack_in{g}") for g in range(G)]
        scores_ready, probs_ready, pv_done = s.sem("scores_ready"), s.sem("probs_ready"), s.sem("pv_done")
        squared, pool_probs = s.sem("squared"), s.sem("pool_probs")
        ln_done, rec_done, once_done, ones = s.sem("ln_done"), s.sem("rec_done"), s.sem("once_done"), s.sem("ones")
        den_ready, den_ln, den_rec, step, acc_free, acc_in = (s.sem(n) for n in (
            "den_ready", "den_ln", "den_rec", "step", "acc_free", "acc_in"))
        side_mm, side_done, max_done, neg_step = (s.sem(n) for n in ("side_mm", "side_done", "max_done", "neg_step"))
        placed = [s.sem(f"placed{i}") for i in range(2)]

        def on_pool(u):
            return yat and u % 4 == 3

        def ready(n):
            return (n - n // 4, n // 4) if yat else (n, 0)

        def after(u):
            g = u // UPG - 1
            return g if g >= 0 and u % UPG == min(6 if yat else 4, UPG - 1) else None

        def side_tasks(u):
            g, i = u // UPG + AHEAD, u % UPG
            if yat or u >= units:
                return []
            over = 4 if window else 12
            mus = range(MU * min(i, over) // over, MU * min(i + 1, over) // over) if g < GR else []
            rows_g = g - 1 if window else g
            rows_due = AHEAD <= rows_g < GR and i == (1 if window else 12)
            return [("max", g, k) for k in mus] + ([("rows", rows_g, 0)] if rows_due else [])

        before = [] if yat else [("max", g, k) for g in range(AHEAD) for k in range(MU)] + [
            ("rows", g, 0) for g in range(AHEAD)]
        order = before + [task for u in range(units) for task in side_tasks(u)]
        number = {task: n for n, task in enumerate(order)}

        with nc.Block() as block:

            @block.sync
            def _(sp):
                def load(gr):
                    b, g = divmod(gr, G)
                    if b:
                        sp.wait_ge(scores_ready, UPG * (gr - G + 1))
                    for rows_of, dram, stack in ((Q_ROWS, m.q_dram, qst), (K_ROWS, m.k_dram, kst)):
                        for i, part in enumerate(rows_of):
                            sp.dma_start(stack[D * i:D * (i + 1), 4 * g:4 * g + 4, :],
                                         dram[b][part, 4 * D * g:4 * D * (g + 1), :].rearrange("(h d) t -> d h t", d=D))\
                                .then_inc(stack_in[g], 16)

                def place(gr):
                    g = gr % G
                    sp.wait_ge(side_done, number["rows", gr, 0] + 1)
                    if gr >= G:
                        sp.wait_ge(scores_ready, UPG * (gr - G + 1))
                    for i in range(MAX_ROWS):
                        sp.dma_start(qst[ROWS + i:ROWS + i + 1, 4 * g:4 * g + 4, :], neg[:, i, :])\
                            .then_inc(placed[gr % 2], 16)
                for gr in range(G):
                    load(gr)
                if not yat:
                    for gr in range(AHEAD):
                        place(gr)
                for gr in range(GR):
                    if not yat and not window and gr + AHEAD < GR:
                        place(gr + AHEAD)
                    if gr + G < GR:
                        load(gr + G)
                    if window and gr + AHEAD < GR:
                        place(gr + AHEAD)

            @block.gpsimd
            def _(pool):
                nc.gpsimd.memset(m.vaug[:, :, :, D:VW], 1.0).then_inc(ones, 1)
                if not yat:
                    pool.wait_ge(ones, 1)
                    nc.gpsimd.memset(kst[ROWS:ROWS + MAX_ROWS, :, :], 1.0).then_inc(ones, 1)
                for u in range(units):
                    if on_pool(u):
                        pool.wait_ge(squared, ready(u + 1)[1])
                        pool.wait_ge(rec_done, u + 1)
                        nc.gpsimd.tensor_tensor(probs[:, u % PR, :], probs[:, u % PR, :], lnb[:, u % 3, :], ALU.mult)\
                            .then_inc(pool_probs, 1)

            @block.tensor
            def _(pe):
                def stacks(gr):
                    pe.wait_ge(stack_in[gr % G], 16 * loads_per_group * (gr // G + 1))

                def side(n):
                    kind, gr, i = order[n]
                    ps = side_ps[n % 3]
                    if n >= 3:
                        pe.wait_ge(side_done, n - 2)
                    if kind == "rows":
                        pe.wait_ge(max_done, gr + 1)
                        for t in range(ST):
                            last = nc.tensor.transpose(ps[0:4, t * P:(t + 1) * P], mxm[:, gr % 2, t, :], R.ident[:, :])
                        last.then_inc(side_mm, 1)
                        return
                    if i == 0:
                        stacks(gr)
                    if window:
                        h, half = 4 * (gr % G) + i // 2, i % 2
                        for t in (2 * half, 2 * half + 1):
                            lo = 0 if t else P
                            out = ps[:, 2 * P * (t % 2) + lo:2 * P * (t % 2 + 1)]
                            nc.tensor.matmul(out, R.ident_b[:, :], R.window[:, 1, lo:], start=True, stop=False)
                            last = nc.tensor.matmul(out, qst[0:ROWS, h, t * P:(t + 1) * P],
                                                    kst[0:ROWS, h, (t - 1) * P + lo:(t + 1) * P],
                                                    start=False, stop=True)
                    else:
                        h, qt, half = 4 * (gr % G) + i // 8, i // 2 % 4, i % 2
                        last = nc.tensor.matmul(ps[:, :], qst[0:ROWS, h, qt * P:(qt + 1) * P],
                                                kst[0:ROWS, h, half * 512:(half + 1) * 512], start=True, stop=True)
                    last.then_inc(side_mm, 1)

                def scores(u, half):
                    gr, kp = u // UPG, u % UPG // 4
                    h, ps = 4 * (gr % G) + u % 4, sc[u % NS]
                    if u % UPG == 0 and half == 0:
                        stacks(gr)
                        if not yat:
                            pe.wait_ge(placed[gr % 2], 16 * MAX_ROWS * (gr // 2 + 1))
                            pe.wait_ge(ones, 2)
                    if u >= NS and half == 0:
                        if on_pool(u - NS):
                            pe.wait_ge(squared, ready(u - NS + 1)[1])
                        else:
                            pe.wait_ge(probs_ready, ready(u - NS + 1)[0])
                    if window:
                        for t in (2 * half, 2 * half + 1):
                            out = ps[:, base[t]:base[t] + width[t]]
                            nc.tensor.matmul(out, R.ident_b[:, :], R.window[:, 0, 0:width[t]], start=True, stop=False)
                            last = nc.tensor.matmul(out, kst[0:rows, h, t * P:(t + 1) * P],
                                                    qst[0:rows, h, t * P:t * P + width[t]], start=False, stop=True)
                    else:
                        kt = 2 * kp + half
                        last = nc.tensor.matmul(ps[:, half * 512:(half + 1) * 512], kst[0:rows, h, kt * P:(kt + 1) * P],
                                                qst[0:rows, h, :], start=True, stop=True)
                    if half == 1:
                        last.then_inc(scores_ready, 1)

                def pv(quad, piece):
                    gr, kp = quad // QPG, quad % QPG
                    b, g = divmod(gr, G)
                    if piece == 0:
                        pe.wait_ge(probs_ready, ready(4 * quad + 4)[0])
                        if yat:
                            pe.wait_ge(pool_probs, ready(4 * quad + 4)[1])
                        pe.wait_ge(ones, 1)
                        if kp == 0 and gr >= NA:
                            pe.wait_ge(acc_free, gr - NA + 1)
                    out, last = acc[gr % NA], None
                    if window:
                        for kt in ([piece] if piece == 0 else [piece - 1, piece]):
                            at = base[kt] + (P if kt < piece else 0)
                            for j in range(4):
                                last = nc.tensor.matmul(
                                    out[VW * j:VW * (j + 1), piece * P:(piece + 1) * P],
                                    m.vaug[:, b * kt_n + kt, 4 * g + j, :], probs[:, (4 * quad + j) % PR, at:at + P],
                                    start=kt == max(piece - 1, 0), stop=kt == piece)
                    else:
                        i, kt = piece // 2, 2 * kp + piece // 2
                        for j in (2 * (piece % 2), 2 * (piece % 2) + 1):
                            last = nc.tensor.matmul(
                                out[VW * j:VW * (j + 1), :], m.vaug[:, b * kt_n + kt, 4 * g + j, :],
                                probs[:, (4 * quad + j) % PR, i * 512:(i + 1) * 512],
                                start=kt == 0, stop=kt == kt_n - 1)
                    if piece == 3:
                        last.then_inc(pv_done, 1)

                for n in range(len(before)):
                    side(n)
                n = len(before)
                for u in range(units + LAG):
                    due = len(side_tasks(u))
                    for piece in range(3):
                        if piece < 2 and u < units:
                            scores(u, piece)
                        if piece == 2 and u >= LAG:
                            pv((u - LAG) // 4, (u - LAG) % 4)
                        for _ in range((due + 2 - piece) // 3):
                            side(n)
                            n += 1

            @block.scalar
            def _(act):
                nc.scalar.preload_act_table_set(TABLE_SET)

                def weights(u):
                    act.wait_ge(scores_ready, u + 1)
                    if u >= PR:
                        act.wait_ge(pv_done, (u - PR) // 4 + 1)
                    nc.scalar.activation(probs[:, u % PR, 0:cols], sc[u % NS][:, 0:cols], ACT.Exp,
                                         scale=float(D) ** -0.5).then_inc(probs_ready, 1)

                def reciprocals(u):
                    act.wait_ge(scores_ready, u + 1)
                    if u >= 3:
                        if on_pool(u - 3):
                            act.wait_ge(pool_probs, ready(u - 2)[1])
                        else:
                            act.wait_ge(probs_ready, ready(u - 2)[0])
                    nc.scalar.activation(lnb[:, u % 3, :], sc[u % NS][:, :], ACT.Ln, bias=R.yat_one[:, 0:1], scale=-1.0)\
                        .then_inc(ln_done, 1)
                    act.wait_ge(ln_done, u + 1)
                    nc.scalar.activation(lnb[:, u % 3, :], lnb[:, u % 3, :], ACT.Exp, scale=-1.0).then_inc(rec_done, 1)
                    if on_pool(u):
                        if u >= PR:
                            act.wait_ge(pv_done, (u - PR) // 4 + 1)
                        nc.scalar.activation(probs[:, u % PR, :], sc[u % NS][:, :], ACT.Square, bias=1.0)\
                            .then_inc(squared, 1)

                def sums(gr):
                    act.wait_ge(den_ready, gr + 1)
                    nc.scalar.activation(rec[:, gr % 2, :], den[:, gr % 2, :], ACT.Ln).then_inc(den_ln, 1)
                    act.wait_ge(den_ln, gr + 1)
                    nc.scalar.activation(rec[:, gr % 2, :], rec[:, gr % 2, :], ACT.Exp, scale=-1.0).then_inc(den_rec, 1)
                for u in range(units):
                    if yat:
                        reciprocals(u)
                    else:
                        weights(u)
                    if not yat and after(u) is not None:
                        sums(after(u))
                    if yat and u and after(u - 1) is not None:
                        sums(after(u - 1))
                sums(GR - 1)

            @block.vector
            def _(dve):
                link = chain_of(dve, step)

                def side(n):
                    kind, gr, i = order[n]
                    ps, out = side_ps[n % 3], mx[:, gr % 2]
                    dve.wait_ge(side_mm, n + 1)
                    if kind == "rows":
                        if gr >= 1:
                            dve.wait_ge(placed[(gr - 1) % 2], 16 * MAX_ROWS * ((gr - 1) // 2 + 1))
                        high, mid = (neg[:, i, :] for i in range(MAX_ROWS))
                        nc.vector.tensor_scalar(high, ps[0:4, :], -1.0, None, ALU.mult).then_inc(neg_step, 1)
                        dve.wait_ge(neg_step, gr + 1)
                        nc.vector.scalar_tensor_tensor(out=mid, in0=ps[0:4, :], scalar=-1.0, in1=high, op0=ALU.mult,
                                                       op1=ALU.subtract).then_inc(side_done, 1)
                        return
                    if window:
                        j, half = i // 2, i % 2
                        if half == 0:
                            nc.vector.tensor_reduce(out=out[:, 0, j, 0:1], in_=ps[:, P:2 * P], op=ALU.max, axis=AX.X)
                            ins = nc.vector.tensor_reduce(out=out[:, 1, j, 0:1], in_=ps[:, 2 * P:4 * P], op=ALU.max,
                                                          axis=AX.X)
                        else:
                            ins = nc.vector.tensor_reduce(out=out[:, 2:4, j, 0],
                                                          in_=ps[:, :].rearrange("p (t k) -> p t k", t=2),
                                                          op=ALU.max, axis=AX.X)
                    else:
                        ins = nc.vector.tensor_reduce(out=out[:, i // 2 % 4, i // 8, i % 2:i % 2 + 1], in_=ps[:, :],
                                                      op=ALU.max, axis=AX.X)
                    ins.then_inc(side_done, 1)
                    if i == MU - 1:
                        dve.wait_ge(side_done, n + 1)
                        if window:
                            nc.vector.tensor_copy(mxm[:, gr % 2], mx[:, gr % 2, :, :, 0]).then_inc(max_done, 1)
                        else:
                            nc.vector.tensor_tensor(mxm[:, gr % 2], mx[:, gr % 2, :, :, 0], mx[:, gr % 2, :, :, 1],
                                                    ALU.max).then_inc(max_done, 1)

                def weights(u):
                    if on_pool(u):
                        return
                    dve.wait_ge(rec_done, u + 1)
                    nc.vector.scalar_tensor_tensor(out=lnb[:, u % 3, :], in0=sc[u % NS][:, :], scalar=1.0,
                                                   in1=lnb[:, u % 3, :], op0=ALU.add, op1=ALU.mult).then_inc(once_done, 1)
                    dve.wait_ge(once_done, ready(u + 1)[0])
                    if u >= PR:
                        dve.wait_ge(pv_done, (u - PR) // 4 + 1)
                    nc.vector.scalar_tensor_tensor(out=probs[:, u % PR, :], in0=sc[u % NS][:, :], scalar=1.0,
                                                   in1=lnb[:, u % 3, :], op0=ALU.add, op1=ALU.mult).then_inc(probs_ready, 1)

                def sums_before(gr):
                    a, d = accs[:, gr % 2, :], den[:, gr % 2, :]
                    dve.wait_ge(pv_done, (gr + 1) * QPG)
                    nc.vector.tensor_copy(a, acc[gr % NA][:, :]).then_inc(acc_free, 1)
                    dve.wait_ge(acc_free, gr + 1)
                    if yat:
                        link(nc.vector.stream_shuffle(d, a, [D + i % D for i in range(VW)]))
                        nc.vector.tensor_scalar_add(d, d, 1e-6).then_inc(den_ready, 1)
                    else:
                        nc.vector.stream_shuffle(d, a, [D + i % D for i in range(VW)]).then_inc(den_ready, 1)

                def sums_after(gr):
                    a, d, r = accs[:, gr % 2, :], den[:, gr % 2, :], rec[:, gr % 2, :]
                    dve.wait_ge(den_rec, gr + 1)
                    link(nc.vector.tensor_tensor(d, d, r, ALU.mult))
                    link(nc.vector.scalar_tensor_tensor(out=d, in0=d, scalar=-2.0, in1=r, op0=ALU.add, op1=ALU.mult))
                    nc.vector.scalar_tensor_tensor(out=m.outT[gr // G][:, gr % G, :], in0=a, scalar=-1.0, in1=d,
                                                   op0=ALU.mult, op1=ALU.mult)
                for n in range(len(before)):
                    side(n)
                n = len(before)
                sums_due = None
                for u in range(units):
                    if after(u) is not None:
                        sums_before(after(u))
                        sums_due = after(u)
                    if yat:
                        weights(u)
                        if u >= 2 and after(u - 2) is not None:
                            sums_after(after(u - 2))
                        continue
                    for _ in side_tasks(u):
                        side(n)
                        n += 1
                    if sums_due is not None:
                        sums_after(sums_due)
                        sums_due = None
                if yat:
                    sums_after(GR - 2)
                sums_before(GR - 1)
                sums_after(GR - 1)


def stage_out(nc, R, tag, outT, w, bias):
    with stage(nc, f"{tag}o") as s:
        ps = [s.ps(f"y{i}") for i in range(NT)]
        ready, added = s.sem("ready"), s.sem("added")
        with nc.Block() as block:

            @block.tensor
            def _(pe):
                for t in range(NT):
                    b, at = t // ST, t % ST * P
                    for g in range(G):
                        last = nc.tensor.matmul(ps[t][:, 0:E], outT[b][:, g, at:at + P], w[:, g, :],
                                                start=g == 0, stop=bias is None and g == G - 1)
                    if bias is not None:
                        last = nc.tensor.matmul(ps[t][:, 0:E], R.ones_row[:, :], bias[:, :], start=False, stop=True)
                    last.then_inc(ready, 1)

            @block.vector
            def _(dve):
                for t in range(NT):
                    dve.wait_ge(ready, t + 1)
                    nc.vector.tensor_tensor(R.x[:, t, :], R.x[:, t, :], ps[t][:, 0:E], ALU.add).then_inc(added, 1)


def attention16(nc, A, R, tag, kind, wq, wk, wv, wo, bq=None, bk=None, bv=None, bo=None):
    keys = CTX if kind == "cross" else S
    with ExitStack() as ctx:
        m = Resident()

        def sb(name, shape, dt=FP32, ctx=ctx):
            return ctx.enter_context(nc.sbuf_tensor(f"{tag}_{name}", shape, dt))
        m.vaug = sb("vaug", [P, B * keys // P, H, VW])
        m.outT = [R.xn[:, :, :].rearrange("p (g a) e -> p g (a e)", g=G), sb("out1", [P, G, S])[:, :, :]]
        m.q_dram, m.k_dram = ([nc.dram_tensor(f"{tag}_{n}_parts{b}", (PARTS, E, t), BF16, kind="Internal").ap()
                               for b in range(B)] for n, t in (("q", S), ("k", keys)))
        w_out = sb("wo", [P, G, E])
        wo_j = wo.rearrange("(g j d) n -> j d g n", g=G, j=4)
        loads = [(w_out[VW * j:VW * j + D, :, :], wo_j[j]) for j in range(4)]
        b_out = None
        if bo is not None:
            b_out = sb("bo", [1, E])
            loads.append((b_out[:, :], bo.rearrange("(a n) -> a n", a=1)))
        with ExitStack() as projection:
            w = [Pair(*(sb(n + part, [P, KE, E], FP32R, projection) for part in "hl")) for n in ("wq", "wk", "wv")]
            bias = []
            for n, a in (("bq", bq), ("bk", bk)):
                t = None
                if a is not None:
                    t = sb(n, [P, KE] if kind == "cross" else [P, E], FP32, projection)
                    loads.append((t[:, :], a.rearrange("(m p) -> p m", p=P) if kind == "cross" else a.partition_broadcast(P)))
                bias.append(t)
            if bv is not None:
                bias.append(sb("bv", [P, E], FP32, projection))
                loads.append((bias[2][:, :], bv.partition_broadcast(P)))
            with ExitStack() as whole:
                w_full = [sb(n, [P, KE, E], FP32, whole) for n in ("wq", "wk", "wv")]
                splits = [(f[:, :, :], p[:, :, :]) for f, p in zip(w_full, w)]
                loads = [(t[:, :, :], a.rearrange("(k p) n -> p k n", p=P)) for t, a in zip(w_full, (wq, wk, wv))] + loads
                stage_norm(nc, R, f"{tag}n", loads, w_out, splits)
            stage_project(nc, R, tag, m, kind, *w, *bias)
        stage_attend(nc, R, tag, m, kind)
        stage_out(nc, R, tag, m.outT, w_out, b_out)


def stage_wide(nc, R, wq, wk, wv, w_out, b_out):
    HP = H1 // 2
    PAIRS = B * HP
    units = PAIRS * CT
    RP, PR, LAG = 3, 3, 2
    CQ = CTX // 512

    def side_tasks(p, i):
        out = []
        if i == 3 and p >= 1:
            out.append(("den", p - 1, 0))
        if p + 1 < PAIRS:
            out += [("max", p + 1, k) for k in range(16 * i // 5, 16 * (i + 1) // 5) if i < 5]
            if i == 6:
                out.append(("rows", p + 1, 0))
        if p // 2 + 1 < PAIRS // 2:
            out += [("v", p // 2 + 1, 2 * (p % 2) + k) for k, at in enumerate((5, 7)) if i == at]
        if p + 2 < PAIRS:
            out += [(kind, p + 2, c) for kind, c, at in (("q", 0, 4), ("k", 0, 5), ("k", 1, 6)) if i == at]
        if p == HP and i >= 6:
            out += [("out", 0, 2 * (i - 6) + k) for k in range(2)]
        return out

    before = [("q", 0, 0), ("k", 0, 0), ("k", 0, 1)] + [("max", 0, i) for i in range(8)]
    before += [("q", 1, 0), ("k", 1, 0), ("k", 1, 1)] + [("max", 0, i) for i in range(8, 16)]
    before += [("v", 0, i) for i in range(2)] + [("rows", 0, 0)] + [("v", 0, i) for i in range(2, 4)]
    behind = [("den", PAIRS - 1, 0)] + [("out", 1, i) for i in range(ST)]
    order = before + [t for p in range(PAIRS) for i in range(CT) for t in side_tasks(p, i)] + behind
    number = {t: n for n, t in enumerate(order)}

    with stage(nc, "c") as s:
        q1, q2 = (s.sb(n, [P, 2 * RP, S], FP32R) for n in ("q1", "q2"))
        k1, k2 = (s.sb(n, [P, 2 * RP, CTX], FP32R) for n in ("k1", "k2"))
        v = s.sb("v", [P, 2, CT, 4 * D1])
        probs = s.sb("probs", [P, PR, 1024])
        total = s.sb("total", [P, 2, 1024])
        rec, den = ([total[:, i, c * 512:(c + 1) * 512] for i in range(2)] for c in range(2))
        acc_s = s.sb("acc_s", [P, 512])
        ones = s.sb("ones", [P, D1])
        mx, mxm = s.sb("mx", [P, 2, 2, ST, CQ]), s.sb("mxm", [P, 2, 2, ST])
        outT = R.xn[:, :, :].rearrange("p (g a) e -> p g (a e)", g=G)
        sc = [s.ps(f"sc{i}", [P, 1024]) for i in range(2)]
        side_ps = [s.ps(f"side{i}") for i in range(2)]
        acc, sums = s.ps("acc"), s.ps("sums")
        side_mm, side_done, high_done = s.sem("side_mm"), s.sem("side_done"), s.sem("high_done")
        twin_done = s.sem("twin_done")
        scores_ready, probs_ready, pv_done, summed = (s.sem(n) for n in ("scores_ready", "probs_ready", "pv_done", "summed"))
        acc_copied, den_ln, den_rec, divided = (s.sem(n) for n in ("acc_copied", "den_ln", "den_rec", "divided"))
        pads, max_done, step = s.sem("pads"), s.sem("max_done"), s.sem("step")

        def halves(j):
            return (slice(0, D1), slice(D1, P)) if j == 0 else (slice(D1, P), slice(0, D1))

        def sums_with(u):
            return (CT - 1) * (u // CT) + max(u % CT, 1)

        with nc.Block() as block:

            @block.gpsimd
            def _(pool):
                nc.gpsimd.memset(ones[:, :], 1.0).then_inc(pads, 1)
                for slot in range(2 * RP):
                    other = halves(slot % 2)[1]
                    pool.wait_ge(pads, 1 + 2 * slot)
                    nc.gpsimd.memset(q2[other, slot, :].bitcast(FP32), 0.0).then_inc(pads, 1)
                    pool.wait_ge(pads, 2 + 2 * slot)
                    nc.gpsimd.memset(k2[other, slot, :].bitcast(FP32), 1.0).then_inc(pads, 1)
                pool.wait_ge(pads, 1 + 4 * RP)
                for u in range(units):
                    p, kt = u // CT, u % CT
                    if kt == 0:
                        continue
                    pool.wait_ge(probs_ready, u + 1)
                    if kt == 1 and p >= 2:
                        pool.wait_ge(divided, p - 1)
                    out = total[:, p % 2, :]
                    if u >= 2:
                        pool.wait_ge(summed, sums_with(u) - 1)
                    nc.gpsimd.tensor_tensor(out, probs[:, (u - 1) % PR, :] if kt == 1 else out, probs[:, u % PR, :],
                                            ALU.add).then_inc(summed, 1)

            @block.tensor
            def _(pe):
                def side(n):
                    kind, p, i = order[n]
                    ps = side_ps[n % 2]
                    if n >= 2:
                        pe.wait_ge(side_done, n - 1)
                    b, g = p // HP, p % HP
                    if kind in "qk":
                        w, x, at = (wq, R.xnT, b * S) if kind == "q" else (wk, R.ctxT, b * CTX + i * 512)
                        for k in range(KE):
                            last = matmul3(nc, ps[:, :], w[:, k, g * P:(g + 1) * P], x[:, k, at:at + 512],
                                           start=k == 0, stop=k == KE - 1)
                    if kind == "v":
                        for j in range(2):
                            at = (p // 2) * CTX + (2 * i + j) * P
                            for k in range(KE):
                                last = matmul3(nc, ps[:, j * 256:(j + 1) * 256], R.ctxT[:, k, at:at + P],
                                               wv[:, k, p % 2 * 256:(p % 2 + 1) * 256], start=k == 0, stop=k == KE - 1)
                    if kind == "max":
                        slot, qt, c = p % RP * 2 + i // 8, i // 2 % 4, i % 2
                        pe.wait_ge(side_done, number["k", p, 1] + 1)
                        pe.wait_ge(twin_done, (1 + CQ) * (p + 1))
                        last = nc.tensor.matmul(ps[:, :], q1[:, slot, qt * P:(qt + 1) * P],
                                                k1[:, slot, c * 512:(c + 1) * 512], start=True, stop=True)
                    if kind == "rows":
                        pe.wait_ge(max_done, p + 1)
                        for j in range(2):
                            row = D1 * (1 - j)
                            for t in range(ST):
                                last = nc.tensor.matmul(ps[row:row + 1, t * P:(t + 1) * P], mxm[:, p % 2, j, t:t + 1],
                                                        R.ident[:, :], start=True, stop=True)
                    if kind == "den":
                        pe.wait_ge(summed, (CT - 1) * (p + 1))
                        pe.wait_ge(pads, 1)
                        for j in range(2):
                            last = nc.tensor.matmul(ps[D1 * j:D1 * (j + 1), :], ones[:, :],
                                                    total[:, p % 2, j * 512:(j + 1) * 512], start=True, stop=True)
                    if kind == "out":
                        pe.wait_ge(divided, HP * (p + 1))
                        for g in range(G):
                            nc.tensor.matmul(ps[:, 0:E], outT[:, g, i * P:(i + 1) * P], w_out[:, g, :],
                                             start=g == 0, stop=False)
                        last = nc.tensor.matmul(ps[:, 0:E], R.ones_row[:, :], b_out[:, :], start=False, stop=True)
                    last.then_inc(side_mm, 1)

                def scores(u, j):
                    p, kt = u // CT, u % CT
                    if kt == 0 and j == 0:
                        pe.wait_ge(side_done, number["rows", p, 0] + 1)
                        pe.wait_ge(pads, 1 + 4 * RP)
                    if u >= 2 and j == 0:
                        pe.wait_ge(probs_ready, u - 1)
                    slot, out = p % RP * 2 + j, sc[u % 2][:, j * 512:(j + 1) * 512]
                    nc.tensor.matmul(out, k1[:, slot, kt * P:(kt + 1) * P], q1[:, slot, :], start=True, stop=False)
                    last = nc.tensor.matmul(out, k2[:, slot, kt * P:(kt + 1) * P], q2[:, slot, :], start=False, stop=True)
                    if j == 1:
                        last.then_inc(scores_ready, 1)

                def pv(u):
                    p, kt = u // CT, u % CT
                    pe.wait_ge(probs_ready, u + 1)
                    if kt == 0:
                        if p >= 1:
                            pe.wait_ge(acc_copied, p)
                        pe.wait_ge(side_done, number["v", p // 2, 3] + 1)
                    for j in range(2):
                        at = (2 * (p % 2) + j) * D1
                        last = nc.tensor.matmul(acc[D1 * j:D1 * (j + 1), :], v[:, p // 2 % 2, kt, at:at + D1],
                                                probs[:, u % PR, j * 512:(j + 1) * 512], start=kt == 0, stop=kt == CT - 1)
                    last.then_inc(pv_done, 1)
                n = 0
                for n in range(len(before)):
                    side(n)
                n = len(before)
                for u in range(units + LAG):
                    due = len(side_tasks(u // CT, u % CT)) if u < units else 0
                    for piece in range(3):
                        if piece < 2 and u < units:
                            scores(u, piece)
                        if piece == 2 and u >= LAG:
                            pv(u - LAG)
                        for _ in range((due + 2 - piece) // 3):
                            side(n)
                            n += 1
                for n in range(n, len(order)):
                    side(n)

            @block.scalar
            def _(act):
                nc.scalar.preload_act_table_set(TABLE_SET)
                copies = [0]

                def side(n):
                    kind, p, i = order[n]
                    if kind == "den":
                        act.wait_ge(side_done, n + 1)
                        nc.scalar.activation(rec[p % 2], den[p % 2], ACT.Ln).then_inc(den_ln, 1)
                        act.wait_ge(den_ln, p + 1)
                        nc.scalar.activation(rec[p % 2], rec[p % 2], ACT.Exp, scale=-1.0).then_inc(den_rec, 1)
                    if kind in "qk":
                        act.wait_ge(side_mm, n + 1)
                        if p >= RP:
                            act.wait_ge(scores_ready, CT * (p - RP + 1))
                        twin, at = (q1, slice(0, S)) if kind == "q" else (k2, slice(i * 512, (i + 1) * 512))
                        first = q1 if kind == "q" else k1
                        for j in range(2):
                            own, slot = halves(j)[0], p % RP * 2 + j
                            last = nc.scalar.activation(first[own, slot, at], side_ps[n % 2][own, :], ACT.Copy)
                        last.then_inc(high_done, 1)
                        copies[0] += 1
                        act.wait_ge(high_done, copies[0])
                        for j in range(2):
                            (own, other), slot = halves(j), p % RP * 2 + j
                            last = nc.scalar.activation(twin[other if kind == "q" else own, slot, at],
                                                        first[own, slot, at].bitcast(FP32), ACT.Copy)
                        last.then_inc(twin_done, 1)

                for n in range(len(before)):
                    side(n)
                n = len(before)
                for u in range(units):
                    act.wait_ge(scores_ready, u + 1)
                    if u >= PR:
                        act.wait_ge(pv_done, u - PR + 1)
                        act.wait_ge(summed, sums_with(u - PR))
                    nc.scalar.activation(probs[:, u % PR, :], sc[u % 2][:, :], ACT.Exp, scale=float(D1) ** -0.5)\
                        .then_inc(probs_ready, 1)
                    for _ in side_tasks(u // CT, u % CT):
                        side(n)
                        n += 1
                for n in range(n, len(order)):
                    side(n)

            @block.vector
            def _(dve):
                link = chain_of(dve, step)
                highs = [0]

                def side(n):
                    kind, p, i = order[n]
                    ps = side_ps[n % 2]
                    dve.wait_ge(side_mm, n + 1)
                    if kind in "qk":
                        highs[0] += 1
                        dve.wait_ge(high_done, highs[0])
                        for j in range(2):
                            own, other = halves(j)
                            slot, at = p % RP * 2 + j, slice(i * 512, (i + 1) * 512)
                            if kind == "q":
                                high, low = q1[own, slot, :], q2[own, slot, :]
                            else:
                                high, low = k1[own, slot, at], k1[other, slot, at]
                            last = nc.vector.tensor_tensor(low, ps[own, :], high.bitcast(FP32), ALU.subtract)
                    if kind == "v":
                        if p >= 2:
                            dve.wait_ge(pv_done, 2 * CT * (p - 1))
                        last = nc.vector.tensor_copy(v[:, p % 2, 2 * i:2 * i + 2, :],
                                                     ps[:, :].rearrange("p (t n) -> p t n", t=2))
                    if kind == "max":
                        last = nc.vector.tensor_reduce(out=mx[:, p % 2, i // 8, i // 2 % 4, i % 2:i % 2 + 1], in_=ps[:, :],
                                                       op=ALU.max, axis=AX.X)
                    if kind == "rows":
                        dve.wait_ge(pads, 1 + 4 * RP)
                        for j in range(2):
                            row = D1 * (1 - j)
                            last = nc.vector.tensor_scalar(q2[row:row + 1, p % RP * 2 + j, :], ps[row:row + 1, :], -1.0,
                                                           None, ALU.mult)
                    if kind == "den":
                        last = nc.vector.tensor_copy(den[p % 2], ps[:, :])
                    if kind == "out":
                        x = R.x[:, p * ST + i, :]
                        last = nc.vector.tensor_tensor(x, x, ps[:, 0:E], ALU.add)
                    last.then_inc(side_done, 1)
                    if kind == "max" and i == 15:
                        dve.wait_ge(side_done, n + 1)
                        nc.vector.tensor_tensor(mxm[:, p % 2], mx[:, p % 2, :, :, 0], mx[:, p % 2, :, :, 1], ALU.max)\
                            .then_inc(max_done, 1)

                def copy_acc(p):
                    dve.wait_ge(pv_done, CT * (p + 1))
                    if p >= 1:
                        dve.wait_ge(divided, p)
                    nc.vector.tensor_copy(acc_s[:, :], acc[:, :]).then_inc(acc_copied, 1)

                def divide(p):
                    dve.wait_ge(den_rec, p + 1)
                    dve.wait_ge(acc_copied, p + 1)
                    d, r = den[p % 2], rec[p % 2]
                    link(nc.vector.tensor_tensor(d, d, r, ALU.mult))
                    link(nc.vector.scalar_tensor_tensor(out=d, in0=d, scalar=-2.0, in1=r, op0=ALU.add, op1=ALU.mult))
                    nc.vector.scalar_tensor_tensor(out=outT[:, p % HP, :], in0=acc_s[:, :], scalar=-1.0, in1=d,
                                                   op0=ALU.mult, op1=ALU.mult).then_inc(divided, 1)
                for n in range(len(before)):
                    side(n)
                n = len(before)
                for u in range(units):
                    p, i = u // CT, u % CT
                    if i == LAG and p >= 1:
                        copy_acc(p - 1)
                    for _ in side_tasks(p, i):
                        side(n)
                        n += 1
                    if i == 4 and p >= 1:
                        divide(p - 1)
                copy_acc(PAIRS - 1)
                side(n)
                divide(PAIRS - 1)
                for n in range(n + 1, len(order)):
                    side(n)


def attention_wide(nc, A, R):
    with ExitStack() as ctx:
        def sb(name, shape, dt=FP32, ctx=ctx):
            return ctx.enter_context(nc.sbuf_tensor(f"c_{name}", shape, dt))
        w_out, b_out = sb("wo", [P, G, E]), sb("bo", [1, E])
        w = [Pair(*(sb(n + part, [P, KE, H1 * D1], FP32R) for part in "hl")) for n in ("wq", "wk", "wv")]
        with ExitStack() as whole:
            w_full = [sb(n, [P, KE, H1 * D1], FP32, whole) for n in ("wq", "wk", "wv")]
            loads = [(t[:, :, :], A[f"L1_xattn_{n}"].rearrange("(k p) n -> p k n", p=P))
                     for t, n in zip(w_full + [w_out], ("Wq", "Wk", "Wv", "Wo"))]
            loads.append((b_out[:, :], A["L1_xattn_bo"].rearrange("(a n) -> a n", a=1)))
            stage_norm(nc, R, "cn", loads, splits=[(f[:, :, :], p[:, :, :]) for f, p in zip(w_full, w)])
        stage_wide(nc, R, *w, w_out, b_out)


def route_top2(nc, R, s, m, gate_w, block):
    NE = 8
    logits = s.ps("logits", [P, NT, NE])
    e, top, we2 = s.sb("e", [P, NT, NE]), s.sb("top", [P, NT, NE]), s.sb("we2", [P, NT, NE])
    idx, idxf = s.sb("idx", [P, NT, NE], U32), s.sb("idxf", [P, NT, NE])
    col = s.sb("col", [P, NT, 1])
    io_i, io_f = s.sb("io_i", [P, NE], I32), s.sb("io_f", [P, NE])
    ready, shifted, exps, iota_done, step = (s.sem(n) for n in ("r_logits", "r_shifted", "r_exps", "r_iota", "r_step"))
    bc = lambda ap: ap.broadcast_to([P, NT, NE])

    @block.tensor
    def _(pe):
        for t in range(NT):
            for k in range(KE):
                last = matmul3(nc, logits[:, t, :], R.xnT[:, k, t * P:(t + 1) * P], gate_w[:, k, :],
                                        start=k == 0, stop=k == KE - 1)
        last.then_inc(ready, 1)

    @block.gpsimd
    def _(pool):
        nc.gpsimd.iota(io_i[:, :], pattern=[[1, NE]], base=0, channel_multiplier=0).then_inc(iota_done, 1)

    @block.scalar
    def _(act):
        act.wait_ge(shifted, 1)
        nc.scalar.activation(e[:, :, :], e[:, :, :], ACT.Exp).then_inc(exps, 1)

    @block.vector
    def _(dve):
        link = chain_of(dve, step)
        v = nc.vector
        dve.wait_ge(ready, 1)
        link(v.tensor_reduce(out=col[:, :, 0], in_=logits[:, :, :], op=ALU.max, axis=AX.X))
        v.tensor_tensor(e[:, :, :], logits[:, :, :], bc(col[:, :, :]), ALU.subtract).then_inc(shifted, 1)
        dve.wait_ge(exps, 1)
        link(v.tensor_reduce(out=col[:, :, 0], in_=e[:, :, :], op=ALU.add, axis=AX.X))
        link(v.reciprocal(col[:, :, :], col[:, :, :]))
        link(v.tensor_tensor(e[:, :, :], e[:, :, :], bc(col[:, :, :]), ALU.mult))
        for t in range(NT):
            last = v.max(top[:, t, :], e[:, t, :])
        link(last)
        for t in range(NT):
            last = v.max_index(idx[:, t, :], top[:, t, :], e[:, t, :])
        link(last)
        link(v.tensor_copy(idxf[:, :, :], idx[:, :, :]))
        link(v.tensor_tensor(col[:, :, :], top[:, :, 0:1], top[:, :, 1:2], ALU.add))
        link(v.tensor_scalar_add(col[:, :, :], col[:, :, :], 1e-20))
        link(v.reciprocal(col[:, :, :], col[:, :, :]))
        link(v.tensor_tensor(top[:, :, :], top[:, :, :], bc(col[:, :, :]), ALU.mult))
        dve.wait_ge(iota_done, 1)
        link(v.tensor_copy(io_f[:, :], io_i[:, :]))
        grid = io_f[:, :].unsqueeze(1).broadcast_to([P, NT, NE])
        link(v.tensor_tensor(m.we[:, :, :], grid, bc(idxf[:, :, 0:1]), ALU.is_equal))
        link(v.tensor_tensor(we2[:, :, :], grid, bc(idxf[:, :, 1:2]), ALU.is_equal))
        link(v.tensor_tensor(m.we[:, :, :], m.we[:, :, :], bc(top[:, :, 0:1]), ALU.mult))
        link(v.tensor_tensor(we2[:, :, :], we2[:, :, :], bc(top[:, :, 1:2]), ALU.mult))
        link(v.tensor_tensor(m.we[:, :, :], m.we[:, :, :], we2[:, :, :], ALU.add))


def route_hash(nc, R, s, m, block):
    NE = 8
    sm, r, a, c = (s.sb(n, [P, NT, 1]) for n in ("sm", "r", "a", "c"))
    hi, hj = s.sb("hi", [P, NT, 1], I32), s.sb("hj", [P, NT, 1], I32)
    io_i, io_f, we2 = s.sb("io_i", [P, NE], I32), s.sb("io_f", [P, NE]), s.sb("we2", [P, NT, NE])
    iota_done, step = s.sem("h_iota"), s.sem("h_step")
    b1_t, b1_ready, wt_mm, wt_done = (s.sem(n) for n in ("h_b1t", "h_b1", "h_wt_mm", "h_wt"))
    tp = s.ps("b1_tp")
    wps = s.ps("wt_ps", [NE, N])
    routed = s.sem("h_routed")

    @block.gpsimd
    def _(pool):
        nc.gpsimd.iota(io_i[:, :], pattern=[[1, NE]], base=0, channel_multiplier=0).then_inc(iota_done, 1)

    @block.tensor
    def _(pe):
        rows = m.b1_rows.shape[0]
        nc.tensor.transpose(tp[:, 0:rows], m.b1_rows[:, :], R.ident[0:rows, 0:rows]).then_inc(b1_t, 1)
        pe.wait_ge(routed, 1)
        for t in range(NT):
            last = nc.tensor.transpose(wps[:, t * P:(t + 1) * P], m.we[:, t, :], R.ident[:, :])
        last.then_inc(wt_mm, 1)

    @block.vector
    def _(dve):
        link = chain_of(dve, step)
        v = nc.vector
        dve.wait_ge(b1_t, 1)
        v.tensor_copy(m.b1[:, :], tp[:, 0:m.b1_rows.shape[0]]).then_inc(b1_ready, 1)
        link(v.tensor_tensor(sm[:, :, :], R.xn[:, :, 0:1], R.xn[:, :, 1:2], ALU.add))
        link(v.tensor_copy(hi[:, :, :], sm[:, :, :]))
        link(v.tensor_copy(r[:, :, :], hi[:, :, :]))
        link(v.tensor_tensor(a[:, :, :], r[:, :, :], sm[:, :, :], ALU.is_gt))
        link(v.tensor_scalar(c[:, :, :], sm[:, :, :], 0.0, None, ALU.is_gt))
        link(v.tensor_tensor(c[:, :, :], a[:, :, :], c[:, :, :], ALU.mult))
        link(v.tensor_tensor(a[:, :, :], r[:, :, :], sm[:, :, :], ALU.is_lt))
        link(v.tensor_tensor(r[:, :, :], r[:, :, :], c[:, :, :], ALU.subtract))
        link(v.tensor_scalar(c[:, :, :], sm[:, :, :], 0.0, None, ALU.is_lt))
        link(v.tensor_tensor(c[:, :, :], a[:, :, :], c[:, :, :], ALU.mult))
        link(v.tensor_tensor(r[:, :, :], r[:, :, :], c[:, :, :], ALU.add))
        dve.wait_ge(iota_done, 1)
        link(v.tensor_copy(io_f[:, :], io_i[:, :]))
        grid = io_f[:, :].unsqueeze(1).broadcast_to([P, NT, NE])
        bc = lambda ap: ap.broadcast_to([P, NT, NE])
        for i, out in enumerate((m.we, we2)):
            link(v.tensor_scalar_add(c[:, :, :], r[:, :, :], float(i)))
            link(v.tensor_copy(hi[:, :, :], c[:, :, :]))
            link(v.tensor_scalar(hj[:, :, :], hi[:, :, :], NE - 1, None, ALU.bitwise_and))
            link(v.tensor_copy(c[:, :, :], hj[:, :, :]))
            link(v.tensor_tensor(out[:, :, :], grid, bc(c[:, :, :]), ALU.is_equal))
        link(v.tensor_tensor(m.we[:, :, :], m.we[:, :, :], we2[:, :, :], ALU.add))
        v.tensor_scalar(m.we[:, :, :], m.we[:, :, :], 0.5, None, ALU.mult).then_inc(routed, 1)
        dve.wait_ge(wt_mm, 1)
        for i in range(2):
            v.tensor_copy(m.weT[:, i * 512:(i + 1) * 512], wps[:, i * 512:(i + 1) * 512]).then_inc(wt_done, 1)


def stage_experts(nc, R, m, tag, experts, hid, gated):
    HT = hid // P
    n_w = 3 if gated else 2
    slot_w = n_w * KE * hid
    CH = N // 512
    units = [(e, c) for e in range(len(experts)) for c in range(CH)]
    with stage(nc, tag) as s:
        wfull = s.sb("wfull", [P, slot_w])
        wslot = Pair(s.sb("wslot_h", [P, 2, slot_w], FP32R), s.sb("wslot_l", [P, 2, slot_w], FP32R))
        hT = Pair(s.sb("hT_h", [P, 2, HT, 512], FP32R), s.sb("hT_l", [P, 2, HT, 512], FP32R))
        act_t = s.sb("act_t", [P, 3, 512]) if gated else None
        hid_t = s.sb("hid_t", [P, 3, 512])
        up = [s.ps(f"up{i}") for i in range(3)]
        gate = [s.ps(f"gate{i}") for i in range(3)] if gated else None
        down = [s.ps(f"down{i}") for i in range(2)]
        w_in, w_high, w_low, hid_done, h_high = (s.sem(n) for n in ("w_in", "w_high", "w_low", "hid_done", "h_high"))
        first_ready, act_done, h_done, y_ready, y_added = (s.sem(n) for n in (
            "first_ready", "act_done", "h_done", "y_ready", "y_added"))

        def weights(e):
            w = wslot[:, e % 2, :]
            k = KE * hid
            ups = [w[:, i * k:(i + 1) * k].rearrange("p (k n) -> p k n", k=KE) for i in range(n_w - 1)]
            return (*ups, w[:, (n_w - 1) * k:n_w * k].rearrange("p (k n) -> p k n", k=HT))

        with nc.Block() as block:

            @block.sync
            def _(sp):
                for e, (*drams, _) in enumerate(experts):
                    if e >= 1:
                        sp.wait_ge(w_low, e)
                    at = 0
                    for src in drams:
                        n = src.shape[0] * src.shape[1] // P
                        sp.dma_start(wfull[:, at:at + n].rearrange("p (k n) -> p k n", n=src.shape[1]),
                                     src.rearrange("(k p) n -> p k n", p=P)).then_inc(w_in, 16)
                        at += n

            @block.tensor
            def _(pe):
                def first(n):
                    e, c = units[n]
                    w = weights(e)
                    if c == 0:
                        pe.wait_ge(w_low, e + 1)
                    for i in range(HT):
                        u = n * HT + i
                        if u >= 3:
                            pe.wait_ge(hid_done, u - 2)
                        for out, wi in zip((gate, up) if gated else (up,), w):
                            for k in range(KE):
                                last = matmul3(nc, out[u % 3][:, :], wi[:, k, i * P:(i + 1) * P],
                                                        R.xnT[:, k, c * 512:(c + 1) * 512],
                                                        start=k == 0, stop=k == KE - 1)
                        last.then_inc(first_ready, 1)

                def second(n):
                    e, c = units[n]
                    wd = weights(e)[-1]
                    pe.wait_ge(h_done, (n + 1) * HT)
                    for t in range(4):
                        u = 4 * n + t
                        if u >= 2:
                            pe.wait_ge(y_added, u - 1)
                        for k in range(HT):
                            last = matmul3(nc, down[u % 2][:, 0:E], hT[:, n % 2, k, t * P:(t + 1) * P],
                                                    wd[:, k, :], start=k == 0, stop=k == HT - 1)
                        last.then_inc(y_ready, 1)
                for n in range(len(units) + 1):
                    if n < len(units):
                        first(n)
                    if n >= 1:
                        second(n - 1)
                if not gated:
                    for t in range(NT):
                        u = 4 * len(units) + t
                        pe.wait_ge(y_added, u - 1)
                        nc.tensor.matmul(down[u % 2][:, 0:E], m.weT[:, t * P:(t + 1) * P], m.b2[:, :],
                                         start=True, stop=True).then_inc(y_ready, 1)

            @block.scalar
            def _(act):
                if not gated:
                    nc.scalar.preload_act_table_set(TABLE_SET)

                def split_weights(e):
                    act.wait_ge(w_in, 16 * n_w * (e + 1))
                    if e >= 2:
                        act.wait_ge(y_ready, 4 * CH * (e - 1))
                    nc.scalar.activation(wslot.hi[:, e % 2, :], wfull[:, :], ACT.Copy).then_inc(w_high, 1)

                def high_part(u):
                    act.wait_ge(hid_done, u + 1)
                    n, i = u // HT, u % HT
                    if n >= 2:
                        act.wait_ge(y_ready, 4 * (n - 1))
                    nc.scalar.activation(hT.hi[:, n % 2, i, :], hid_t[:, u % 3, :], ACT.Copy).then_inc(h_high, 1)
                split_weights(0)
                for n, (e, c) in enumerate(units):
                    for i in range(HT):
                        u = n * HT + i
                        act.wait_ge(first_ready, u + 1)
                        if gated:
                            if u >= 3:
                                act.wait_ge(hid_done, u - 2)
                            nc.scalar.activation(act_t[:, u % 3, :], gate[u % 3][:, :], ACT.Silu).then_inc(act_done, 1)
                        else:
                            if u >= 3:
                                act.wait_ge(h_done, u - 2)
                            nc.scalar.activation(hid_t[:, u % 3, :], up[u % 3][:, :], ACT.Relu,
                                                 bias=m.b1[:, e * HT + i:e * HT + i + 1]).then_inc(hid_done, 1)
                        if u >= 1:
                            high_part(u - 1)
                        if c == CH - 1 and i == 0 and e + 1 < len(experts):
                            split_weights(e + 1)
                high_part(len(units) * HT - 1)

            @block.vector
            def _(dve):
                def low_weights(e):
                    dve.wait_ge(w_high, e + 1)
                    nc.vector.tensor_tensor(wslot.lo[:, e % 2, :], wfull[:, :], wslot.hi[:, e % 2, :].bitcast(FP32),
                                            ALU.subtract).then_inc(w_low, 1)

                def low_part(u):
                    n, i = u // HT, u % HT
                    dve.wait_ge(h_high, u + 1)
                    nc.vector.tensor_tensor(hT.lo[:, n % 2, i, :], hid_t[:, u % 3, :],
                                            hT.hi[:, n % 2, i, :].bitcast(FP32), ALU.subtract).then_inc(h_done, 1)

                def residual(n):
                    e, c = units[n]
                    column = experts[e][-1]
                    for t in range(4):
                        x = R.x[:, 4 * c + t, :]
                        u = 4 * n + t
                        dve.wait_ge(y_ready, u + 1)
                        if column is None:
                            nc.vector.tensor_tensor(x, down[u % 2][:, 0:E], x, ALU.add).then_inc(y_added, 1)
                        else:
                            nc.vector.scalar_tensor_tensor(out=x, in0=down[u % 2][:, 0:E],
                                                           scalar=m.we[:, 4 * c + t, column:column + 1], in1=x,
                                                           op0=ALU.mult, op1=ALU.add).then_inc(y_added, 1)
                low_weights(0)
                for n in range(len(units) + 1):
                    if n < len(units):
                        for i in range(HT):
                            u = n * HT + i
                            if gated:
                                dve.wait_ge(act_done, u + 1)
                                if u >= 3:
                                    dve.wait_ge(h_done, u - 2)
                                nc.vector.tensor_tensor(hid_t[:, u % 3, :], act_t[:, u % 3, :], up[u % 3][:, :], ALU.mult)\
                                    .then_inc(hid_done, 1)
                            if u >= 1:
                                low_part(u - 1)
                            e, c = units[n]
                            if c == CH - 1 and i == 1 and e + 1 < len(experts):
                                low_weights(e + 1)
                            if i == HT // 2 and n >= 1:
                                residual(n - 1)
                    else:
                        low_part(n * HT - 1)
                        residual(n - 1)
                if not gated:
                    for t in range(NT):
                        u = 4 * len(units) + t
                        dve.wait_ge(y_ready, u + 1)
                        dve.wait_ge(y_added, u)
                        nc.vector.tensor_tensor(R.x[:, t, :], down[u % 2][:, 0:E], R.x[:, t, :], ALU.add).then_inc(y_added, 1)


def experts_top2(nc, A, R):
    with ExitStack() as ctx:
        m = Resident()
        m.we = ctx.enter_context(nc.sbuf_tensor("f_we", [P, NT, 8], FP32))
        full = ctx.enter_context(nc.sbuf_tensor("f_gate_w", [P, KE, 8], FP32))
        gate_w = Pair(*(ctx.enter_context(nc.sbuf_tensor(f"f_gate_{n}", [P, KE, 8], FP32R)) for n in "hl"))
        stage_norm(nc, R, "fn", [(full[:, :, :], A["L0_ffn_gate_w"].rearrange("(k p) n -> p k n", p=P))],
                   splits=[(full[:, :, :], gate_w[:, :, :])])
        with stage(nc, "fr") as s:
            with nc.Block() as block:
                route_top2(nc, R, s, m, gate_w, block)
        experts = [(A["L0_ffn_ws_gate"], A["L0_ffn_ws_up"], A["L0_ffn_ws_down"], None)]
        experts += [(A["L0_ffn_w_gate"][e], A["L0_ffn_w_up"][e], A["L0_ffn_w_down"][e], e) for e in range(8)]
        stage_experts(nc, R, m, "fe", experts, 512, True)


def experts_hash(nc, A, R):
    with ExitStack() as ctx:
        m = Resident()

        def sb(name, shape):
            return ctx.enter_context(nc.sbuf_tensor(f"g_{name}", shape, FP32))
        n_e, hid = A["L1_ffn_b1"].shape
        m.we, m.weT = sb("we", [P, NT, 8]), sb("weT", [8, N])
        m.b1_rows, m.b1, m.b2 = sb("b1_rows", [n_e * hid // P, P]), sb("b1", [P, n_e * hid // P]), sb("b2", [n_e, E])
        stage_norm(nc, R, "gn", [(m.b1_rows[:, :], A["L1_ffn_b1"].rearrange("e (m p) -> (e m) p", p=P)),
                                 (m.b2[:, :], A["L1_ffn_b2"])])
        with stage(nc, "gr") as s:
            with nc.Block() as block:
                route_hash(nc, R, s, m, block)
        stage_experts(nc, R, m, "ge", [(A["L1_ffn_W1"][e], A["L1_ffn_W2"][e], e) for e in range(n_e)], hid, False)


class Resident:
    pass


def build(nc, A, out, upto=None):
    with ExitStack() as ctx:
        def sb(name, shape, dt=FP32):
            return ctx.enter_context(nc.sbuf_tensor(name, shape, dt))
        R = Resident()
        R.x = sb("x", [P, NT, E])
        R.xn = sb("xn", [P, NT, E])
        R.xnT = Pair(sb("xnT_h", [P, KE, N], FP32R), sb("xnT_l", [P, KE, N], FP32R))
        R.ident = sb("ident", [P, P])
        R.ident_b = sb("ident_b", [P, P], BF16)
        R.window = sb("window", [P, 2, 2 * P], BF16)
        R.ones_row = sb("ones_row", [1, P])
        R.yat_one = sb("yat_one", [P, 1])
        R.rope = sb("rope_t", [P, 2, ST, D])
        stored = ctx.enter_context(nc.semaphore("out_stored"))
        a = lambda p, names: [A[f"{p}_{n}"] for n in names]
        wqkv = A["L1_attn_Wqkv"]
        parts = [
            lambda: attention16(nc, A, R, "ya", "yat", *a("L0_attn", ("Wq", "Wk", "Wv", "Wo", "bq", "bk", "bv", "bo"))),
            lambda: attention16(nc, A, R, "xa", "cross",
                                *a("L0_xattn", ("Wq", "Wk", "Wv", "Wo", "bq", "bk", "bv", "bo"))),
            lambda: experts_top2(nc, A, R),
            lambda: attention16(nc, A, R, "wa", "rope", *(wqkv[:, i * E:(i + 1) * E] for i in range(3)),
                                A["L1_attn_Wout"]),
            lambda: attention_wide(nc, A, R),
        ]
        with ExitStack() as ctx_tiles:
            R.ctxT = Pair(*(ctx_tiles.enter_context(nc.sbuf_tensor(f"ctxT_{n}", [P, KE, B * CTX], FP32R)) for n in "hl"))
            stage_setup(nc, A, R)
            for i, part in enumerate(parts):
                if upto is None or i in upto:
                    part()
        if upto is None or len(parts) in upto:
            experts_hash(nc, A, R)
        with stage(nc, "store") as s:
            with nc.Block() as block:
                @block.sync
                def _(sp):
                    sp.dma_start(out.rearrange("b (t p) e -> p (b t) e", p=P), R.x[:, :, :]).then_inc(stored, 16)
                    sp.wait_ge(stored, 16)


_INS = ["x", "ctx_1024", "L0_attn_Wq", "L0_attn_bq", "L0_attn_Wk", "L0_attn_bk", "L0_attn_Wv", "L0_attn_bv",
        "L0_attn_Wo", "L0_attn_bo", "L0_xattn_Wq", "L0_xattn_bq", "L0_xattn_Wk", "L0_xattn_bk", "L0_xattn_Wv",
        "L0_xattn_bv", "L0_xattn_Wo", "L0_xattn_bo", "L0_ffn_gate_w", "L0_ffn_w_gate", "L0_ffn_w_up",
        "L0_ffn_w_down", "L0_ffn_ws_gate", "L0_ffn_ws_up", "L0_ffn_ws_down", "L1_attn_Wqkv", "L1_attn_Wout",
        "L1_xattn_Wq", "L1_xattn_Wk", "L1_xattn_Wv", "L1_xattn_Wo", "L1_xattn_bo", "L1_ffn_W1", "L1_ffn_b1",
        "L1_ffn_W2", "L1_ffn_b2", "rope"]


def shape_constants():
    half = D // 2
    theta = (1.0 / np.float32(10000.0) ** (np.arange(half, dtype=np.float32) / np.float32(half))).astype(np.float32)
    freqs = np.arange(S, dtype=np.float32)[:, None] * theta[None, :]
    cos, sin = np.cos(freqs), np.sin(freqs)
    return {"rope": np.stack([np.concatenate([cos, cos], 1), np.concatenate([-sin, sin], 1)]).astype(np.float32)}


def kernel(**inputs):
    import concourse.bacc as bacc
    from concourse.bass_utils import run_bass_kernel_spmd

    nc = bacc.Bacc("TRN2", target_bir_lowering=False, num_devices=1)
    arrays, patterns = {}, {}
    for name, value in {**inputs, **shape_constants()}.items():
        value = np.ascontiguousarray(value)
        arrays[f"in_{name}"] = value
        patterns[name] = nc.dram_tensor(f"in_{name}", value.shape, mybir.dt.from_np(value.dtype), kind="ExternalInput").ap()
    out = nc.dram_tensor("out", (B, S, E), FP32, kind="ExternalOutput").ap()
    build(nc, patterns, out)
    return run_bass_kernel_spmd(nc, [arrays], core_ids=[0]).results[0]["out"]
```

```python
import numpy as np
from contextlib import ExitStack, contextmanager

import concourse.bass as bass
from concourse import mybir

FP32 = mybir.dt.float32
BF16 = mybir.dt.bfloat16
FP32R = mybir.dt.float32r
I32 = mybir.dt.int32
U32 = mybir.dt.uint32
ALU = mybir.AluOpType
ACT = mybir.ActivationFunctionType
AX = mybir.AxisListType

P = 128
B, S, E = 2, 512, 256
CTX = 1024
N = B * S
NT = N // P
ST = S // P
CT = CTX // P
KE = E // P
H, D = 16, 16
G = H // 4
VW = 32
PARTS = 3
Q_ROWS = (0, 0, 0, 1, 1, 2)
K_ROWS = (0, 1, 2, 0, 1, 0)
ROWS = D * len(Q_ROWS)
MAX_ROWS = 2
H1, D1 = 8, 64
LN_EPS = 1e-5
YAT_EPS = 0.1
NEG = -1e30
TABLE_SET = "natural_log_exp_and_others"


class Scope:

    def __init__(self, nc, ctx, sem_ctx, tag):
        self.nc, self.ctx, self.sem_ctx, self.tag, self.sems = nc, ctx, sem_ctx, tag, []

    def sb(self, name, shape, dt=FP32):
        return self.ctx.enter_context(self.nc.sbuf_tensor(f"{self.tag}_{name}", shape, dt))

    def ps(self, name, shape=(P, 512), dt=FP32):
        return self.ctx.enter_context(self.nc.psum_tensor(f"{self.tag}_{name}", list(shape), dt))

    def sem(self, name):
        s = self.sem_ctx.enter_context(self.nc.semaphore(f"{self.tag}_{name}"))
        self.sems.append(s)
        return s


class Stages:

    def __init__(self):
        self.sems, self.held = [], ExitStack()


@contextmanager
def stage(nc, R, tag):
    with ExitStack() as ctx:
        sem_ctx = ExitStack()
        s = Scope(nc, ctx, sem_ctx, tag)
        for sem in R.stages.sems:
            nc.gpsimd.sem_clear(sem)
        yield s
        R.stages.held.close()
        R.stages.sems, R.stages.held = s.sems, sem_ctx


class Pair:

    def __init__(self, hi, lo):
        self.hi, self.lo = hi, lo

    def __getitem__(self, key):
        return Pair(self.hi[key], self.lo[key])

    def rearrange(self, *a, **k):
        return Pair(self.hi.rearrange(*a, **k), self.lo.rearrange(*a, **k))


def matmul3(nc, out, a, b, start, stop):
    nc.tensor.matmul(out, a.hi, b.hi, start=start, stop=False)
    nc.tensor.matmul(out, a.hi, b.lo, start=False, stop=False)
    return nc.tensor.matmul(out, a.lo, b.hi, start=False, stop=stop)


def chain_of(engine, sem):
    n = [0]

    def link(ins):
        n[0] += 1
        ins.then_inc(sem, 1)
        engine.wait_ge(sem, n[0])
    return link


def setup_work(nc, A, R, s):
    ctx_tok = s.sb("ctx_tok", [P, B * CT, E])
    tp = [s.ps(f"ctx_tp{i}") for i in range(4)]
    x_in, ctx_in, w_in = s.sem("x_in"), [s.sem(f"ctx_in{b}") for b in range(B)], s.sem("w_in")
    ident_step, ident_ready = s.sem("ident_step"), s.sem("ident_ready")
    transposed, evacuated = s.sem("ctx_transposed"), s.sem("ctx_evacuated")
    made, high_done = s.sem("made"), s.sem("ctx_high")
    banks = [(b, k, q) for b in range(B) for q in range(CT // 4) for k in range(KE)]

    def sync_before(sp):
        sp.dma_start(R.x[:, :, :], A["x"].rearrange("b (t p) e -> p (b t) e", p=P)).then_inc(x_in, 16)
        sp.dma_start(R.rope[:, :, :, :], A["rope"].rearrange("c (t p) d -> p c t d", p=P)).then_inc(w_in, 16)

    def sync_behind(sp):
        for b in range(B):
            sp.dma_start(ctx_tok[:, b * CT:(b + 1) * CT, :],
                         A["ctx_1024"][b].rearrange("(t p) e -> p t e", p=P)).then_inc(ctx_in[b], 16)
        sp.wait_ge(w_in, 16)

    def gpsimd_before(pool):
        nc.gpsimd.memset(R.ident[:, :], 0.0).then_inc(ident_step, 1)
        nc.gpsimd.memset(R.ones_row[:, :], 1.0).then_inc(made, 1)
        nc.gpsimd.memset(R.yat_one[:, :], 1.0 + YAT_EPS).then_inc(made, 1)
        nc.gpsimd.memset(R.window[:, :, :], 0.0).then_inc(ident_step, 1)
        pool.wait_ge(ident_step, 1)
        nc.gpsimd.affine_select(out=R.ident[:, :], in_=R.ident[:, :], compare_op=ALU.not_equal, fill=1.0,
                                base=0, pattern=[[-1, P]], channel_multiplier=1).then_inc(ident_ready, 1)
        pool.wait_ge(ident_step, 2)
        nc.gpsimd.affine_select(out=R.window[:, 0, 0:P], in_=R.window[:, 0, 0:P], compare_op=ALU.is_ge,
                                fill=NEG, base=0, pattern=[[1, P]], channel_multiplier=-1).then_inc(made, 1)
        nc.gpsimd.affine_select(out=R.window[:, 0, P:2 * P], in_=R.window[:, 0, P:2 * P],
                                compare_op=ALU.is_gt, fill=NEG, base=0, pattern=[[-1, P]],
                                channel_multiplier=1).then_inc(made, 1)
        nc.gpsimd.affine_select(out=R.window[:, 1, 0:P], in_=R.window[:, 1, 0:P], compare_op=ALU.is_gt,
                                fill=NEG, base=0, pattern=[[1, P]], channel_multiplier=-1).then_inc(made, 1)
        nc.gpsimd.affine_select(out=R.window[:, 1, P:2 * P], in_=R.window[:, 1, P:2 * P],
                                compare_op=ALU.is_ge, fill=NEG, base=0, pattern=[[-1, P]],
                                channel_multiplier=1).then_inc(made, 1)
        pool.wait_ge(ident_ready, 1)
        nc.gpsimd.tensor_copy(R.ident_b[:, :], R.ident[:, :]).then_inc(made, 1)

    def vector_before(dve):
        dve.wait_ge(x_in, 16)

    def scalar_before(act):
        act.wait_ge(x_in, 16)

    def tensor_before(pe):
        pe.wait_ge(ident_ready, 1)

    def tensor_behind(pe):
        for n, (b, k, q) in enumerate(banks):
            pe.wait_ge(ctx_in[b], 16)
            if n >= 4:
                pe.wait_ge(evacuated, n - 3)
            for i in range(4):
                last = nc.tensor.transpose(tp[n % 4][:, i * P:(i + 1) * P],
                                           ctx_tok[:, b * CT + 4 * q + i, k * P:(k + 1) * P], R.ident[:, :])
            last.then_inc(transposed, 1)

    def vector_behind(dve):
        for n, (b, k, q) in enumerate(banks):
            dve.wait_ge(high_done, n + 1)
            part = R.ctxT[:, k, b * CTX + q * 512:b * CTX + (q + 1) * 512]
            nc.vector.tensor_tensor(part.lo, tp[n % 4][:, :], part.hi.bitcast(FP32), ALU.subtract)\
                .then_inc(evacuated, 1)

    def scalar_behind(act):
        for n, (b, k, q) in enumerate(banks):
            act.wait_ge(transposed, n + 1)
            nc.scalar.activation(R.ctxT[:, k, b * CTX + q * 512:b * CTX + (q + 1) * 512].hi,
                                 tp[n % 4][:, :], ACT.Copy).then_inc(high_done, 1)
    before = {"sync": sync_before, "gpsimd": gpsimd_before, "vector": vector_before, "scalar": scalar_before,
              "tensor": tensor_before}
    behind = {"sync": sync_behind, "vector": vector_behind, "scalar": scalar_behind, "tensor": tensor_behind}
    return before, behind


def stage_norm(nc, R, tag, loads=(), padded=None, splits=(), ahead=(), setup=None):
    with stage(nc, R, tag) as s:
        stats = s.sb("stats", [P, NT, 6])
        mv = s.sb("mv", [P, NT, 2])
        ve, lnv, r, a, nb = (s.sb(n, [P, NT]) for n in ("ve", "lnv", "r", "a", "nb"))
        tp = [s.ps(f"tp{i}") for i in range(4)]
        step, var_ready, rs_step, rs_ready = s.sem("step"), s.sem("var"), s.sem("rs_step"), s.sem("rs")
        normed, transposed, high_done, evac = s.sem("normed"), s.sem("transposed"), s.sem("high_done"), s.sem("evac")
        w_high, w_low = s.sem("w_high"), s.sem("w_low")
        weights_in, zeroed = s.sem("weights_in"), s.sem("zeroed")
        to_split = s.sem("to_split")
        n_split = min(3, len(loads)) if splits else 0
        scale_ready, normed_odd = s.sem("scale_ready"), s.sem("normed_odd")
        banks = [(k, q) for q in range(NT // 4) for k in range(KE)]
        before, behind = setup(s) if setup else ({}, {})
        nothing = lambda engine: None
        with nc.Block() as block:

            @block.gpsimd
            def _(pool):
                before.get("gpsimd", nothing)(pool)
                if padded is not None:
                    nc.gpsimd.memset(padded[:, :, :], 0.0).then_inc(zeroed, 1)

            @block.sync
            def _(sp):
                before.get("sync", nothing)(sp)
                for dst, src in loads[:n_split]:
                    sp.dma_start(dst, src).then_inc(to_split, 16)
                if padded is not None:
                    sp.wait_ge(zeroed, 1)
                for dst, src in loads[n_split:]:
                    sp.dma_start(dst, src, allow_slow_non_contiguous=True).then_inc(weights_in, 16)
                behind.get("sync", nothing)(sp)
                for dst, src, sem in ahead:
                    sp.dma_start(dst, src).then_inc(sem, 16)
                if len(loads) > n_split:
                    sp.wait_ge(weights_in, 16 * (len(loads) - n_split))

            @block.vector
            def _(dve):
                before.get("vector", nothing)(dve)
                link = chain_of(dve, step)
                for t in range(NT):
                    ins = nc.vector.bn_stats(stats[:, t, :], R.x[:, t, :])
                link(ins)
                for t in range(NT):
                    ins = nc.vector.bn_aggr(mv[:, t, :], stats[:, t, :])
                link(ins)
                nc.vector.tensor_scalar_add(ve[:, :], mv[:, :, 1], LN_EPS).then_inc(var_ready, 1)
                dve.wait_ge(rs_ready, 1)
                dve.wait_ge(var_ready, 1)
                link(nc.vector.tensor_tensor(a[:, :], r[:, :], r[:, :], ALU.mult))
                link(nc.vector.tensor_tensor(a[:, :], a[:, :], ve[:, :], ALU.mult))
                link(nc.vector.tensor_scalar(a[:, :], a[:, :], -0.5, 1.5, ALU.mult, ALU.add))
                link(nc.vector.tensor_tensor(r[:, :], r[:, :], a[:, :], ALU.mult))
                nc.vector.scalar_tensor_tensor(out=nb[:, :], in0=mv[:, :, 0], scalar=-1.0, in1=r[:, :],
                                               op0=ALU.mult, op1=ALU.mult).then_inc(scale_ready, 1)
                dve.wait_ge(scale_ready, 1)
                for t in range(0, NT, 2):
                    nc.vector.tensor_scalar(R.xn[:, t, :], R.x[:, t, :], r[:, t:t + 1], nb[:, t:t + 1],
                                            ALU.mult, ALU.add).then_inc(normed, 1)
                for i, (full, part) in enumerate(splits):
                    dve.wait_ge(w_high, i + 1)
                    nc.vector.tensor_tensor(part.lo, full, part.hi.bitcast(FP32), ALU.subtract).then_inc(w_low, 1)
                for n, (k, q) in enumerate(banks):
                    dve.wait_ge(high_done, n + 1)
                    part = R.xnT[:, k, q * 512:(q + 1) * 512]
                    nc.vector.tensor_tensor(part.lo, tp[n][:, :], part.hi.bitcast(FP32), ALU.subtract).then_inc(evac, 1)
                behind.get("vector", nothing)(dve)

            @block.scalar
            def _(act):
                nc.scalar.preload_act_table_set(TABLE_SET)
                before.get("scalar", nothing)(act)
                act.wait_ge(var_ready, 1)
                nc.scalar.activation(lnv[:, :], ve[:, :], ACT.Ln).then_inc(rs_step, 1)
                act.wait_ge(rs_step, 1)
                nc.scalar.activation(r[:, :], lnv[:, :], ACT.Exp, scale=-0.5).then_inc(rs_ready, 1)
                act.wait_ge(scale_ready, 1)
                for t in range(1, NT, 2):
                    nc.scalar.activation(R.xn[:, t, :], R.x[:, t, :], ACT.Identity, scale=r[:, t:t + 1],
                                         bias=nb[:, t:t + 1]).then_inc(normed_odd, 1)
                if splits:
                    act.wait_ge(to_split, 16 * n_split)
                for full, part in splits:
                    nc.scalar.activation(part.hi, full, ACT.Copy).then_inc(w_high, 1)
                for n, (k, q) in enumerate(banks):
                    act.wait_ge(transposed, n + 1)
                    nc.scalar.activation(R.xnT[:, k, q * 512:(q + 1) * 512].hi, tp[n][:, :], ACT.Copy)\
                        .then_inc(high_done, 1)
                behind.get("scalar", nothing)(act)

            @block.tensor
            def _(pe):
                before.get("tensor", nothing)(pe)
                for n, (k, q) in enumerate(banks):
                    for i in range(4):
                        t = 4 * q + i
                        pe.wait_ge(normed_odd if t % 2 else normed, t // 2 + 1)
                        last = nc.tensor.transpose(tp[n][:, i * P:(i + 1) * P],
                                                   R.xn[:, 4 * q + i, k * P:(k + 1) * P], R.ident[:, :])
                    last.then_inc(transposed, 1)
                behind.get("tensor", nothing)(pe)


def stage_project(nc, R, tag, m, kind, wq, wk, wv, bq=None, bk=None, bv=None):
    cross = kind == "cross"
    src, kt_n = (R.ctxT, CT) if cross else (R.xnT, ST)
    keys = kt_n * P
    chunks = [(b, w, k, c) for b in range(B) for w, n in (("q", 1), ("k", keys // 512)) for k in range(KE)
              for c in range(n)]
    n_tok = 0 if cross else 2 * NT
    n_v = B * kt_n // 2
    with stage(nc, R, f"{tag}p") as s:
        qc = s.sb("qc", [P, PARTS, B, KE, S], BF16)
        kc = s.sb("kc", [P, PARTS, B, KE, keys], BF16)
        rest = s.sb("rest", [P, 2, 512])
        feat = [s.ps(f"feat{i}") for i in range(4)]
        vps = [s.ps(f"v{i}") for i in range(2)]
        tok = [s.ps(f"tok{i}") for i in range(2)]
        if n_tok:
            qk = s.sb("qk", [P, n_tok, E])
            aux = s.sb("aux", [P, 4, E])
            ss, lns = s.sb("ss", [P, n_tok, H]), s.sb("lns", [P, n_tok, H])
        tok_mm, tok_evac, tok_ready = s.sem("tok_mm"), s.sem("tok_evac"), s.sem("tok_ready")
        aux_used, ss_ready, norm_step, norm_ready = (s.sem(n) for n in ("aux_used", "ss_ready", "norm_step", "norm_ready"))
        v_mm, v_evac = s.sem("v_mm"), s.sem("v_evac")
        feat_ready, high_ready, rest_ready, rest_used = (s.sem(n) for n in ("feat", "high", "rest", "rest_used"))
        dve_step, middle_ready, stored, reduced = (s.sem(n) for n in ("dve_step", "middle_ready", "stored", "reduced"))

        def part_of(chunk, part):
            b, which, k, c = chunk
            return qc[:, part, b, k, :] if which == "q" else kc[:, part, b, k, c * 512:(c + 1) * 512]

        with nc.Block() as block:

            @block.tensor
            def _(pe):
                for n in range(n_tok):
                    t, w = n // 2, (wq, wk)[n % 2]
                    if n >= 2:
                        pe.wait_ge(tok_evac, n - 1)
                    for k in range(KE):
                        last = matmul3(nc, tok[n % 2][:, 0:E], R.xnT[:, k, t * P:(t + 1) * P], w[:, k, :],
                                       start=k == 0, stop=k == KE - 1)
                    last.then_inc(tok_mm, 1)

                def value(n):
                    if n >= 2:
                        pe.wait_ge(v_evac, n - 1)
                    for i in range(2):
                        at = (2 * n + i) * P
                        for k in range(KE):
                            last = matmul3(nc, vps[n % 2][:, i * E:(i + 1) * E], src[:, k, at:at + P], wv[:, k, :],
                                           start=k == 0, stop=k == KE - 1)
                    last.then_inc(v_mm, 1)
                if not cross:
                    for n in range(n_v):
                        value(n)
                for n, (b, which, mt, c) in enumerate(chunks):
                    if n >= 4:
                        pe.wait_ge(rest_ready, n - 3)
                    if cross:
                        w, x, at = (wq, R.xnT, b * S) if which == "q" else (wk, src, b * CTX + c * 512)
                        for k in range(KE):
                            last = matmul3(nc, feat[n % 4][:, :], w[:, k, mt * P:(mt + 1) * P],
                                           x[:, k, at:at + 512], start=k == 0, stop=k == KE - 1)
                    else:
                        pe.wait_ge(tok_ready, 2 * ST * (b + 1))
                        for t in range(ST):
                            last = nc.tensor.transpose(feat[n % 4][:, t * P:(t + 1) * P],
                                                       qk[:, 2 * (b * ST + t) + (which == "k"), mt * P:(mt + 1) * P],
                                                       R.ident[:, :])
                    last.then_inc(feat_ready, 1)
                if cross:
                    for n in range(n_v):
                        value(n)

            @block.scalar
            def _(act):
                nc.scalar.preload_act_table_set(TABLE_SET)
                if kind == "yat":
                    act.wait_ge(ss_ready, 1)
                    nc.scalar.activation(lns[:, :, :], ss[:, :, :], ACT.Ln).then_inc(norm_step, 1)
                    act.wait_ge(norm_step, 1)
                    nc.scalar.activation(lns[:, :, :], lns[:, :, :], ACT.Exp, scale=0.5).then_inc(norm_ready, 1)
                for n, chunk in enumerate(chunks):
                    bias = {"q": bq, "k": bk}[chunk[1]] if cross else None
                    act.wait_ge(feat_ready, n + 1)
                    if bias is None:
                        nc.scalar.activation(part_of(chunk, 0), feat[n % 4][:, :], ACT.Copy).then_inc(high_ready, 1)
                    else:
                        nc.scalar.activation(part_of(chunk, 0), feat[n % 4][:, :], ACT.Identity,
                                             bias=bias[:, chunk[2]:chunk[2] + 1]).then_inc(high_ready, 1)

            @block.vector
            def _(dve):
                link = chain_of(dve, dve_step)
                heads = lambda ap: ap.rearrange("p (d h) -> p h d", d=D)

                def value(n):
                    dve.wait_ge(v_mm, n + 1)
                    out = m.vaug[:, 2 * n:2 * n + 2, :, 0:D]
                    ps = vps[n % 2][:, :].rearrange("p (i h d) -> p i h d", i=2, d=D)
                    for i in range(2):
                        if bv is not None:
                            ins = nc.vector.tensor_tensor(out[:, i], ps[:, i], bv[:, :].rearrange("p (h d) -> p h d", d=D), ALU.add)
                        else:
                            ins = nc.vector.tensor_copy(out[:, i], ps[:, i])
                    ins.then_inc(v_evac, 1)
                if kind == "yat":
                    for n in range(n_tok + 2):
                        if n < n_tok:
                            dve.wait_ge(tok_mm, n + 1)
                            nc.vector.tensor_tensor(heads(qk[:, n, :]), heads(tok[n % 2][:, 0:E]),
                                                    (bq, bk)[n % 2][:, :].rearrange("p (h d) -> p h d", d=D), ALU.add)\
                                .then_inc(tok_evac, 1)
                        if n >= 2:
                            dve.wait_ge(aux_used, n - 1)
                            nc.vector.tensor_reduce(out=ss[:, n - 2, :], in_=heads(aux[:, (n - 2) % 4, :]),
                                                    op=ALU.add, axis=AX.X).then_inc(reduced, 1)
                    dve.wait_ge(reduced, n_tok)
                    nc.vector.tensor_scalar_max(ss[:, :, :], ss[:, :, :], 1e-19).then_inc(ss_ready, 1)
                    for n in range(n_v):
                        value(n)
                    dve.wait_ge(norm_ready, 1)
                    link(nc.vector.tensor_scalar_add(lns[:, :, :], lns[:, :, :], 1e-8))
                    link(nc.vector.reciprocal(lns[:, :, :], lns[:, :, :]))
                    for n in range(n_tok):
                        nc.vector.tensor_tensor(heads(qk[:, n, :]), heads(qk[:, n, :]),
                                                lns[:, n, :].unsqueeze(2).broadcast_to([P, H, D]), ALU.mult)\
                            .then_inc(tok_ready, 1)
                if kind == "rope":
                    half = D // 2
                    for n in range(n_tok):
                        dve.wait_ge(tok_mm, n + 1)
                        if n >= 4:
                            dve.wait_ge(tok_ready, n - 3)
                        ps, a, r = heads(tok[n % 2][:, 0:E]), heads(qk[:, n, :]), heads(aux[:, n % 4, :])
                        t = n // 2 % ST
                        table = lambda c, lo, hi: R.rope[:, c, t, lo:hi].unsqueeze(1).broadcast_to([P, H, hi - lo])
                        nc.vector.tensor_tensor(a, ps, table(0, 0, D), ALU.mult)
                        nc.vector.tensor_tensor(r[:, :, 0:half], ps[:, :, half:D], table(1, 0, half), ALU.mult)
                        nc.vector.tensor_tensor(r[:, :, half:D], ps[:, :, 0:half], table(1, half, D), ALU.mult)\
                            .then_inc(tok_evac, 1)
                    for n in range(n_v):
                        value(n)
                for n, chunk in enumerate(chunks):
                    bias = {"q": bq, "k": bk}[chunk[1]] if cross else None
                    dve.wait_ge(high_ready, n + 1)
                    if n >= 2:
                        dve.wait_ge(rest_used, n - 1)
                    nc.vector.scalar_tensor_tensor(
                        out=rest[:, n % 2, :], in0=feat[n % 4][:, :],
                        scalar=0.0 if bias is None else bias[:, chunk[2]:chunk[2] + 1],
                        in1=part_of(chunk, 0), op0=ALU.add, op1=ALU.subtract).then_inc(rest_ready, 1)
                    dve.wait_ge(rest_ready, n + 1)
                    nc.vector.tensor_copy(part_of(chunk, 1), rest[:, n % 2, :]).then_inc(middle_ready, 1)
                if cross:
                    for n in range(n_v):
                        value(n)

            @block.gpsimd
            def _(pool):
                for n in range(n_tok):
                    pool.wait_ge(tok_evac, n + 1)
                    if kind == "yat":
                        if n >= 4:
                            pool.wait_ge(reduced, n - 3)
                        nc.gpsimd.tensor_tensor(aux[:, n % 4, :], qk[:, n, :], qk[:, n, :], ALU.mult).then_inc(aux_used, 1)
                    else:
                        nc.gpsimd.tensor_tensor(qk[:, n, :], qk[:, n, :], aux[:, n % 4, :], ALU.add).then_inc(tok_ready, 1)
                for n, chunk in enumerate(chunks):
                    pool.wait_ge(middle_ready, n + 1)
                    nc.gpsimd.tensor_tensor(part_of(chunk, 2), rest[:, n % 2, :], part_of(chunk, 1), ALU.subtract)\
                        .then_inc(rest_used, 1)

            @block.sync
            def _(sp):
                done = n_dma = 0
                for b in range(B):
                    for which, comp, scratch, n in (("q", qc, m.q_dram[b], 1), ("k", kc, m.k_dram[b], keys // 512)):
                        for k in range(KE):
                            done += n
                            sp.wait_ge(rest_used, done)
                            sp.dma_start(scratch[:, k * D // KE:(k + 1) * D // KE, :, :].rearrange("c d h t -> (d h) c t"),
                                         comp[:, :, b, k, :]).then_inc(stored, 16)
                            n_dma += 1
                        if b == 1 and which == "q":
                            sp.wait_ge(stored, 16 * n_dma)
                            load_stacks(sp, m, 0)
                sp.wait_ge(stored, 16 * n_dma)


def load_stacks(sp, m, gr, which="qk"):
    b, g = divmod(gr, G)
    for dram, stack in [(m.q_dram[b], m.qst)] * ("q" in which) + [(m.k_dram[b], m.kst)] * ("k" in which):
        at = 0
        for n, part in ((3, 0), (2, 1), (1, 2)):
            src = dram[0:n, :, 4 * g:4 * g + 4, :] if stack is m.kst else \
                dram[part:part + 1, :, 4 * g:4 * g + 4, :].broadcast_to([n, D, 4, dram.shape[3]])
            sp.dma_start(stack[at:at + D * n, 4 * g:4 * g + 4, :], src).then_inc(m.stack_in[g], 16)
            at += D * n


def stage_attend(nc, R, tag, m, kind, w_out, b_out):
    yat, window = kind == "yat", kind == "rope"
    kt_n = CT if kind == "cross" else ST
    GR = B * G
    QPG = 1 if window else kt_n // 2
    UPG = 4 * QPG
    units = GR * UPG
    cols = 7 * P if window else 1024
    rows = ROWS if yat else ROWS + MAX_ROWS
    PR = 8
    NS, NA = (3, 2) if yat else (2, 1)
    AHEAD = 2 if window else 1
    MU = 8 if window else 32
    LAG = 6 if yat else 4
    base = [2 * P * t for t in range(ST)]
    width = [2 * P] * (ST - 1) + [P]
    loads_per_group = 2 * PARTS
    with stage(nc, R, f"{tag}a") as s:
        s.sems += m.stack_in
        qst, kst = m.qst, m.kst
        probs = s.sb("probs", [P, PR, 1024])
        lnb = s.sb("lnb", [P, 3, 1024]) if yat else None
        den, rec, accs = (s.sb(n, [P, 2, 512]) for n in ("den", "rec", "accs"))
        sc = [s.ps(f"sc{i}", [P, 1024]) for i in range(NS)]
        acc = [s.ps(f"acc{i}") for i in range(NA)]
        if not yat:
            side_ps = [s.ps(f"side{i}") for i in range(3)]
            mx = s.sb("mx", [P, 2, ST, 4, 2])
            mxm = s.sb("mxm", [P, 2, ST, 4])
            neg = s.sb("neg", [4, MAX_ROWS, S], BF16)
        scores_ready, probs_ready, pv_done = s.sem("scores_ready"), s.sem("probs_ready"), s.sem("pv_done")
        squared, pool_probs = s.sem("squared"), s.sem("pool_probs")
        divided, biased, pool_step = s.sem("divided"), s.sem("biased"), s.sem("pool_step")
        ln_done, rec_done, once_done, ones = s.sem("ln_done"), s.sem("rec_done"), s.sem("once_done"), s.sem("ones")
        den_ready, den_ln, den_rec, step, acc_free = (s.sem(n) for n in (
            "den_ready", "den_ln", "den_rec", "step", "acc_free"))
        side_mm, side_done, max_done, neg_step = (s.sem(n) for n in ("side_mm", "side_done", "max_done", "neg_step"))
        placed = [s.sem(f"placed{i}") for i in range(2)]

        def on_pool(u):
            return yat and u % 4 == 3

        def ready(n):
            return (n - n // 4, n // 4) if yat else (n, 0)

        def after(u):
            g = u // UPG - 1
            return g if g >= 0 and u % UPG == min(6 if yat else 4, UPG - 1) else None

        def side_tasks(u):
            g, i = u // UPG + AHEAD, u % UPG
            if yat or u >= units:
                return []
            over = 4 if window else 12
            mus = range(MU * min(i, over) // over, MU * min(i + 1, over) // over) if g < GR else []
            rows_g = g - 1 if window else g
            rows_due = AHEAD <= rows_g < GR and i == (1 if window else 12)
            out = [t for t in range(ST) if u == ((G + 2) * UPG + t if window else G * UPG + 12 + t)]
            return [("max", g, k) for k in mus] + ([("rows", rows_g, 0)] if rows_due else []) + [
                ("out", 0, t) for t in out]

        before = [] if yat else [("max", g, k) for g in range(AHEAD) for k in range(MU)] + [
            ("rows", g, 0) for g in range(AHEAD)]
        order = before + [task for u in range(units) for task in side_tasks(u)]
        number = {task: n for n, task in enumerate(order)}

        with nc.Block() as block:

            @block.sync
            def _(sp):
                def load(gr):
                    sp.wait_ge(scores_ready, UPG * (gr - G + 1))
                    load_stacks(sp, m, gr)

                def place(gr):
                    g = gr % G
                    sp.wait_ge(side_done, number["rows", gr, 0] + 1)
                    if gr >= G:
                        sp.wait_ge(scores_ready, UPG * (gr - G + 1))
                    for i in range(MAX_ROWS):
                        sp.dma_start(qst[ROWS + i:ROWS + i + 1, 4 * g:4 * g + 4, :], neg[:, i, :])\
                            .then_inc(placed[gr % 2], 16)
                for gr in range(1, G):
                    load_stacks(sp, m, gr)
                if not yat:
                    for gr in range(AHEAD):
                        place(gr)
                for gr in range(GR):
                    if not yat and not window and gr + AHEAD < GR:
                        place(gr + AHEAD)
                    if gr + G < GR:
                        load(gr + G)
                    if window and gr + AHEAD < GR:
                        place(gr + AHEAD)

            @block.gpsimd
            def _(pool):
                link = chain_of(pool, pool_step)
                nc.gpsimd.memset(m.vaug[:, :, :, D:VW], 1.0).then_inc(ones, 1)
                if not yat:
                    pool.wait_ge(ones, 1)
                    nc.gpsimd.memset(kst[ROWS:ROWS + MAX_ROWS, :, :], 1.0).then_inc(ones, 1)
                if b_out is not None:
                    pool.wait_ge(ones, 1 if yat else 2)
                    for t in range(NT):
                        nc.gpsimd.tensor_tensor(R.x[:, t, :], R.x[:, t, :], b_out[:, :], ALU.add).then_inc(biased, 1)
                        pool.wait_ge(biased, t + 1)
                for gr in range(0 if yat else GR):
                    a, d, r = accs[:, gr % 2, :], den[:, gr % 2, :], rec[:, gr % 2, :]
                    pool.wait_ge(den_rec, gr + 1)
                    link(nc.gpsimd.tensor_tensor(d, d, r, ALU.mult))
                    link(nc.gpsimd.tensor_scalar(d, d, -1.0, 2.0, ALU.mult, ALU.add))
                    link(nc.gpsimd.tensor_tensor(d, d, r, ALU.mult))
                    nc.gpsimd.tensor_tensor(m.outT[gr // G][:, gr % G, :], a, d, ALU.mult).then_inc(divided, 1)
                    pool.wait_ge(divided, gr + 1)
                for u in range(units):
                    if on_pool(u):
                        pool.wait_ge(squared, ready(u + 1)[1])
                        pool.wait_ge(rec_done, u + 1)
                        nc.gpsimd.tensor_tensor(probs[:, u % PR, :], probs[:, u % PR, :], lnb[:, u % 3, :], ALU.mult)\
                            .then_inc(pool_probs, 1)

            @block.tensor
            def _(pe):
                def stacks(gr):
                    pe.wait_ge(m.stack_in[gr % G], 16 * loads_per_group * (gr // G + 1))

                def side(n):
                    kind, gr, i = order[n]
                    ps = side_ps[n % 3]
                    if n >= 3:
                        pe.wait_ge(side_done, n - 2)
                    if kind == "out":
                        pe.wait_ge(divided, G)
                        for g in range(G):
                            last = nc.tensor.matmul(ps[:, 0:E], m.outT[0][:, g, i * P:(i + 1) * P], w_out[:, g, :],
                                                    start=g == 0, stop=g == G - 1)
                        last.then_inc(side_mm, 1)
                        return
                    if kind == "rows":
                        pe.wait_ge(max_done, gr + 1)
                        for t in range(ST):
                            last = nc.tensor.transpose(ps[0:4, t * P:(t + 1) * P], mxm[:, gr % 2, t, :], R.ident[:, :])
                        last.then_inc(side_mm, 1)
                        return
                    if i == 0:
                        stacks(gr)
                    if window:
                        h, half = 4 * (gr % G) + i // 2, i % 2
                        for t in (2 * half, 2 * half + 1):
                            lo = 0 if t else P
                            out = ps[:, 2 * P * (t % 2) + lo:2 * P * (t % 2 + 1)]
                            nc.tensor.matmul(out, R.ident_b[:, :], R.window[:, 1, lo:], start=True, stop=False)
                            last = nc.tensor.matmul(out, qst[0:ROWS, h, t * P:(t + 1) * P],
                                                    kst[0:ROWS, h, (t - 1) * P + lo:(t + 1) * P],
                                                    start=False, stop=True)
                    else:
                        h, qt, half = 4 * (gr % G) + i // 8, i // 2 % 4, i % 2
                        last = nc.tensor.matmul(ps[:, :], qst[0:ROWS, h, qt * P:(qt + 1) * P],
                                                kst[0:ROWS, h, half * 512:(half + 1) * 512], start=True, stop=True)
                    last.then_inc(side_mm, 1)

                def scores(u, half):
                    gr, kp = u // UPG, u % UPG // 4
                    h, ps = 4 * (gr % G) + u % 4, sc[u % NS]
                    if u % UPG == 0 and half == 0:
                        stacks(gr)
                        if not yat:
                            pe.wait_ge(placed[gr % 2], 16 * MAX_ROWS * (gr // 2 + 1))
                            pe.wait_ge(ones, 2)
                    if u >= NS and half == 0:
                        if on_pool(u - NS):
                            pe.wait_ge(squared, ready(u - NS + 1)[1])
                        else:
                            pe.wait_ge(probs_ready, ready(u - NS + 1)[0])
                    if window:
                        for t in (2 * half, 2 * half + 1):
                            out = ps[:, base[t]:base[t] + width[t]]
                            nc.tensor.matmul(out, R.ident_b[:, :], R.window[:, 0, 0:width[t]], start=True, stop=False)
                            last = nc.tensor.matmul(out, kst[0:rows, h, t * P:(t + 1) * P],
                                                    qst[0:rows, h, t * P:t * P + width[t]], start=False, stop=True)
                    else:
                        kt = 2 * kp + half
                        last = nc.tensor.matmul(ps[:, half * 512:(half + 1) * 512], kst[0:rows, h, kt * P:(kt + 1) * P],
                                                qst[0:rows, h, :], start=True, stop=True)
                    if half == 1:
                        last.then_inc(scores_ready, 1)

                def pv(quad, piece):
                    gr, kp = quad // QPG, quad % QPG
                    b, g = divmod(gr, G)
                    if piece == 0:
                        pe.wait_ge(probs_ready, ready(4 * quad + 4)[0])
                        if yat:
                            pe.wait_ge(pool_probs, ready(4 * quad + 4)[1])
                        pe.wait_ge(ones, 1)
                        if kp == 0 and gr >= NA:
                            pe.wait_ge(acc_free, gr - NA + 1)
                    out, last = acc[gr % NA], None
                    if window:
                        for kt in ([piece] if piece == 0 else [piece - 1, piece]):
                            at = base[kt] + (P if kt < piece else 0)
                            for j in range(4):
                                last = nc.tensor.matmul(
                                    out[VW * j:VW * (j + 1), piece * P:(piece + 1) * P],
                                    m.vaug[:, b * kt_n + kt, 4 * g + j, :], probs[:, (4 * quad + j) % PR, at:at + P],
                                    start=kt == max(piece - 1, 0), stop=kt == piece)
                    else:
                        i, kt = piece // 2, 2 * kp + piece // 2
                        for j in (2 * (piece % 2), 2 * (piece % 2) + 1):
                            last = nc.tensor.matmul(
                                out[VW * j:VW * (j + 1), :], m.vaug[:, b * kt_n + kt, 4 * g + j, :],
                                probs[:, (4 * quad + j) % PR, i * 512:(i + 1) * 512],
                                start=kt == 0, stop=kt == kt_n - 1)
                    if piece == 3:
                        last.then_inc(pv_done, 1)

                for n in range(len(before)):
                    side(n)
                n = len(before)
                for u in range(units + LAG):
                    due = len(side_tasks(u))
                    for piece in range(3):
                        if piece < 2 and u < units:
                            scores(u, piece)
                        if piece == 2 and u >= LAG:
                            pv((u - LAG) // 4, (u - LAG) % 4)
                        for _ in range((due + (piece if window else 2 - piece)) // 3):
                            side(n)
                            n += 1

            @block.scalar
            def _(act):
                nc.scalar.preload_act_table_set(TABLE_SET)

                def weights(u):
                    act.wait_ge(scores_ready, u + 1)
                    if u >= PR:
                        act.wait_ge(pv_done, (u - PR) // 4 + 1)
                    nc.scalar.activation(probs[:, u % PR, 0:cols], sc[u % NS][:, 0:cols], ACT.Exp,
                                         scale=float(D) ** -0.5).then_inc(probs_ready, 1)

                def reciprocals(u):
                    act.wait_ge(scores_ready, u + 1)
                    if u >= 3:
                        if on_pool(u - 3):
                            act.wait_ge(pool_probs, ready(u - 2)[1])
                        else:
                            act.wait_ge(probs_ready, ready(u - 2)[0])
                    nc.scalar.activation(lnb[:, u % 3, :], sc[u % NS][:, :], ACT.Ln, bias=R.yat_one[:, 0:1], scale=-1.0)\
                        .then_inc(ln_done, 1)
                    act.wait_ge(ln_done, u + 1)
                    nc.scalar.activation(lnb[:, u % 3, :], lnb[:, u % 3, :], ACT.Exp, scale=-1.0).then_inc(rec_done, 1)
                    if on_pool(u):
                        if u >= PR:
                            act.wait_ge(pv_done, (u - PR) // 4 + 1)
                        nc.scalar.activation(probs[:, u % PR, :], sc[u % NS][:, :], ACT.Square, bias=1.0)\
                            .then_inc(squared, 1)

                def sums(gr):
                    act.wait_ge(den_ready, gr + 1)
                    nc.scalar.activation(rec[:, gr % 2, :], den[:, gr % 2, :], ACT.Ln).then_inc(den_ln, 1)
                    act.wait_ge(den_ln, gr + 1)
                    nc.scalar.activation(rec[:, gr % 2, :], rec[:, gr % 2, :], ACT.Exp, scale=-1.0).then_inc(den_rec, 1)
                for u in range(units):
                    if yat:
                        reciprocals(u)
                    else:
                        weights(u)
                    if not yat and after(u) is not None:
                        sums(after(u))
                    if yat and u and after(u - 1) is not None:
                        sums(after(u - 1))
                sums(GR - 1)

            @block.vector
            def _(dve):
                link = chain_of(dve, step)

                def side(n):
                    kind, gr, i = order[n]
                    ps, out = side_ps[n % 3], mx[:, gr % 2]
                    dve.wait_ge(side_mm, n + 1)
                    if kind == "out":
                        if b_out is not None and i == 0:
                            dve.wait_ge(biased, NT)
                        nc.vector.tensor_tensor(R.x[:, i, :], R.x[:, i, :], ps[:, 0:E], ALU.add).then_inc(side_done, 1)
                        return
                    if kind == "rows":
                        if gr >= 1:
                            dve.wait_ge(placed[(gr - 1) % 2], 16 * MAX_ROWS * ((gr - 1) // 2 + 1))
                        high, mid = (neg[:, i, :] for i in range(MAX_ROWS))
                        nc.vector.tensor_scalar(high, ps[0:4, :], -1.0, None, ALU.mult).then_inc(neg_step, 1)
                        dve.wait_ge(neg_step, gr + 1)
                        nc.vector.scalar_tensor_tensor(out=mid, in0=ps[0:4, :], scalar=-1.0, in1=high, op0=ALU.mult,
                                                       op1=ALU.subtract).then_inc(side_done, 1)
                        return
                    if window:
                        j, half = i // 2, i % 2
                        if half == 0:
                            nc.vector.tensor_reduce(out=out[:, 0, j, 0:1], in_=ps[:, P:2 * P], op=ALU.max, axis=AX.X)
                            ins = nc.vector.tensor_reduce(out=out[:, 1, j, 0:1], in_=ps[:, 2 * P:4 * P], op=ALU.max,
                                                          axis=AX.X)
                        else:
                            ins = nc.vector.tensor_reduce(out=out[:, 2:4, j, 0],
                                                          in_=ps[:, :].rearrange("p (t k) -> p t k", t=2),
                                                          op=ALU.max, axis=AX.X)
                    else:
                        ins = nc.vector.tensor_reduce(out=out[:, i // 2 % 4, i // 8, i % 2:i % 2 + 1], in_=ps[:, :],
                                                      op=ALU.max, axis=AX.X)
                    ins.then_inc(side_done, 1)
                    if i == MU - 1:
                        dve.wait_ge(side_done, n + 1)
                        if window:
                            nc.vector.tensor_copy(mxm[:, gr % 2], mx[:, gr % 2, :, :, 0]).then_inc(max_done, 1)
                        else:
                            nc.vector.tensor_tensor(mxm[:, gr % 2], mx[:, gr % 2, :, :, 0], mx[:, gr % 2, :, :, 1],
                                                    ALU.max).then_inc(max_done, 1)

                def weights(u):
                    if on_pool(u):
                        return
                    dve.wait_ge(rec_done, u + 1)
                    nc.vector.scalar_tensor_tensor(out=lnb[:, u % 3, :], in0=sc[u % NS][:, :], scalar=1.0,
                                                   in1=lnb[:, u % 3, :], op0=ALU.add, op1=ALU.mult).then_inc(once_done, 1)
                    dve.wait_ge(once_done, ready(u + 1)[0])
                    if u >= PR:
                        dve.wait_ge(pv_done, (u - PR) // 4 + 1)
                    nc.vector.scalar_tensor_tensor(out=probs[:, u % PR, :], in0=sc[u % NS][:, :], scalar=1.0,
                                                   in1=lnb[:, u % 3, :], op0=ALU.add, op1=ALU.mult).then_inc(probs_ready, 1)

                def sums_before(gr):
                    a, d = accs[:, gr % 2, :], den[:, gr % 2, :]
                    dve.wait_ge(pv_done, (gr + 1) * QPG)
                    if gr >= 2:
                        dve.wait_ge(divided, gr - 1)
                    nc.vector.tensor_copy(a, acc[gr % NA][:, :]).then_inc(acc_free, 1)
                    dve.wait_ge(acc_free, gr + 1)
                    if yat:
                        link(nc.vector.stream_shuffle(d, a, [D + i % D for i in range(VW)]))
                        nc.vector.tensor_scalar_add(d, d, 1e-6).then_inc(den_ready, 1)
                    else:
                        nc.vector.stream_shuffle(d, a, [D + i % D for i in range(VW)]).then_inc(den_ready, 1)

                def sums_after(gr):
                    a, d, r = accs[:, gr % 2, :], den[:, gr % 2, :], rec[:, gr % 2, :]
                    dve.wait_ge(den_rec, gr + 1)
                    link(nc.vector.tensor_tensor(d, d, r, ALU.mult))
                    link(nc.vector.scalar_tensor_tensor(out=d, in0=d, scalar=-2.0, in1=r, op0=ALU.add, op1=ALU.mult))
                    nc.vector.scalar_tensor_tensor(out=m.outT[gr // G][:, gr % G, :], in0=a, scalar=-1.0, in1=d,
                                                   op0=ALU.mult, op1=ALU.mult).then_inc(divided, 1)
                for n in range(len(before)):
                    side(n)
                n = len(before)
                for u in range(units):
                    if after(u) is not None:
                        sums_before(after(u))
                    if yat:
                        weights(u)
                        if u >= 2 and after(u - 2) is not None:
                            sums_after(after(u - 2))
                        continue
                    for _ in side_tasks(u):
                        side(n)
                        n += 1
                if yat:
                    sums_after(GR - 2)
                sums_before(GR - 1)
                if yat:
                    sums_after(GR - 1)


def stage_out(nc, R, tag, outT, w, tiles):
    with stage(nc, R, f"{tag}o") as s:
        ps = [s.ps(f"y{i}") for i in range(NT)]
        ready, added = s.sem("ready"), s.sem("added")
        with nc.Block() as block:

            @block.tensor
            def _(pe):
                for t in tiles:
                    b, at = t // ST, t % ST * P
                    for g in range(G):
                        last = nc.tensor.matmul(ps[t][:, 0:E], outT[b][:, g, at:at + P], w[:, g, :],
                                                start=g == 0, stop=g == G - 1)
                    last.then_inc(ready, 1)

            @block.vector
            def _(dve):
                for n, t in enumerate(tiles):
                    dve.wait_ge(ready, n + 1)
                    nc.vector.tensor_tensor(R.x[:, t, :], R.x[:, t, :], ps[t][:, 0:E], ALU.add).then_inc(added, 1)


def attention16(nc, A, R, tag, kind, wq, wk, wv, wo, bq=None, bk=None, bv=None, bo=None, setup=None):
    keys = CTX if kind == "cross" else S
    with ExitStack() as ctx:
        m = Resident()

        def sb(name, shape, dt=FP32, ctx=ctx):
            return ctx.enter_context(nc.sbuf_tensor(f"{tag}_{name}", shape, dt))
        m.vaug = sb("vaug", [P, B * keys // P, H, VW])
        m.qst = sb("qst", [ROWS + MAX_ROWS, H, S], BF16)
        m.kst = sb("kst", [ROWS + MAX_ROWS, H, keys], BF16)
        m.stack_in = [R.ctx.enter_context(nc.semaphore(f"{tag}_stack_in{g}")) for g in range(G)]
        m.q_dram, m.k_dram = ([nc.dram_tensor(f"{tag}_{n}_parts{b}", (PARTS, D, H, t), BF16, kind="Internal").ap()
                               for b in range(B)] for n, t in (("q", S), ("k", keys)))
        w_out = sb("wo", [P, G, E])
        wo_j = wo.rearrange("(g j d) n -> j d g n", g=G, j=4)
        loads = [(w_out[VW * j:VW * j + D, :, :], wo_j[j]) for j in range(4)]
        b_out = None
        if bo is not None:
            b_out = sb("bo", [P, E])
            loads.append((b_out[:, :], bo.partition_broadcast(P)))
        with ExitStack() as projection:
            w = [Pair(*(sb(n + part, [P, KE, E], FP32R, projection) for part in "hl")) for n in ("wq", "wk", "wv")]
            bias = []
            for n, a in (("bq", bq), ("bk", bk)):
                t = None
                if a is not None:
                    t = sb(n, [P, KE] if kind == "cross" else [P, E], FP32, projection)
                    if kind == "cross":
                        a = a.rearrange("(h m d) -> m d h", m=KE, d=D // KE)
                        loads += [(t[:, i:i + 1], a[i]) for i in range(KE)]
                    else:
                        loads.append((t[:, :], a.partition_broadcast(P)))
                bias.append(t)
            if bv is not None:
                bias.append(sb("bv", [P, E], FP32, projection))
                loads.append((bias[2][:, :], bv.partition_broadcast(P)))
            with ExitStack() as whole:
                w_full = [sb(n, [P, KE, E], FP32, whole) for n in ("wq", "wk", "wv")]
                splits = [(f[:, k, :].rearrange("p (h d) -> p d h", d=D), p[:, k, :].rearrange("p (d h) -> p d h", d=D))
                          for f, p in zip(w_full[0:2], w[0:2]) for k in range(KE)] + [(w_full[2][:, :, :], w[2][:, :, :])]
                loads = [(t[:, :, :], a.rearrange("(k p) n -> p k n", p=P)) for t, a in zip(w_full, (wq, wk, wv))] + loads
                stage_norm(nc, R, f"{tag}n", loads, w_out, splits, setup=setup)
            stage_project(nc, R, tag, m, kind, *w, *bias)
        m.outT = [R.xn[:, :, :].rearrange("p (g a) e -> p g (a e)", g=G), sb("out1", [P, G, S])[:, :, :]]
        stage_attend(nc, R, tag, m, kind, w_out, b_out)
        stage_out(nc, R, tag, m.outT, w_out, range(0 if kind == "yat" else ST, NT))


def stage_wide(nc, R, wq, wk, wv, w_out, b_out):
    HP = H1 // 2
    PAIRS = B * HP
    units = PAIRS * CT
    RP, PR, LAG = 3, 3, 2
    CQ = CTX // 512

    def side_tasks(p, i):
        out = []
        if i == 3 and p >= 1:
            out.append(("den", p - 1, 0))
        if p + 1 < PAIRS:
            out += [("max", p + 1, k) for k in range(16 * i // 5, 16 * (i + 1) // 5) if i < 5]
            if i == 6:
                out.append(("rows", p + 1, 0))
        if p // 2 + 1 < PAIRS // 2:
            out += [("v", p // 2 + 1, 2 * (p % 2) + k) for k, at in enumerate((5, 7)) if i == at]
        if p + 2 < PAIRS:
            out += [(kind, p + 2, c) for kind, c, at in (("q", 0, 4), ("k", 0, 5), ("k", 1, 6)) if i == at]
        if p == HP and i >= 6:
            out += [("out", 0, 2 * (i - 6) + k) for k in range(2)]
        return out

    before = [("q", 0, 0), ("k", 0, 0), ("k", 0, 1)] + [("max", 0, i) for i in range(8)]
    before += [("q", 1, 0), ("k", 1, 0), ("k", 1, 1)] + [("max", 0, i) for i in range(8, 16)]
    before += [("v", 0, i) for i in range(2)] + [("rows", 0, 0)] + [("v", 0, i) for i in range(2, 4)]
    behind = [("den", PAIRS - 1, 0)] + [("out", 1, i) for i in range(ST)]
    order = before + [t for p in range(PAIRS) for i in range(CT) for t in side_tasks(p, i)] + behind
    number = {t: n for n, t in enumerate(order)}

    with stage(nc, R, "c") as s:
        q1, q2 = (s.sb(n, [P, 2 * RP, S], FP32R) for n in ("q1", "q2"))
        k1, k2 = (s.sb(n, [P, 2 * RP, CTX], FP32R) for n in ("k1", "k2"))
        v = s.sb("v", [P, 2, CT, 4 * D1])
        probs = s.sb("probs", [P, PR, 1024])
        total = s.sb("total", [P, 2, 1024])
        rec, den = ([total[:, i, c * 512:(c + 1) * 512] for i in range(2)] for c in range(2))
        acc_s = s.sb("acc_s", [P, 512])
        ones = s.sb("ones", [P, D1])
        mx, mxm = s.sb("mx", [P, 2, 2, ST, CQ]), s.sb("mxm", [P, 2, 2, ST])
        outT = R.xn[:, :, :].rearrange("p (g a) e -> p g (a e)", g=G)
        sc = [s.ps(f"sc{i}", [P, 1024]) for i in range(2)]
        side_ps = [s.ps(f"side{i}") for i in range(3)]
        acc = s.ps("acc")
        side_mm, side_done, high_done = s.sem("side_mm"), s.sem("side_done"), s.sem("high_done")
        twin_done = s.sem("twin_done")
        scores_ready, probs_ready, pv_done, summed = (s.sem(n) for n in ("scores_ready", "probs_ready", "pv_done", "summed"))
        acc_copied, den_ln, den_rec, divided = (s.sem(n) for n in ("acc_copied", "den_ln", "den_rec", "divided"))
        pads, max_done, step = s.sem("pads"), s.sem("max_done"), s.sem("step")

        def halves(j):
            return (slice(0, D1), slice(D1, P)) if j == 0 else (slice(D1, P), slice(0, D1))

        def sums_with(u):
            return (CT - 1) * (u // CT) + max(u % CT, 1)

        with nc.Block() as block:

            @block.gpsimd
            def _(pool):
                nc.gpsimd.memset(ones[:, :], 1.0).then_inc(pads, 1)
                for slot in range(2 * RP):
                    other = halves(slot % 2)[1]
                    pool.wait_ge(pads, 1 + 2 * slot)
                    nc.gpsimd.memset(q2[other, slot, :].bitcast(FP32), 0.0).then_inc(pads, 1)
                    pool.wait_ge(pads, 2 + 2 * slot)
                    nc.gpsimd.memset(k2[other, slot, :].bitcast(FP32), 1.0).then_inc(pads, 1)
                pool.wait_ge(pads, 1 + 4 * RP)
                for u in range(units):
                    p, kt = u // CT, u % CT
                    if kt == 0:
                        continue
                    pool.wait_ge(probs_ready, u + 1)
                    if kt == 1 and p >= 2:
                        pool.wait_ge(divided, p - 1)
                    out = total[:, p % 2, :]
                    if u >= 2:
                        pool.wait_ge(summed, sums_with(u) - 1)
                    nc.gpsimd.tensor_tensor(out, probs[:, (u - 1) % PR, :] if kt == 1 else out, probs[:, u % PR, :],
                                            ALU.add).then_inc(summed, 1)

            @block.tensor
            def _(pe):
                def side(n):
                    kind, p, i = order[n]
                    ps = side_ps[n % 3]
                    if n >= 3:
                        pe.wait_ge(side_done, n - 2)
                    b, g = p // HP, p % HP
                    if kind in "qk":
                        w, x, at = (wq, R.xnT, b * S) if kind == "q" else (wk, R.ctxT, b * CTX + i * 512)
                        for k in range(KE):
                            last = matmul3(nc, ps[:, :], w[:, k, g * P:(g + 1) * P], x[:, k, at:at + 512],
                                           start=k == 0, stop=k == KE - 1)
                    if kind == "v":
                        for j in range(2):
                            at = (p // 2) * CTX + (2 * i + j) * P
                            for k in range(KE):
                                last = matmul3(nc, ps[:, j * 256:(j + 1) * 256], R.ctxT[:, k, at:at + P],
                                               wv[:, k, p % 2 * 256:(p % 2 + 1) * 256], start=k == 0, stop=k == KE - 1)
                    if kind == "max":
                        slot, qt, c = p % RP * 2 + i // 8, i // 2 % 4, i % 2
                        pe.wait_ge(side_done, number["k", p, 1] + 1)
                        pe.wait_ge(twin_done, (1 + CQ) * (p + 1))
                        last = nc.tensor.matmul(ps[:, :], q1[:, slot, qt * P:(qt + 1) * P],
                                                k1[:, slot, c * 512:(c + 1) * 512], start=True, stop=True)
                    if kind == "rows":
                        pe.wait_ge(max_done, p + 1)
                        for j in range(2):
                            row = D1 * (1 - j)
                            for t in range(ST):
                                last = nc.tensor.matmul(ps[row:row + 1, t * P:(t + 1) * P], mxm[:, p % 2, j, t:t + 1],
                                                        R.ident[:, :], start=True, stop=True)
                    if kind == "den":
                        pe.wait_ge(summed, (CT - 1) * (p + 1))
                        pe.wait_ge(pads, 1)
                        for j in range(2):
                            last = nc.tensor.matmul(ps[D1 * j:D1 * (j + 1), :], ones[:, :],
                                                    total[:, p % 2, j * 512:(j + 1) * 512], start=True, stop=True)
                    if kind == "out":
                        pe.wait_ge(divided, HP * (p + 1))
                        for g in range(G):
                            nc.tensor.matmul(ps[:, 0:E], outT[:, g, i * P:(i + 1) * P], w_out[:, g, :],
                                             start=g == 0, stop=False)
                        last = nc.tensor.matmul(ps[:, 0:E], R.ones_row[:, :], b_out[:, :], start=False, stop=True)
                    last.then_inc(side_mm, 1)

                def scores(u, j):
                    p, kt = u // CT, u % CT
                    if kt == 0 and j == 0:
                        pe.wait_ge(side_done, number["rows", p, 0] + 1)
                        pe.wait_ge(pads, 1 + 4 * RP)
                    if u >= 2 and j == 0:
                        pe.wait_ge(probs_ready, u - 1)
                    slot, out = p % RP * 2 + j, sc[u % 2][:, j * 512:(j + 1) * 512]
                    nc.tensor.matmul(out, k1[:, slot, kt * P:(kt + 1) * P], q1[:, slot, :], start=True, stop=False)
                    last = nc.tensor.matmul(out, k2[:, slot, kt * P:(kt + 1) * P], q2[:, slot, :], start=False, stop=True)
                    if j == 1:
                        last.then_inc(scores_ready, 1)

                def pv(u):
                    p, kt = u // CT, u % CT
                    pe.wait_ge(probs_ready, u + 1)
                    if kt == 0:
                        if p >= 1:
                            pe.wait_ge(acc_copied, p)
                        pe.wait_ge(side_done, number["v", p // 2, 3] + 1)
                    for j in range(2):
                        at = (2 * (p % 2) + j) * D1
                        last = nc.tensor.matmul(acc[D1 * j:D1 * (j + 1), :], v[:, p // 2 % 2, kt, at:at + D1],
                                                probs[:, u % PR, j * 512:(j + 1) * 512], start=kt == 0, stop=kt == CT - 1)
                    last.then_inc(pv_done, 1)
                for n in range(len(before)):
                    side(n)
                n = len(before)
                for u in range(units + LAG):
                    due = len(side_tasks(u // CT, u % CT)) if u < units else 0
                    for piece in range(3):
                        if piece < 2 and u < units:
                            scores(u, piece)
                        if piece == 2 and u >= LAG:
                            pv(u - LAG)
                        for _ in range((due + piece) // 3):
                            side(n)
                            n += 1
                for n in range(n, len(order)):
                    side(n)

            @block.scalar
            def _(act):
                nc.scalar.preload_act_table_set(TABLE_SET)
                copies = [0]

                def side(n):
                    kind, p, i = order[n]
                    if kind == "den":
                        act.wait_ge(side_done, n + 1)
                        nc.scalar.activation(rec[p % 2], den[p % 2], ACT.Ln).then_inc(den_ln, 1)
                        act.wait_ge(den_ln, p + 1)
                        nc.scalar.activation(rec[p % 2], rec[p % 2], ACT.Exp, scale=-1.0).then_inc(den_rec, 1)
                    if kind in "qk":
                        act.wait_ge(side_mm, n + 1)
                        if p >= RP:
                            act.wait_ge(scores_ready, CT * (p - RP + 1))
                        twin, at = (q1, slice(0, S)) if kind == "q" else (k2, slice(i * 512, (i + 1) * 512))
                        first = q1 if kind == "q" else k1
                        for j in range(2):
                            own, slot = halves(j)[0], p % RP * 2 + j
                            last = nc.scalar.activation(first[own, slot, at], side_ps[n % 3][own, :], ACT.Copy)
                        last.then_inc(high_done, 1)
                        copies[0] += 1
                        act.wait_ge(high_done, copies[0])
                        for j in range(2):
                            (own, other), slot = halves(j), p % RP * 2 + j
                            last = nc.scalar.activation(twin[other if kind == "q" else own, slot, at],
                                                        first[own, slot, at].bitcast(FP32), ACT.Copy)
                        last.then_inc(twin_done, 1)

                for n in range(len(before)):
                    side(n)
                n = len(before)
                for u in range(units):
                    act.wait_ge(scores_ready, u + 1)
                    if u >= PR:
                        act.wait_ge(pv_done, u - PR + 1)
                        act.wait_ge(summed, sums_with(u - PR))
                    nc.scalar.activation(probs[:, u % PR, :], sc[u % 2][:, :], ACT.Exp, scale=float(D1) ** -0.5)\
                        .then_inc(probs_ready, 1)
                    for _ in side_tasks(u // CT, u % CT):
                        side(n)
                        n += 1
                for n in range(n, len(order)):
                    side(n)

            @block.vector
            def _(dve):
                link = chain_of(dve, step)
                highs = [0]

                def side(n):
                    kind, p, i = order[n]
                    ps = side_ps[n % 3]
                    dve.wait_ge(side_mm, n + 1)
                    if kind in "qk":
                        highs[0] += 1
                        dve.wait_ge(high_done, highs[0])
                        for j in range(2):
                            own, other = halves(j)
                            slot, at = p % RP * 2 + j, slice(i * 512, (i + 1) * 512)
                            if kind == "q":
                                high, low = q1[own, slot, :], q2[own, slot, :]
                            else:
                                high, low = k1[own, slot, at], k1[other, slot, at]
                            last = nc.vector.tensor_tensor(low, ps[own, :], high.bitcast(FP32), ALU.subtract)
                    if kind == "v":
                        if p >= 2:
                            dve.wait_ge(pv_done, 2 * CT * (p - 1))
                        last = nc.vector.tensor_copy(v[:, p % 2, 2 * i:2 * i + 2, :],
                                                     ps[:, :].rearrange("p (t n) -> p t n", t=2))
                    if kind == "max":
                        last = nc.vector.tensor_reduce(out=mx[:, p % 2, i // 8, i // 2 % 4, i % 2:i % 2 + 1], in_=ps[:, :],
                                                       op=ALU.max, axis=AX.X)
                    if kind == "rows":
                        dve.wait_ge(pads, 1 + 4 * RP)
                        for j in range(2):
                            row = D1 * (1 - j)
                            last = nc.vector.tensor_scalar(q2[row:row + 1, p % RP * 2 + j, :], ps[row:row + 1, :], -1.0,
                                                           None, ALU.mult)
                    if kind == "den":
                        last = nc.vector.tensor_copy(den[p % 2], ps[:, :])
                    if kind == "out":
                        x = R.x[:, p * ST + i, :]
                        last = nc.vector.tensor_tensor(x, x, ps[:, 0:E], ALU.add)
                    last.then_inc(side_done, 1)
                    if kind == "max" and i == 15:
                        dve.wait_ge(side_done, n + 1)
                        nc.vector.tensor_tensor(mxm[:, p % 2], mx[:, p % 2, :, :, 0], mx[:, p % 2, :, :, 1], ALU.max)\
                            .then_inc(max_done, 1)

                def copy_acc(p):
                    dve.wait_ge(pv_done, CT * (p + 1))
                    if p >= 1:
                        dve.wait_ge(divided, p)
                    nc.vector.tensor_copy(acc_s[:, :], acc[:, :]).then_inc(acc_copied, 1)

                def divide(p):
                    dve.wait_ge(den_rec, p + 1)
                    dve.wait_ge(acc_copied, p + 1)
                    d, r = den[p % 2], rec[p % 2]
                    link(nc.vector.tensor_tensor(d, d, r, ALU.mult))
                    link(nc.vector.scalar_tensor_tensor(out=d, in0=d, scalar=-2.0, in1=r, op0=ALU.add, op1=ALU.mult))
                    nc.vector.scalar_tensor_tensor(out=outT[:, p % HP, :], in0=acc_s[:, :], scalar=-1.0, in1=d,
                                                   op0=ALU.mult, op1=ALU.mult).then_inc(divided, 1)
                for n in range(len(before)):
                    side(n)
                n = len(before)
                for u in range(units):
                    p, i = u // CT, u % CT
                    if i == LAG and p >= 1:
                        copy_acc(p - 1)
                    for _ in side_tasks(p, i):
                        side(n)
                        n += 1
                    if i == 4 and p >= 1:
                        divide(p - 1)
                copy_acc(PAIRS - 1)
                side(n)
                divide(PAIRS - 1)
                for n in range(n + 1, len(order)):
                    side(n)


def attention_wide(nc, A, R):
    with ExitStack() as ctx:
        def sb(name, shape, dt=FP32, ctx=ctx):
            return ctx.enter_context(nc.sbuf_tensor(f"c_{name}", shape, dt))
        w_out, b_out = sb("wo", [P, G, E]), sb("bo", [1, E])
        w = [Pair(*(sb(n + part, [P, KE, H1 * D1], FP32R) for part in "hl")) for n in ("wq", "wk", "wv")]
        with ExitStack() as whole:
            w_full = [sb(n, [P, KE, H1 * D1], FP32, whole) for n in ("wq", "wk", "wv")]
            loads = [(t[:, :, :], A[f"L1_xattn_{n}"].rearrange("(k p) n -> p k n", p=P))
                     for t, n in zip(w_full + [w_out], ("Wq", "Wk", "Wv", "Wo"))]
            loads.append((b_out[:, :], A["L1_xattn_bo"].rearrange("(a n) -> a n", a=1)))
            stage_norm(nc, R, "cn", loads, splits=[(f[:, :, :], p[:, :, :]) for f, p in zip(w_full, w)])
        stage_wide(nc, R, *w, w_out, b_out)


def route_top2(nc, R, s, m, gate_w, ps):
    NE = 8
    logits = ps[:, 0:NT * NE].rearrange("p (t n) -> p t n", n=NE)
    e, top, we2 = s.sb("e", [P, NT, NE]), s.sb("top", [P, NT, NE]), s.sb("we2", [P, NT, NE])
    idx, idxf = s.sb("idx", [P, NT, NE], U32), s.sb("idxf", [P, NT, NE])
    col = s.sb("col", [P, NT, 1])
    io_i, io_f = s.sb("io_i", [P, NE], I32), s.sb("io_f", [P, NE])
    ready, shifted, exps, iota_done, step = (s.sem(n) for n in ("r_logits", "r_shifted", "r_exps", "r_iota", "r_step"))
    bc = lambda ap: ap.broadcast_to([P, NT, NE])

    def tensor(pe):
        for t in range(NT):
            for k in range(KE):
                last = matmul3(nc, logits[:, t, :], R.xnT[:, k, t * P:(t + 1) * P], gate_w[:, k, :],
                                        start=k == 0, stop=k == KE - 1)
        last.then_inc(ready, 1)

    def gpsimd(pool):
        nc.gpsimd.iota(io_i[:, :], pattern=[[1, NE]], base=0, channel_multiplier=0).then_inc(iota_done, 1)

    def scalar(act):
        act.wait_ge(shifted, 1)
        nc.scalar.activation(e[:, :, :], e[:, :, :], ACT.Exp).then_inc(exps, 1)

    def vector(dve):
        link = chain_of(dve, step)
        v = nc.vector
        dve.wait_ge(ready, 1)
        link(v.tensor_reduce(out=col[:, :, 0], in_=logits[:, :, :], op=ALU.max, axis=AX.X))
        v.tensor_tensor(e[:, :, :], logits[:, :, :], bc(col[:, :, :]), ALU.subtract).then_inc(shifted, 1)
        dve.wait_ge(exps, 1)
        link(v.tensor_reduce(out=col[:, :, 0], in_=e[:, :, :], op=ALU.add, axis=AX.X))
        link(v.reciprocal(col[:, :, :], col[:, :, :]))
        link(v.tensor_tensor(e[:, :, :], e[:, :, :], bc(col[:, :, :]), ALU.mult))
        for t in range(NT):
            last = v.max(top[:, t, :], e[:, t, :])
        link(last)
        for t in range(NT):
            last = v.max_index(idx[:, t, :], top[:, t, :], e[:, t, :])
        link(last)
        link(v.tensor_copy(idxf[:, :, :], idx[:, :, :]))
        link(v.tensor_tensor(col[:, :, :], top[:, :, 0:1], top[:, :, 1:2], ALU.add))
        link(v.tensor_scalar_add(col[:, :, :], col[:, :, :], 1e-20))
        link(v.reciprocal(col[:, :, :], col[:, :, :]))
        link(v.tensor_tensor(top[:, :, :], top[:, :, :], bc(col[:, :, :]), ALU.mult))
        dve.wait_ge(iota_done, 1)
        link(v.tensor_copy(io_f[:, :], io_i[:, :]))
        grid = io_f[:, :].unsqueeze(1).broadcast_to([P, NT, NE])
        link(v.tensor_tensor(m.we[:, :, :], grid, bc(idxf[:, :, 0:1]), ALU.is_equal))
        link(v.tensor_tensor(we2[:, :, :], grid, bc(idxf[:, :, 1:2]), ALU.is_equal))
        link(v.tensor_tensor(m.we[:, :, :], m.we[:, :, :], bc(top[:, :, 0:1]), ALU.mult))
        link(v.tensor_tensor(we2[:, :, :], we2[:, :, :], bc(top[:, :, 1:2]), ALU.mult))
        v.tensor_tensor(m.we[:, :, :], m.we[:, :, :], we2[:, :, :], ALU.add).then_inc(m.routed, 1)
    return tensor, scalar, vector, gpsimd


def route_hash(nc, R, s, m, ps):
    NE = 8
    sm, r, a, c = (s.sb(n, [P, NT, 1]) for n in ("sm", "r", "a", "c"))
    hi, hj = s.sb("hi", [P, NT, 1], I32), s.sb("hj", [P, NT, 1], I32)
    io_i, io_f, we2 = s.sb("io_i", [P, NE], I32), s.sb("io_f", [P, NE]), s.sb("we2", [P, NT, NE])
    iota_done, step = s.sem("h_iota"), s.sem("h_step")
    b1_t = s.sem("h_b1t")
    tp = ps

    def gpsimd(pool):
        nc.gpsimd.iota(io_i[:, :], pattern=[[1, NE]], base=0, channel_multiplier=0).then_inc(iota_done, 1)

    def tensor(pe):
        rows = m.b1_rows.shape[0]
        nc.tensor.transpose(tp[:, 0:rows], m.b1_rows[:, :], R.ident[0:rows, 0:rows]).then_inc(b1_t, 1)

    def vector(dve):
        link = chain_of(dve, step)
        v = nc.vector
        dve.wait_ge(b1_t, 1)
        v.tensor_copy(m.b1[:, :], tp[:, 0:m.b1_rows.shape[0]]).then_inc(m.b1_ready, 1)
        link(v.tensor_tensor(sm[:, :, :], R.xn[:, :, 0:1], R.xn[:, :, 1:2], ALU.add))
        link(v.tensor_copy(hi[:, :, :], sm[:, :, :]))
        link(v.tensor_copy(r[:, :, :], hi[:, :, :]))
        link(v.tensor_tensor(a[:, :, :], r[:, :, :], sm[:, :, :], ALU.is_gt))
        link(v.tensor_scalar(c[:, :, :], sm[:, :, :], 0.0, None, ALU.is_gt))
        link(v.tensor_tensor(c[:, :, :], a[:, :, :], c[:, :, :], ALU.mult))
        link(v.tensor_tensor(a[:, :, :], r[:, :, :], sm[:, :, :], ALU.is_lt))
        link(v.tensor_tensor(r[:, :, :], r[:, :, :], c[:, :, :], ALU.subtract))
        link(v.tensor_scalar(c[:, :, :], sm[:, :, :], 0.0, None, ALU.is_lt))
        link(v.tensor_tensor(c[:, :, :], a[:, :, :], c[:, :, :], ALU.mult))
        link(v.tensor_tensor(r[:, :, :], r[:, :, :], c[:, :, :], ALU.add))
        dve.wait_ge(iota_done, 1)
        link(v.tensor_copy(io_f[:, :], io_i[:, :]))
        grid = io_f[:, :].unsqueeze(1).broadcast_to([P, NT, NE])
        bc = lambda ap: ap.broadcast_to([P, NT, NE])
        for i, out in enumerate((m.we, we2)):
            link(v.tensor_scalar_add(c[:, :, :], r[:, :, :], float(i)))
            link(v.tensor_copy(hi[:, :, :], c[:, :, :]))
            link(v.tensor_scalar(hj[:, :, :], hi[:, :, :], NE - 1, None, ALU.bitwise_and))
            link(v.tensor_copy(c[:, :, :], hj[:, :, :]))
            link(v.tensor_tensor(out[:, :, :], grid, bc(c[:, :, :]), ALU.is_equal))
        link(v.tensor_tensor(m.we[:, :, :], m.we[:, :, :], we2[:, :, :], ALU.add))
        v.tensor_scalar(m.we[:, :, :], m.we[:, :, :], 0.5, None, ALU.mult).then_inc(m.routed, 1)

    def scalar(act):
        act.wait_ge(m.b1_ready, 1)
    return tensor, scalar, vector, gpsimd


class Experts:

    def __init__(self, nc, R, ctx, tag, experts, hid):
        self.experts, self.hid, self.HT = experts, hid, hid // P
        self.n_w = n_w = len(experts[0]) - 1
        self.first_cols, cols = (n_w - 1) * KE * hid, n_w * KE * hid
        self.whole = ctx.enter_context(nc.sbuf_tensor(f"{tag}_whole", [P, cols], FP32))
        self.parts = Pair(*(ctx.enter_context(nc.sbuf_tensor(f"{tag}_parts_{n}", [P, 2, cols], FP32R)) for n in "hl"))
        self.w_in = R.ctx.enter_context(nc.semaphore(f"{tag}_w_in"))

    def loads(self, e):
        out, at = [], 0
        for src in self.experts[e][:-1]:
            n = src.shape[0] * src.shape[1] // P
            out.append((self.whole[:, at:at + n].rearrange("p (k n) -> p k n", n=src.shape[1]),
                        src.rearrange("(k p) n -> p k n", p=P)))
            at += n
        return out

    def first(self, w):
        return w[:, 0:self.first_cols].rearrange("p (w k n) -> p w k n", k=KE, n=self.hid)

    def second(self, w):
        return w[:, self.first_cols:].rearrange("p (k n) -> p k n", k=self.HT)

    def pieces(self, w, i):
        return self.first(w)[:, :, :, i * P:(i + 1) * P], self.second(w)[:, i, :]


def stage_experts(nc, R, m, tag, X, gated, route, store=None):
    HT, experts = X.HT, X.experts
    CH = N // 512
    UR = 3 if gated else 6
    units = [(e, c) for e in range(len(experts)) for c in range(CH)]
    with stage(nc, R, tag) as s:
        s.sems.append(X.w_in)
        hT = Pair(s.sb("hT_h", [P, 2, HT, 512], FP32R), s.sb("hT_l", [P, 2, HT, 512], FP32R))
        act_t = s.sb("act_t", [P, 3, 512]) if gated else None
        hid_t = s.sb("hid_t", [P, UR, 512])
        up = [s.ps(f"up{i}") for i in range(UR)]
        gate = [s.ps(f"gate{i}") for i in range(3)] if gated else None
        down = [s.ps(f"down{i}") for i in range(2)]
        w_high, w_low, hid_done, h_high = (s.sem(n) for n in ("w_high", "w_low", "hid_done", "h_high"))
        act_done, h_done, y_ready, y_added = (s.sem(n) for n in ("act_done", "h_done", "y_ready", "y_added"))
        first_ready = s.sem("first_ready")
        m.routed, m.b1_ready, wt_mm, wt_done = (s.sem(n) for n in ("routed", "b1_ready", "wt_mm", "wt_done"))
        route_pe, route_act, route_dve, route_pool = route(nc, R, s, m, down[1])

        with nc.Block() as block:

            @block.sync
            def _(sp):
                for e in range(1, len(experts)):
                    sp.wait_ge(w_low, HT * e)
                    for dst, src in X.loads(e):
                        sp.dma_start(dst, src).then_inc(X.w_in, 16)
                if store:
                    out, stored = store
                    for t in range(NT):
                        sp.wait_ge(y_added, 4 * len(units) + t + 1)
                        sp.dma_start(out[t // ST, t % ST * P:(t % ST + 1) * P, :], R.x[:, t, :]).then_inc(stored, 16)
                    sp.wait_ge(stored, 16 * NT)

            @block.gpsimd
            def _(pool):
                route_pool(pool)

            @block.tensor
            def _(pe):
                def first(n):
                    e, c = units[n]
                    w = X.first(X.parts[:, e % 2, :])
                    for i in range(HT):
                        u = n * HT + i
                        if c == 0:
                            pe.wait_ge(w_low, e * HT + i + 1)
                        if u >= UR:
                            pe.wait_ge(hid_done, u - UR + 1)
                        for j, out in enumerate((gate, up) if gated else (up,)):
                            for k in range(KE):
                                last = matmul3(nc, out[u % UR][:, :], w[:, j, k, i * P:(i + 1) * P],
                                               R.xnT[:, k, c * 512:(c + 1) * 512], start=k == 0, stop=k == KE - 1)
                        last.then_inc(first_ready, 1)

                def second(n):
                    e, c = units[n]
                    w = X.second(X.parts[:, e % 2, :])
                    pe.wait_ge(h_done, (n + 1) * HT)
                    for t in range(4):
                        u = 4 * n + t
                        if u >= 2:
                            pe.wait_ge(y_added, u - 1)
                        elif u == 1:
                            pe.wait_ge(m.routed, 1)
                        for k in range(HT):
                            last = matmul3(nc, down[u % 2][:, 0:E], hT[:, n % 2, k, t * P:(t + 1) * P], w[:, k, :],
                                           start=k == 0, stop=k == HT - 1)
                        last.then_inc(y_ready, 1)
                route_pe(pe)
                for n in range(len(units) + 1):
                    if n < len(units):
                        first(n)
                    if n >= 1:
                        second(n - 1)
                if not gated:
                    pe.wait_ge(hid_done, len(units) * HT)
                    for t in range(NT):
                        last = nc.tensor.transpose(up[t // 4][0:8, t % 4 * P:(t % 4 + 1) * P], m.we[:, t, :], R.ident[:, :])
                    last.then_inc(wt_mm, 1)
                    pe.wait_ge(wt_done, 1)
                    for t in range(NT):
                        u = 4 * len(units) + t
                        pe.wait_ge(y_added, u - 1)
                        nc.tensor.matmul(down[u % 2][:, 0:E], m.weT[:, t * P:(t + 1) * P], m.b2[:, :],
                                         start=True, stop=True).then_inc(y_ready, 1)

            @block.scalar
            def _(act):
                if not gated:
                    nc.scalar.preload_act_table_set(TABLE_SET)

                def split_weights(e, i):
                    if i == 0:
                        act.wait_ge(X.w_in, 16 * X.n_w * (e + 1))
                        if e >= 2:
                            act.wait_ge(y_ready, 4 * CH * (e - 1))
                    for part, whole in zip(X.pieces(X.parts.hi[:, e % 2, :], i), X.pieces(X.whole[:, :], i)):
                        last = nc.scalar.activation(part, whole, ACT.Copy)
                    last.then_inc(w_high, 1)

                def high_part(u):
                    act.wait_ge(hid_done, u + 1)
                    n, i = u // HT, u % HT
                    if n >= 2:
                        act.wait_ge(y_ready, 4 * (n - 1))
                    nc.scalar.activation(hT.hi[:, n % 2, i, :], hid_t[:, u % UR, :], ACT.Copy).then_inc(h_high, 1)
                for i in range(HT):
                    split_weights(0, i)
                route_act(act)
                for n, (e, c) in enumerate(units):
                    for i in range(HT):
                        u = n * HT + i
                        act.wait_ge(first_ready, u + 1)
                        if gated:
                            if u >= 3:
                                act.wait_ge(hid_done, u - 2)
                            nc.scalar.activation(act_t[:, u % 3, :], gate[u % 3][:, :], ACT.Silu).then_inc(act_done, 1)
                        else:
                            if u >= UR:
                                act.wait_ge(h_done, u - UR + 1)
                            nc.scalar.activation(hid_t[:, u % UR, :], up[u % UR][:, :], ACT.Relu,
                                                 bias=m.b1[:, e * HT + i:e * HT + i + 1]).then_inc(hid_done, 1)
                        if i >= 1:
                            high_part(u - 1)
                        if c == CH - 1 and e + 1 < len(experts):
                            split_weights(e + 1, i)
                    high_part(n * HT + HT - 1)

            @block.vector
            def _(dve):
                def low_weights(e, i):
                    dve.wait_ge(w_high, e * HT + i + 1)
                    for low, high, whole in zip(X.pieces(X.parts.lo[:, e % 2, :], i), X.pieces(X.parts.hi[:, e % 2, :], i),
                                                X.pieces(X.whole[:, :], i)):
                        last = nc.vector.tensor_tensor(low, whole, high.bitcast(FP32), ALU.subtract)
                    last.then_inc(w_low, 1)

                def low_part(u):
                    n, i = u // HT, u % HT
                    dve.wait_ge(h_high, u + 1)
                    nc.vector.tensor_tensor(hT.lo[:, n % 2, i, :], hid_t[:, u % UR, :],
                                            hT.hi[:, n % 2, i, :].bitcast(FP32), ALU.subtract).then_inc(h_done, 1)

                def residual(n, tiles):
                    e, c = units[n]
                    column = experts[e][-1]
                    for t in tiles:
                        x = R.x[:, 4 * c + t, :]
                        u = 4 * n + t
                        dve.wait_ge(y_ready, u + 1)
                        if column is None:
                            nc.vector.tensor_tensor(x, down[u % 2][:, 0:E], x, ALU.add).then_inc(y_added, 1)
                        else:
                            nc.vector.scalar_tensor_tensor(out=x, in0=down[u % 2][:, 0:E],
                                                           scalar=m.we[:, 4 * c + t, column:column + 1], in1=x,
                                                           op0=ALU.mult, op1=ALU.add).then_inc(y_added, 1)
                for i in range(HT):
                    low_weights(0, i)
                route_dve(dve)
                for n, (e, c) in enumerate(units):
                    for i in range(HT):
                        u = n * HT + i
                        if gated:
                            dve.wait_ge(act_done, u + 1)
                            if u >= 3:
                                dve.wait_ge(h_done, u - 2)
                            nc.vector.tensor_tensor(hid_t[:, u % 3, :], act_t[:, u % 3, :], up[u % 3][:, :], ALU.mult)\
                                .then_inc(hid_done, 1)
                        if i >= 1:
                            low_part(u - 1)
                        if c == CH - 1 and e + 1 < len(experts):
                            low_weights(e + 1, i)
                    if n >= 1:
                        residual(n - 1, range(0, 1))
                    low_part(n * HT + HT - 1)
                    if n >= 1:
                        residual(n - 1, range(1, 4))
                residual(len(units) - 1, range(4))
                if not gated:
                    dve.wait_ge(wt_mm, 1)
                    nc.vector.tensor_copy(m.weT[:, 0:512], up[0][0:8, :])
                    nc.vector.tensor_copy(m.weT[:, 512:1024], up[1][0:8, :]).then_inc(wt_done, 1)
                    for t in range(NT):
                        u = 4 * len(units) + t
                        dve.wait_ge(y_ready, u + 1)
                        dve.wait_ge(y_added, u)
                        nc.vector.tensor_tensor(R.x[:, t, :], down[u % 2][:, 0:E], R.x[:, t, :], ALU.add).then_inc(y_added, 1)


def experts_top2(nc, A, R):
    with ExitStack() as ctx:
        m = Resident()
        m.we = ctx.enter_context(nc.sbuf_tensor("f_we", [P, NT, 8], FP32))
        full = ctx.enter_context(nc.sbuf_tensor("f_gate_w", [P, KE, 8], FP32))
        gate_w = Pair(*(ctx.enter_context(nc.sbuf_tensor(f"f_gate_{n}", [P, KE, 8], FP32R)) for n in "hl"))
        experts = [(A["L0_ffn_ws_gate"], A["L0_ffn_ws_up"], A["L0_ffn_ws_down"], None)]
        experts += [(A["L0_ffn_w_gate"][e], A["L0_ffn_w_up"][e], A["L0_ffn_w_down"][e], e) for e in range(8)]
        X = Experts(nc, R, ctx, "f", experts, A["L0_ffn_ws_gate"].shape[1])
        stage_norm(nc, R, "fn", [(full[:, :, :], A["L0_ffn_gate_w"].rearrange("(k p) n -> p k n", p=P))],
                   splits=[(full[:, :, :], gate_w[:, :, :])], ahead=[(*load, X.w_in) for load in X.loads(0)])
        stage_experts(nc, R, m, "fe", X, True, lambda nc, R, s, m, ps: route_top2(nc, R, s, m, gate_w, ps))


def experts_hash(nc, A, R, store):
    with ExitStack() as ctx:
        m = Resident()

        def sb(name, shape):
            return ctx.enter_context(nc.sbuf_tensor(f"g_{name}", shape, FP32))
        n_e, hid = A["L1_ffn_b1"].shape
        m.we, m.weT = sb("we", [P, NT, 8]), sb("weT", [8, N])
        m.b1_rows, m.b1, m.b2 = sb("b1_rows", [n_e * hid // P, P]), sb("b1", [P, n_e * hid // P]), sb("b2", [n_e, E])
        X = Experts(nc, R, ctx, "g", [(A["L1_ffn_W1"][e], A["L1_ffn_W2"][e], e) for e in range(n_e)], hid)
        stage_norm(nc, R, "gn", [(m.b1_rows[:, :], A["L1_ffn_b1"].rearrange("e (m p) -> (e m) p", p=P)),
                                 (m.b2[:, :], A["L1_ffn_b2"])], ahead=[(*load, X.w_in) for load in X.loads(0)])
        stage_experts(nc, R, m, "ge", X, False, route_hash, store)


class Resident:
    pass


def build(nc, A, out):
    with ExitStack() as ctx:
        def sb(name, shape, dt=FP32):
            return ctx.enter_context(nc.sbuf_tensor(name, shape, dt))
        R = Resident()
        R.stages, R.ctx = Stages(), ctx
        R.x = sb("x", [P, NT, E])
        R.xn = sb("xn", [P, NT, E])
        R.xnT = Pair(sb("xnT_h", [P, KE, N], FP32R), sb("xnT_l", [P, KE, N], FP32R))
        R.ident = sb("ident", [P, P])
        R.ident_b = sb("ident_b", [P, P], BF16)
        R.window = sb("window", [P, 2, 2 * P], BF16)
        R.ones_row = sb("ones_row", [1, P])
        R.yat_one = sb("yat_one", [P, 1])
        R.rope = sb("rope_t", [P, 2, ST, D])
        stored = ctx.enter_context(nc.semaphore("out_stored"))
        a = lambda p, names: [A[f"{p}_{n}"] for n in names]
        wqkv = A["L1_attn_Wqkv"]
        with ExitStack() as ctx_tiles:
            R.ctxT = Pair(*(ctx_tiles.enter_context(nc.sbuf_tensor(f"ctxT_{n}", [P, KE, B * CTX], FP32R)) for n in "hl"))
            attention16(nc, A, R, "ya", "yat", *a("L0_attn", ("Wq", "Wk", "Wv", "Wo", "bq", "bk", "bv", "bo")),
                        lambda s: setup_work(nc, A, R, s))
            attention16(nc, A, R, "xa", "cross", *a("L0_xattn", ("Wq", "Wk", "Wv", "Wo", "bq", "bk", "bv", "bo")))
            experts_top2(nc, A, R)
            attention16(nc, A, R, "wa", "rope", *(wqkv[:, i * E:(i + 1) * E] for i in range(3)), A["L1_attn_Wout"])
            attention_wide(nc, A, R)
        experts_hash(nc, A, R, (out, stored))
        R.stages.held.close()


def shape_constants():
    half = D // 2
    theta = (1.0 / np.float32(10000.0) ** (np.arange(half, dtype=np.float32) / np.float32(half))).astype(np.float32)
    freqs = np.arange(S, dtype=np.float32)[:, None] * theta[None, :]
    cos, sin = np.cos(freqs), np.sin(freqs)
    return {"rope": np.stack([np.concatenate([cos, cos], 1), np.concatenate([-sin, sin], 1)]).astype(np.float32)}


def kernel(**inputs):
    import concourse.bacc as bacc
    from concourse.bass_utils import run_bass_kernel_spmd

    nc = bacc.Bacc("TRN2", target_bir_lowering=False, num_devices=1)
    arrays, patterns = {}, {}
    for name, value in {**inputs, **shape_constants()}.items():
        value = np.ascontiguousarray(value)
        arrays[f"in_{name}"] = value
        patterns[name] = nc.dram_tensor(f"in_{name}", value.shape, mybir.dt.from_np(value.dtype), kind="ExternalInput").ap()
    out = nc.dram_tensor("out", (B, S, E), FP32, kind="ExternalOutput").ap()
    build(nc, patterns, out)
    return run_bass_kernel_spmd(nc, [arrays], core_ids=[0]).results[0]["out"]
```
